# Optimizing a Trainium2 kernel written in Bass

```python
import numpy as np
import jax
import jax.numpy as jnp

def _softmax(x, axis=-1):
    return jax.nn.softmax(x, axis=axis)

def _gelu(x):
    return jax.nn.gelu(x, approximate=True)

def _silu(x):
    return jax.nn.silu(x)

def _sigmoid(x):
    return jax.nn.sigmoid(x)

def _layernorm(x, axis=-1, eps=1e-05):
    m = jnp.mean(x, axis=axis, keepdims=True)
    v = jnp.var(x, axis=axis, keepdims=True)
    return (x - m) / jnp.sqrt(v + eps)

def _scatter_add(tgt, idx, src, axis=0):
    return tgt.at[idx].add(src)

def _segment_sum(src, seg, n):
    return jax.ops.segment_sum(src, seg, n)
kernel_name = 'mk_perceiver_d2_seqx_r4_3e1983'

def setup_inputs(seed: int=0):
    np.random.seed(seed)
    _w = jnp.asarray

    def _rec_inputs():
        import jax
        import jax.numpy as jnp
        _rk = jax.random.key(seed)
        x = 7.22e-05 + 1 * jax.random.normal(jax.random.fold_in(_rk, 1), (16, 64, 512), jnp.float32)
        _lenS = 64 - jax.random.randint(jax.random.fold_in(_rk, 7), (16,), 0, max(1, 64 // 4) + 1, jnp.int32)
        _lenS2 = 1601 - jax.random.randint(jax.random.fold_in(_rk, 8), (16,), 0, max(1, 1601 // 4) + 1, jnp.int32)
        _ctx_1024P = jax.random.normal(jax.random.fold_in(_rk, 11), (16, 16, 256), jnp.float32)
        _ctx_1024c = jax.random.dirichlet(jax.random.fold_in(_rk, 511), 0.3 * jnp.ones((16,), jnp.float32), (16, 1601))
        _ctx_1024t = jnp.einsum('bsk,bkd->bsd', _ctx_1024c, _ctx_1024P)
        _ctx_1024t = _ctx_1024t * jax.lax.rsqrt(jnp.mean(jnp.square(_ctx_1024t)) + 1e-12) * 0.953939
        ctx_1024 = -0.000673644 + 1.00013 * (_ctx_1024t + 0.3 * jax.random.normal(jax.random.fold_in(_rk, 611), (16, 1601, 256), jnp.float32))
        return (x, ctx_1024)
    x, ctx_1024 = _rec_inputs()

    def _L0_xattn_setup():
        import jax, jax.numpy as jnp
        import numpy as np
        B, S1, S2, DCA = (2, 512, 256, 16)
        QDIM, KDIM, H = (512, 256, 16)
        HD = QDIM // H
        SCALE = HD ** (-0.5)
        EPS = 1e-06
        DCA_WEIGHT = 1.0

        def _ln(t, w, b):
            m = jnp.mean(t, axis=-1, keepdims=True)
            v = jnp.var(t, axis=-1, keepdims=True)
            return (t - m) * jax.lax.rsqrt(v + EPS) * w + b

        def _attn(q, k, v):
            s = jnp.einsum('bhqd,bhkd->bhqk', q, k) * SCALE
            p = jax.nn.softmax(s, axis=-1)
            return jnp.einsum('bhqk,bhkd->bhqd', p, v)
        key = jax.random.key(seed)
        ks = jax.random.split(key, 8)
        w = lambda k, shape: jax.random.normal(k, shape, jnp.float32) * 0.02
        return {'x': jax.random.normal(ks[0], (B, S1, QDIM), jnp.float32), 'y': jax.random.normal(ks[1], (B, S2 + DCA, KDIM), jnp.float32), 'Wq': w(ks[2], (QDIM, QDIM)), 'bq': jnp.zeros((QDIM,), jnp.float32), 'Wk': w(ks[3], (KDIM, QDIM)), 'bk': jnp.zeros((QDIM,), jnp.float32), 'Wv': w(ks[4], (KDIM, QDIM)), 'bv': jnp.zeros((QDIM,), jnp.float32), 'Wkv_dca': w(ks[5], (KDIM, 2 * QDIM)), 'bkv_dca': jnp.zeros((2 * QDIM,), jnp.float32), 'qn_w': jnp.ones((HD,), jnp.float32), 'qn_b': jnp.zeros((HD,), jnp.float32), 'kn_w': jnp.ones((HD,), jnp.float32), 'kn_b': jnp.zeros((HD,), jnp.float32), 'kn_dca_w': jnp.ones((HD,), jnp.float32), 'kn_dca_b': jnp.zeros((HD,), jnp.float32), 'Wo': w(ks[6], (QDIM, QDIM)), 'bo': jnp.zeros((QDIM,), jnp.float32)}
    _L0_xattn_all = _L0_xattn_setup()
    _L0_xattn_in = {k: v for k, v in _L0_xattn_all.items() if k in ('Wq', 'bq', 'Wk', 'bk', 'Wv', 'bv', 'Wkv_dca', 'bkv_dca', 'qn_w', 'qn_b', 'kn_w', 'kn_b', 'kn_dca_w', 'kn_dca_b', 'Wo', 'bo')}
    del _L0_xattn_all

    def _L0_attn_setup():
        import jax, jax.numpy as jnp
        import numpy as np
        NUM_HEADS = 16
        key = jax.random.key(seed)
        ks = jax.random.split(key, 9)
        B, S, H = (4, 512, 512)
        scale = 1.0 / np.sqrt(H)
        return {'x': jax.random.normal(ks[0], (B, S, H), dtype=jnp.float32), 'Wq': jax.random.normal(ks[1], (H, H), dtype=jnp.float32) * scale, 'bq': jax.random.normal(ks[2], (H,), dtype=jnp.float32) * 0.01, 'Wk': jax.random.normal(ks[3], (H, H), dtype=jnp.float32) * scale, 'bk': jax.random.normal(ks[4], (H,), dtype=jnp.float32) * 0.01, 'Wv': jax.random.normal(ks[5], (H, H), dtype=jnp.float32) * scale, 'bv': jax.random.normal(ks[6], (H,), dtype=jnp.float32) * 0.01, 'Wo': jax.random.normal(ks[7], (H, H), dtype=jnp.float32) * scale, 'bo': jax.random.normal(ks[8], (H,), dtype=jnp.float32) * 0.01}
    _L0_attn_all = _L0_attn_setup()
    _L0_attn_in = {k: v for k, v in _L0_attn_all.items() if k in ('Wq', 'bq', 'Wk', 'bk', 'Wv', 'bv', 'Wo', 'bo')}
    del _L0_attn_all

    def _L0_ffn_setup():
        import jax, jax.numpy as jnp
        import numpy as np
        H = 512
        I = 256
        E = 32
        K = 4
        N_SHARED = 1
        EPS = 1e-06

        def _rmsnorm(x, w, eps=EPS):
            var = jnp.mean(jnp.square(x), axis=-1, keepdims=True)
            return x * jax.lax.rsqrt(var + eps) * w

        def _moe_core(x, gate_w, w13, w2):
            T = x.shape[0]
            N = T * K
            C = 2 * N // E
            logits = jnp.einsum('th,eh->te', x.astype(jnp.float32), gate_w.astype(jnp.float32))
            scores = jax.nn.softmax(logits, axis=-1)
            topk_w, topk_ids = jax.lax.top_k(scores, K)
            topk_w = topk_w / jnp.sum(topk_w, axis=-1, keepdims=True)
            flat_ids = topk_ids.reshape(-1)
            flat_w = topk_w.reshape(-1)
            order = jnp.argsort(flat_ids)
            sorted_eid = flat_ids[order]
            tok = order // K
            counts = jnp.zeros((E,), jnp.int32).at[flat_ids].add(1)
            starts = jnp.cumsum(counts) - counts
            pos = jnp.arange(N) - starts[sorted_eid]
            buf = jnp.zeros((E, C, x.shape[1]), x.dtype).at[sorted_eid, pos].set(x[tok], mode='drop')
            gu = jnp.einsum('ech,ehf->ecf', buf, w13)
            g, u = jnp.split(gu, 2, axis=-1)
            act = jax.nn.silu(g) * u
            eo = jnp.einsum('eci,eih->ech', act, w2)
            out_slots = eo[sorted_eid, pos]
            routed = jnp.zeros_like(x).at[tok].add(out_slots * flat_w[order][:, None])
            return routed
        key = jax.random.key(seed)
        ks = jax.random.split(key, 8)
        s = 1.0 / np.sqrt(H)
        si = 1.0 / np.sqrt(I)
        return {'hidden_states': jax.random.normal(ks[0], (1, 1024, H), jnp.float32), 'norm_w': jnp.ones((H,), jnp.float32), 'gate_w': jax.random.normal(ks[1], (E, H), jnp.float32) * s, 'w13': jax.random.normal(ks[2], (E, H, 2 * I), jnp.float32) * s, 'w2': jax.random.normal(ks[3], (E, I, H), jnp.float32) * si, 'shared_gate_w': jax.random.normal(ks[4], (H, I * N_SHARED), jnp.float32) * s, 'shared_up_w': jax.random.normal(ks[5], (H, I * N_SHARED), jnp.float32) * s, 'shared_down_w': jax.random.normal(ks[6], (I * N_SHARED, H), jnp.float32) * si}
    _L0_ffn_all = _L0_ffn_setup()
    _L0_ffn_in = {k: v for k, v in _L0_ffn_all.items() if k in ('norm_w', 'gate_w', 'w13', 'w2', 'shared_gate_w', 'shared_up_w', 'shared_down_w')}
    del _L0_ffn_all

    def _L1_xattn_setup():
        import jax, jax.numpy as jnp
        import numpy as np
        B, S1, S2, DCA = (2, 512, 256, 16)
        QDIM, KDIM, H = (512, 256, 16)
        HD = QDIM // H
        SCALE = HD ** (-0.5)
        EPS = 1e-06
        DCA_WEIGHT = 1.0

        def _ln(t, w, b):
            m = jnp.mean(t, axis=-1, keepdims=True)
            v = jnp.var(t, axis=-1, keepdims=True)
            return (t - m) * jax.lax.rsqrt(v + EPS) * w + b

        def _attn(q, k, v):
            s = jnp.einsum('bhqd,bhkd->bhqk', q, k) * SCALE
            p = jax.nn.softmax(s, axis=-1)
            return jnp.einsum('bhqk,bhkd->bhqd', p, v)
        key = jax.random.key(seed)
        ks = jax.random.split(key, 8)
        w = lambda k, shape: jax.random.normal(k, shape, jnp.float32) * 0.02
        return {'x': jax.random.normal(ks[0], (B, S1, QDIM), jnp.float32), 'y': jax.random.normal(ks[1], (B, S2 + DCA, KDIM), jnp.float32), 'Wq': w(ks[2], (QDIM, QDIM)), 'bq': jnp.zeros((QDIM,), jnp.float32), 'Wk': w(ks[3], (KDIM, QDIM)), 'bk': jnp.zeros((QDIM,), jnp.float32), 'Wv': w(ks[4], (KDIM, QDIM)), 'bv': jnp.zeros((QDIM,), jnp.float32), 'Wkv_dca': w(ks[5], (KDIM, 2 * QDIM)), 'bkv_dca': jnp.zeros((2 * QDIM,), jnp.float32), 'qn_w': jnp.ones((HD,), jnp.float32), 'qn_b': jnp.zeros((HD,), jnp.float32), 'kn_w': jnp.ones((HD,), jnp.float32), 'kn_b': jnp.zeros((HD,), jnp.float32), 'kn_dca_w': jnp.ones((HD,), jnp.float32), 'kn_dca_b': jnp.zeros((HD,), jnp.float32), 'Wo': w(ks[6], (QDIM, QDIM)), 'bo': jnp.zeros((QDIM,), jnp.float32)}
    _L1_xattn_all = _L1_xattn_setup()
    _L1_xattn_in = {k: v for k, v in _L1_xattn_all.items() if k in ('Wq', 'bq', 'Wk', 'bk', 'Wv', 'bv', 'Wkv_dca', 'bkv_dca', 'qn_w', 'qn_b', 'kn_w', 'kn_b', 'kn_dca_w', 'kn_dca_b', 'Wo', 'bo')}
    del _L1_xattn_all

    def _L1_attn_setup():
        import jax, jax.numpy as jnp
        import numpy as np
        N_HEADS = 16
        N_KV_HEADS = 4
        WINDOW = 128
        THETA = 10000.0

        def _rope_cos_sin(T, half):
            inv = 1.0 / THETA ** (jnp.arange(half, dtype=jnp.float32) / half)
            f = jnp.arange(T, dtype=jnp.float32)[:, None] * inv[None, :]
            return (jnp.cos(f), jnp.sin(f))

        def _apply_rope(x, cos, sin):
            xr, xi = (x[..., 0::2], x[..., 1::2])
            out_r = xr * cos - xi * sin
            out_i = xr * sin + xi * cos
            return jnp.stack([out_r, out_i], axis=-1).reshape(x.shape)
        key = jax.random.key(seed)
        ks = jax.random.split(key, 6)
        B, T, C = (1, 1024, 512)
        kvC = C // N_HEADS * N_KV_HEADS
        return {'x': jax.random.normal(ks[0], (B, T, C), dtype=jnp.float32), 'wq': jax.random.normal(ks[1], (C, C), dtype=jnp.float32) * 0.02, 'wk': jax.random.normal(ks[2], (C, kvC), dtype=jnp.float32) * 0.02, 'wv': jax.random.normal(ks[3], (C, kvC), dtype=jnp.float32) * 0.02, 'wo': jax.random.normal(ks[4], (C, C), dtype=jnp.float32) * 0.02, 'sink': jnp.zeros((1, N_HEADS, 1, 1), dtype=jnp.float32)}
    _L1_attn_all = _L1_attn_setup()
    _L1_attn_in = {k: v for k, v in _L1_attn_all.items() if k in ('wq', 'wk', 'wv', 'wo', 'sink')}
    del _L1_attn_all

    def _L1_ffn_setup():
        import jax, jax.numpy as jnp
        import numpy as np
        D_MODEL = 512
        HIDDEN = int(2 * D_MODEL * 4 / 3)

        def ternary_quant(w):
            s = jnp.mean(jnp.abs(w))
            q = jnp.clip(jnp.round(w / s), -1.0, 1.0) * s
            return w + jax.lax.stop_gradient(q - w)
        key = jax.random.key(seed)
        k0, k1, k2, k3 = jax.random.split(key, 4)
        x = jax.random.normal(k0, (4, 1024, D_MODEL), dtype=jnp.float32)
        std_in = 1.0 / np.sqrt(D_MODEL)
        std_h = 1.0 / np.sqrt(HIDDEN)
        w1 = jax.random.uniform(k1, (HIDDEN, D_MODEL), jnp.float32, -std_in, std_in)
        w3 = jax.random.uniform(k2, (HIDDEN, D_MODEL), jnp.float32, -std_in, std_in)
        w2 = jax.random.uniform(k3, (D_MODEL, HIDDEN), jnp.float32, -std_h, std_h)
        return {'x': x, 'w1': w1, 'w3': w3, 'w2': w2}
    _L1_ffn_all = _L1_ffn_setup()
    _L1_ffn_in = {k: v for k, v in _L1_ffn_all.items() if k in ('w1', 'w3', 'w2')}
    del _L1_ffn_all
    return {'x': x, 'ctx_1024': ctx_1024, 'L0_xattn_Wq': _L0_xattn_in['Wq'], 'L0_xattn_bq': _L0_xattn_in['bq'], 'L0_xattn_Wk': _L0_xattn_in['Wk'], 'L0_xattn_bk': _L0_xattn_in['bk'], 'L0_xattn_Wv': _L0_xattn_in['Wv'], 'L0_xattn_bv': _L0_xattn_in['bv'], 'L0_xattn_Wkv_dca': _L0_xattn_in['Wkv_dca'], 'L0_xattn_bkv_dca': _L0_xattn_in['bkv_dca'], 'L0_xattn_qn_w': _L0_xattn_in['qn_w'], 'L0_xattn_qn_b': _L0_xattn_in['qn_b'], 'L0_xattn_kn_w': _L0_xattn_in['kn_w'], 'L0_xattn_kn_b': _L0_xattn_in['kn_b'], 'L0_xattn_kn_dca_w': _L0_xattn_in['kn_dca_w'], 'L0_xattn_kn_dca_b': _L0_xattn_in['kn_dca_b'], 'L0_xattn_Wo': _L0_xattn_in['Wo'], 'L0_xattn_bo': _L0_xattn_in['bo'], 'L0_attn_Wq': _L0_attn_in['Wq'], 'L0_attn_bq': _L0_attn_in['bq'], 'L0_attn_Wk': _L0_attn_in['Wk'], 'L0_attn_bk': _L0_attn_in['bk'], 'L0_attn_Wv': _L0_attn_in['Wv'], 'L0_attn_bv': _L0_attn_in['bv'], 'L0_attn_Wo': _L0_attn_in['Wo'], 'L0_attn_bo': _L0_attn_in['bo'], 'L0_ffn_norm_w': _L0_ffn_in['norm_w'], 'L0_ffn_gate_w': _L0_ffn_in['gate_w'], 'L0_ffn_w13': _L0_ffn_in['w13'], 'L0_ffn_w2': _L0_ffn_in['w2'], 'L0_ffn_shared_gate_w': _L0_ffn_in['shared_gate_w'], 'L0_ffn_shared_up_w': _L0_ffn_in['shared_up_w'], 'L0_ffn_shared_down_w': _L0_ffn_in['shared_down_w'], 'L1_xattn_Wq': _L1_xattn_in['Wq'], 'L1_xattn_bq': _L1_xattn_in['bq'], 'L1_xattn_Wk': _L1_xattn_in['Wk'], 'L1_xattn_bk': _L1_xattn_in['bk'], 'L1_xattn_Wv': _L1_xattn_in['Wv'], 'L1_xattn_bv': _L1_xattn_in['bv'], 'L1_xattn_Wkv_dca': _L1_xattn_in['Wkv_dca'], 'L1_xattn_bkv_dca': _L1_xattn_in['bkv_dca'], 'L1_xattn_qn_w': _L1_xattn_in['qn_w'], 'L1_xattn_qn_b': _L1_xattn_in['qn_b'], 'L1_xattn_kn_w': _L1_xattn_in['kn_w'], 'L1_xattn_kn_b': _L1_xattn_in['kn_b'], 'L1_xattn_kn_dca_w': _L1_xattn_in['kn_dca_w'], 'L1_xattn_kn_dca_b': _L1_xattn_in['kn_dca_b'], 'L1_xattn_Wo': _L1_xattn_in['Wo'], 'L1_xattn_bo': _L1_xattn_in['bo'], 'L1_attn_wq': _L1_attn_in['wq'], 'L1_attn_wk': _L1_attn_in['wk'], 'L1_attn_wv': _L1_attn_in['wv'], 'L1_attn_wo': _L1_attn_in['wo'], 'L1_attn_sink': _L1_attn_in['sink'], 'L1_ffn_w1': _L1_ffn_in['w1'], 'L1_ffn_w3': _L1_ffn_in['w3'], 'L1_ffn_w2': _L1_ffn_in['w2']}

def reference(x, ctx_1024, L0_xattn_Wq, L0_xattn_bq, L0_xattn_Wk, L0_xattn_bk, L0_xattn_Wv, L0_xattn_bv, L0_xattn_Wkv_dca, L0_xattn_bkv_dca, L0_xattn_qn_w, L0_xattn_qn_b, L0_xattn_kn_w, L0_xattn_kn_b, L0_xattn_kn_dca_w, L0_xattn_kn_dca_b, L0_xattn_Wo, L0_xattn_bo, L0_attn_Wq, L0_attn_bq, L0_attn_Wk, L0_attn_bk, L0_attn_Wv, L0_attn_bv, L0_attn_Wo, L0_attn_bo, L0_ffn_norm_w, L0_ffn_gate_w, L0_ffn_w13, L0_ffn_w2, L0_ffn_shared_gate_w, L0_ffn_shared_up_w, L0_ffn_shared_down_w, L1_xattn_Wq, L1_xattn_bq, L1_xattn_Wk, L1_xattn_bk, L1_xattn_Wv, L1_xattn_bv, L1_xattn_Wkv_dca, L1_xattn_bkv_dca, L1_xattn_qn_w, L1_xattn_qn_b, L1_xattn_kn_w, L1_xattn_kn_b, L1_xattn_kn_dca_w, L1_xattn_kn_dca_b, L1_xattn_Wo, L1_xattn_bo, L1_attn_wq, L1_attn_wk, L1_attn_wv, L1_attn_wo, L1_attn_sink, L1_ffn_w1, L1_ffn_w3, L1_ffn_w2):
    import jax
    import jax.numpy as jnp

    def _L0_xattn_ref(x, y, Wq, bq, Wk, bk, Wv, bv, Wkv_dca, bkv_dca, qn_w, qn_b, kn_w, kn_b, kn_dca_w, kn_dca_b, Wo, bo):
        import jax, jax.numpy as jnp
        import numpy as np
        B, S1, S2, DCA = (2, 512, 256, 16)
        QDIM, KDIM, H = (512, 256, 16)
        HD = QDIM // H
        SCALE = HD ** (-0.5)
        EPS = 1e-06
        DCA_WEIGHT = 1.0

        def _ln(t, w, b):
            m = jnp.mean(t, axis=-1, keepdims=True)
            v = jnp.var(t, axis=-1, keepdims=True)
            return (t - m) * jax.lax.rsqrt(v + EPS) * w + b

        def _attn(q, k, v):
            s = jnp.einsum('bhqd,bhkd->bhqk', q, k) * SCALE
            p = jax.nn.softmax(s, axis=-1)
            return jnp.einsum('bhqk,bhkd->bhqd', p, v)
        b, s1, _ = x.shape
        y_dca = y[:, -DCA:, :]
        y_main = y[:, :-DCA, :]
        kv_dca = (y_dca @ Wkv_dca + bkv_dca).reshape(b, DCA, 2, H, HD)
        k_dca = _ln(kv_dca[:, :, 0], kn_dca_w, kn_dca_b)
        v_dca = kv_dca[:, :, 1]
        s2 = y_main.shape[1]
        q = _ln((x @ Wq + bq).reshape(b, s1, H, HD), qn_w, qn_b)
        kv = jnp.concatenate([y_main @ Wk + bk, y_main @ Wv + bv], axis=-1)
        kv = kv.reshape(b, s2, H, 2 * HD)
        k = _ln(kv[..., :HD], kn_w, kn_b)
        v = kv[..., HD:]
        qT = q.transpose(0, 2, 1, 3)
        ctx = _attn(qT, k.transpose(0, 2, 1, 3), v.transpose(0, 2, 1, 3))
        ctx = ctx.transpose(0, 2, 1, 3).reshape(b, s1, QDIM)
        ctx_dca = _attn(qT, k_dca.transpose(0, 2, 1, 3), v_dca.transpose(0, 2, 1, 3))
        ctx_dca = ctx_dca.transpose(0, 2, 1, 3).reshape(b, s1, QDIM)
        ctx = ctx + DCA_WEIGHT * ctx_dca
        return ctx @ Wo + bo

    def _L0_attn_ref(x, Wq, bq, Wk, bk, Wv, bv, Wo, bo):
        import jax, jax.numpy as jnp
        import numpy as np
        NUM_HEADS = 16
        B, S, H = x.shape
        nh = NUM_HEADS
        hd = H // nh

        def split_heads(t):
            return t.reshape(B, S, nh, hd).transpose(0, 2, 1, 3)
        q = split_heads(x @ Wq + bq)
        k = split_heads(x @ Wk + bk)
        v = split_heads(x @ Wv + bv)
        inv_sqrt_hd = jnp.asarray(1.0 / np.sqrt(hd), dtype=x.dtype)
        attn = jnp.einsum('bhqd,bhkd->bhqk', q, k) * inv_sqrt_hd
        attn = jax.nn.softmax(attn, axis=-1)
        out = jnp.einsum('bhqk,bhkd->bhqd', attn, v)
        out = out.transpose(0, 2, 1, 3).reshape(B, S, H)
        return out @ Wo + bo

    def _L0_ffn_ref(hidden_states, norm_w, gate_w, w13, w2, shared_gate_w, shared_up_w, shared_down_w):
        import jax, jax.numpy as jnp
        import numpy as np
        H = 512
        I = 256
        E = 32
        K = 4
        N_SHARED = 1
        EPS = 1e-06

        def _rmsnorm(x, w, eps=EPS):
            var = jnp.mean(jnp.square(x), axis=-1, keepdims=True)
            return x * jax.lax.rsqrt(var + eps) * w

        def _moe_core(x, gate_w, w13, w2):
            T = x.shape[0]
            N = T * K
            C = 2 * N // E
            logits = jnp.einsum('th,eh->te', x.astype(jnp.float32), gate_w.astype(jnp.float32))
            scores = jax.nn.softmax(logits, axis=-1)
            topk_w, topk_ids = jax.lax.top_k(scores, K)
            topk_w = topk_w / jnp.sum(topk_w, axis=-1, keepdims=True)
            flat_ids = topk_ids.reshape(-1)
            flat_w = topk_w.reshape(-1)
            order = jnp.argsort(flat_ids)
            sorted_eid = flat_ids[order]
            tok = order // K
            counts = jnp.zeros((E,), jnp.int32).at[flat_ids].add(1)
            starts = jnp.cumsum(counts) - counts
            pos = jnp.arange(N) - starts[sorted_eid]
            buf = jnp.zeros((E, C, x.shape[1]), x.dtype).at[sorted_eid, pos].set(x[tok], mode='drop')
            gu = jnp.einsum('ech,ehf->ecf', buf, w13)
            g, u = jnp.split(gu, 2, axis=-1)
            act = jax.nn.silu(g) * u
            eo = jnp.einsum('eci,eih->ech', act, w2)
            out_slots = eo[sorted_eid, pos]
            routed = jnp.zeros_like(x).at[tok].add(out_slots * flat_w[order][:, None])
            return routed
        B, S, Hd = hidden_states.shape
        residual = hidden_states
        h = _rmsnorm(hidden_states, norm_w)
        x = h.reshape(-1, Hd)
        routed = _moe_core(x, gate_w, w13, w2)
        shared = jax.nn.silu(x @ shared_gate_w) * (x @ shared_up_w) @ shared_down_w
        out = residual + (routed + shared).reshape(B, S, Hd)
        return out

    def _L1_xattn_ref(x, y, Wq, bq, Wk, bk, Wv, bv, Wkv_dca, bkv_dca, qn_w, qn_b, kn_w, kn_b, kn_dca_w, kn_dca_b, Wo, bo):
        import jax, jax.numpy as jnp
        import numpy as np
        B, S1, S2, DCA = (2, 512, 256, 16)
        QDIM, KDIM, H = (512, 256, 16)
        HD = QDIM // H
        SCALE = HD ** (-0.5)
        EPS = 1e-06
        DCA_WEIGHT = 1.0

        def _ln(t, w, b):
            m = jnp.mean(t, axis=-1, keepdims=True)
            v = jnp.var(t, axis=-1, keepdims=True)
            return (t - m) * jax.lax.rsqrt(v + EPS) * w + b

        def _attn(q, k, v):
            s = jnp.einsum('bhqd,bhkd->bhqk', q, k) * SCALE
            p = jax.nn.softmax(s, axis=-1)
            return jnp.einsum('bhqk,bhkd->bhqd', p, v)
        b, s1, _ = x.shape
        y_dca = y[:, -DCA:, :]
        y_main = y[:, :-DCA, :]
        kv_dca = (y_dca @ Wkv_dca + bkv_dca).reshape(b, DCA, 2, H, HD)
        k_dca = _ln(kv_dca[:, :, 0], kn_dca_w, kn_dca_b)
        v_dca = kv_dca[:, :, 1]
        s2 = y_main.shape[1]
        q = _ln((x @ Wq + bq).reshape(b, s1, H, HD), qn_w, qn_b)
        kv = jnp.concatenate([y_main @ Wk + bk, y_main @ Wv + bv], axis=-1)
        kv = kv.reshape(b, s2, H, 2 * HD)
        k = _ln(kv[..., :HD], kn_w, kn_b)
        v = kv[..., HD:]
        qT = q.transpose(0, 2, 1, 3)
        ctx = _attn(qT, k.transpose(0, 2, 1, 3), v.transpose(0, 2, 1, 3))
        ctx = ctx.transpose(0, 2, 1, 3).reshape(b, s1, QDIM)
        ctx_dca = _attn(qT, k_dca.transpose(0, 2, 1, 3), v_dca.transpose(0, 2, 1, 3))
        ctx_dca = ctx_dca.transpose(0, 2, 1, 3).reshape(b, s1, QDIM)
        ctx = ctx + DCA_WEIGHT * ctx_dca
        return ctx @ Wo + bo

    def _L1_attn_ref(x, wq, wk, wv, wo, sink):
        import jax, jax.numpy as jnp
        import numpy as np
        N_HEADS = 16
        N_KV_HEADS = 4
        WINDOW = 128
        THETA = 10000.0

        def _rope_cos_sin(T, half):
            inv = 1.0 / THETA ** (jnp.arange(half, dtype=jnp.float32) / half)
            f = jnp.arange(T, dtype=jnp.float32)[:, None] * inv[None, :]
            return (jnp.cos(f), jnp.sin(f))

        def _apply_rope(x, cos, sin):
            xr, xi = (x[..., 0::2], x[..., 1::2])
            out_r = xr * cos - xi * sin
            out_i = xr * sin + xi * cos
            return jnp.stack([out_r, out_i], axis=-1).reshape(x.shape)
        B, T, C = x.shape
        hd = C // N_HEADS
        n_rep = N_HEADS // N_KV_HEADS
        q = (x @ wq).reshape(B, T, N_HEADS, hd).transpose(0, 2, 1, 3)
        k = (x @ wk).reshape(B, T, N_KV_HEADS, hd).transpose(0, 2, 1, 3)
        v = (x @ wv).reshape(B, T, N_KV_HEADS, hd).transpose(0, 2, 1, 3)
        cos, sin = _rope_cos_sin(T, hd // 2)
        q = _apply_rope(q, cos, sin)
        k = _apply_rope(k, cos, sin)
        k = jnp.repeat(k, n_rep, axis=1)
        v = jnp.repeat(v, n_rep, axis=1)
        att = jnp.einsum('bhqd,bhkd->bhqk', q, k) * hd ** (-0.5) + sink
        idx = jnp.arange(T)
        band = jnp.abs(idx[:, None] - idx[None, :]) <= WINDOW // 2
        att = jnp.where(band[None, None, :, :], att, -jnp.inf)
        att = jax.nn.softmax(att, axis=-1)
        att = jnp.where(jnp.isnan(att), 1.0 / T, att)
        out = jnp.einsum('bhqk,bhkd->bqhd', att, v).reshape(B, T, C)
        return out @ wo

    def _L1_ffn_ref(x, w1, w3, w2):
        import jax, jax.numpy as jnp
        import numpy as np
        D_MODEL = 512
        HIDDEN = int(2 * D_MODEL * 4 / 3)

        def ternary_quant(w):
            s = jnp.mean(jnp.abs(w))
            q = jnp.clip(jnp.round(w / s), -1.0, 1.0) * s
            return w + jax.lax.stop_gradient(q - w)
        w1q = ternary_quant(w1)
        w3q = ternary_quant(w3)
        w2q = ternary_quant(w2)
        h1 = jnp.einsum('bsd,hd->bsh', x, w1q)
        h3 = jnp.einsum('bsd,hd->bsh', x, w3q)
        g = jax.nn.silu(h1) * h3
        return jnp.einsum('bsh,dh->bsd', g, w2q)
    x = x + _L0_xattn_ref(_layernorm(x, axis=-1), ctx_1024, L0_xattn_Wq, L0_xattn_bq, L0_xattn_Wk, L0_xattn_bk, L0_xattn_Wv, L0_xattn_bv, L0_xattn_Wkv_dca, L0_xattn_bkv_dca, L0_xattn_qn_w, L0_xattn_qn_b, L0_xattn_kn_w, L0_xattn_kn_b, L0_xattn_kn_dca_w, L0_xattn_kn_dca_b, L0_xattn_Wo, L0_xattn_bo)
    x = x + _L0_attn_ref(_layernorm(x, axis=-1), L0_attn_Wq, L0_attn_bq, L0_attn_Wk, L0_attn_bk, L0_attn_Wv, L0_attn_bv, L0_attn_Wo, L0_attn_bo)
    x = x + _L0_ffn_ref(_layernorm(x, axis=-1), L0_ffn_norm_w, L0_ffn_gate_w, L0_ffn_w13, L0_ffn_w2, L0_ffn_shared_gate_w, L0_ffn_shared_up_w, L0_ffn_shared_down_w)
    x = x + _L1_xattn_ref(_layernorm(x, axis=-1), ctx_1024, L1_xattn_Wq, L1_xattn_bq, L1_xattn_Wk, L1_xattn_bk, L1_xattn_Wv, L1_xattn_bv, L1_xattn_Wkv_dca, L1_xattn_bkv_dca, L1_xattn_qn_w, L1_xattn_qn_b, L1_xattn_kn_w, L1_xattn_kn_b, L1_xattn_kn_dca_w, L1_xattn_kn_dca_b, L1_xattn_Wo, L1_xattn_bo)
    x = x + _L1_attn_ref(_layernorm(x, axis=-1), L1_attn_wq, L1_attn_wk, L1_attn_wv, L1_attn_wo, L1_attn_sink)
    x = x + _L1_ffn_ref(_layernorm(x, axis=-1), L1_ffn_w1, L1_ffn_w3, L1_ffn_w2)
    return x

_drawn_inputs = setup_inputs


def setup_inputs(seed=0):
    import zlib

    import numpy as np

    out = dict(_drawn_inputs(seed))
    spreads = {'L0_xattn_bq': (0.0, 0.361),
     'L0_xattn_bk': (0.0, 0.1),
     'L0_xattn_bv': (0.0, 0.1),
     'L0_xattn_bkv_dca': (0.0, 0.1),
     'L0_xattn_qn_w': (1.0, 0.6),
     'L0_xattn_qn_b': (0.0, 0.8),
     'L0_xattn_kn_w': (1.0, 0.6),
     'L0_xattn_kn_b': (0.0, 2.0),
     'L0_xattn_kn_dca_w': (1.0, 0.6),
     'L0_xattn_kn_dca_b': (0.0, 2.0),
     'L0_xattn_bo': (0.0, 0.1),
     'L0_ffn_norm_w': (1.0, 0.2),
     'L1_xattn_bq': (0.0, 0.8),
     'L1_xattn_bk': (0.0, 0.579),
     'L1_xattn_bv': (0.0, 0.544),
     'L1_xattn_bkv_dca': (0.0, 0.386),
     'L1_xattn_qn_w': (1.0, 0.6),
     'L1_xattn_qn_b': (0.0, 2.0),
     'L1_xattn_kn_w': (1.0, 0.6),
     'L1_xattn_kn_b': (0.0, 2.0),
     'L1_xattn_kn_dca_w': (1.0, 0.6),
     'L1_xattn_kn_dca_b': (0.0, 2.0),
     'L1_xattn_bo': (0.0, 0.1),
     'L1_attn_sink': (0.0, 2.0)}
    factors = {'L0_attn_bq': 23.06,
     'L0_attn_bk': 64.0,
     'L0_attn_bv': 3.905,
     'L0_attn_bo': 4.208,
     'L1_attn_wq': 8.0,
     'L1_attn_wk': 8.0,
     'L1_xattn_Wq': 3.34}
    for name, (base, spread) in spreads.items():
        noise = np.random.default_rng([zlib.crc32(name.encode()), seed]).standard_normal(out[name].shape)
        drawn = base * np.exp(spread * noise) if base else spread * noise
        out[name] = jnp.asarray(drawn.astype(out[name].dtype))
    for name, factor in factors.items():
        out[name] = (out[name] * factor).astype(out[name].dtype)
    return out
```

```python
from contextlib import ExitStack

import numpy as np
import concourse.bass as bass
from concourse import mybir

F32 = mybir.dt.float32
F32R = mybir.dt.float32r
F16 = mybir.dt.float16
BF16 = mybir.dt.bfloat16
I32 = mybir.dt.int32
U32 = mybir.dt.uint32
ALU = mybir.AluOpType
ACT = mybir.ActivationFunctionType
AX = mybir.AxisListType

P = 128
B, S, D = 16, 64, 512
H, HD = 16, 32
PAIRS = H // 2
GROUPS = D // P
TT = B * S // P
CTX, KD, DCA = 1601, 256, 16
MAIN = CTX - DCA
DC0 = MAIN + MAIN % 2
KEYS = DC0 + DCA
KC = KD // P
KT = -(-MAIN // P)
TAIL = MAIN - (KT - 1) * P
DROW = DC0 - (KT - 1) * P
KPAD = KT * P
CH = [(c * 512, min(512, KEYS - c * 512)) for c in range(-(-KEYS // 512))]
NCH = len(CH)
YA = 6
LN_EPS, HEAD_EPS = 1e-5, 1e-6
SCALE = float(HD) ** -0.5



AT = {"k": 0.0, "v": 0.579, "kt": 1.798, "y": 0.45, "first": 0.051, "pace": 1.026}
PAIR_AT = {("s", 0): -0.176, ("s", 1): -0.165, ("s", 2): -0.016, ("s", 3): 0.064, ("exp", 0): 0.482,
           ("pt", 0): 0.972, ("pt", 1): 0.999, ("norm", 0): 1.064, ("pv", 0): 1.132, ("pt", 2): 1.142,
           ("pv", 1): 1.192, ("pt", 3): 1.212, ("pv", 2): 1.327, ("pv", 3): 1.352, ("o", 0): 1.384}


def batch_steps():
    tile, pair = 1.0, KT / PAIRS
    steps = [(-1.0, ("y", 0, 0))]
    for i in range(KT):
        steps += [((i + AT[kind]) * tile, (kind, i, 0)) for kind in ("k", "v", "kt")]
        if i + 1 < KT:
            steps.append(((i + AT["y"]) * tile, ("y", i + 1, 0)))
    for p in range(PAIRS):
        steps += [(AT["first"] + (p + t) * pair * AT["pace"], (kind, p, c)) for (kind, c), t in PAIR_AT.items()]
    return [step for _, step in sorted(steps, key=lambda x: x[0])]


STEPS = batch_steps()
TILE_STEPS = ("y", "k", "v", "kt")


def context_attention(nc, env, ctx_dram, qs_dram, kd_dram, vd_dram, wk, wv, bk2, kw_col, kb_col):
    with ExitStack() as ctx:
        sb = lambda name, shape, dt: ctx.enter_context(nc.sbuf_tensor(name, shape, dt))
        ps = lambda name, shape, dt: ctx.enter_context(nc.psum_tensor(name, shape, dt))
        pre = env.prefix
        sems = []

        def sem(name):
            s = ctx.enter_context(nc.semaphore(pre + name))
            sems.append(s)
            return s

        y = sb(pre + "y", [P, KC, MAIN], F32)
        yh = sb(pre + "yh", [P, 2, KC, P], F32R)
        yl = sb(pre + "yl", [P, 2, KC, P], F32R)
        kh = sb(pre + "kh", [P, 2, GROUPS, KEYS], F16)
        kl = sb(pre + "kl", [P, 2, GROUPS, KEYS], F16)
        v = sb(pre + "v", [P, 2, KT, PAIRS, 2, 64], F16)
        qs = sb(pre + "qs", [P, 2, PAIRS, 2, P], F16)
        p = sb(pre + "p", [P, 2, KPAD], F32)
        pth = sb(pre + "pth", [P, 2, KT, P], F16)
        ptl = sb(pre + "ptl", [P, 2, KT, P], F16)
        sq = sb(pre + "sq", [P, D], F32)
        kc = sb(pre + "kc", [P, 2, D], F32)
        khat = sb(pre + "khat", [P, 2, D], F32)
        kf = sb(pre + "kf", [P, 2, GROUPS, P], F32)
        var = sb(pre + "var", [P, 2, H], F32)
        rstd = sb(pre + "rstd", [P, H], F32)
        half = sb(pre + "half", [P, H], F32)
        eps = sb(pre + "eps", [P, H], F32)
        nm4 = sb(pre + "nm4", [P, 2, NCH + 1], F32)
        nm = sb(pre + "nm", [P, 2, 2], F32)
        lsum = sb(pre + "lsum", [P, 2, 2], F32)
        rl = sb(pre + "rl", [P, 2, 2], F32)
        fd = sb(pre + "fd", [P, 2, 1], F32)

        ps_s = ps(pre + "ps_s", [P, 2, 512], F32)
        ps_t = ps(pre + "ps_t", [P, 2, 512], F32)
        ps_o = ps(pre + "ps_o", [P, 512], F32)
        ps_k = ps(pre + "ps_k", [P, 512], F32)
        ps_v = ps(pre + "ps_v", [P, 512], F32)
        ps_kt = ps(pre + "ps_kt", [P, GROUPS, P], F32)
        o_reg = ps_o[:, 0:64]

        y_a, y_b = sem("y_a"), sem("y_b")
        qs_in, dk_in, dv_in = sem("qs_in"), sem("dk_in"), sem("dv_in")
        const_ok = sem("const_ok")
        yh_done, yl_done = sem("yh_done"), sem("yl_done")
        k_done, v_done = sem("k_done"), sem("v_done")
        kc_done, sq_done, red_done, rstd_done, hat_done = sem("kc_done"), sem("sq_done"), sem("red_done"), sem("rstd_done"), sem("hat_done")
        kt_done, kf_done, kh_done, kl_done = sem("kt_done"), sem("kf_done"), sem("kh_done"), sem("kl_done")
        vh_done, vl_done = sem("vh_done"), sem("vl_done")
        s_done, s_copied = sem("s_done"), sem("s_copied")
        min_done, nm_done, exp_done = sem("min_done"), sem("nm_done"), sem("exp_done")
        rl_done, fd1_done, fd_done = sem("rl_done"), sem("fd1_done"), sem("fd_done")
        pt_done, pth_done, ptl_done = sem("pt_done"), sem("pth_done"), sem("ptl_done")
        pv_done, o_done = sem("pv_done"), sem("o_done")
        eps_done = sem("eps_done")

        ident, ones2 = env.ident, env.ones2
        ob = env.ob

        def rows(i):
            return P if i < KT - 1 else TAIL


        def pe_proj(pe, nb, i, t, which):
            n = nb * KT + i
            r = rows(i)
            first = isinstance(n, int) and n == 0
            if which == "k":
                pe.wait_ge(yh_done, n + 1)
                pe.wait_ge(yl_done, n + 1)
                if not first:
                    pe.wait_ge(kc_done, n)
                w, out, done = wk, ps_k, k_done
            else:
                if not first:
                    pe.wait_ge(vl_done, n)
                w, out, done = wv, ps_v, v_done
            steps = [(yh, 0), (yl, 0), (yh, 1)]
            for c in range(KC):
                for a, (part, wpart) in enumerate(steps):
                    m = pe.matmul(out[0:r, :], part[:, t, c, 0:r], w[:, wpart, c, :],
                                  start=(c == 0 and a == 0),
                                  stop=(which == "v" and c == KC - 1 and a == 2))
            if which == "k":
                m = pe.matmul(out[0:r, :], ones2[:, 0:r], bk2[:, :], start=False, stop=True)
            m.then_inc(done, 1)

        def pe_kt(pe, nb, i, t):
            n = nb * KT + i
            r = rows(i)
            pe.wait_ge(hat_done, n + 1)
            if not (isinstance(n, int) and n == 0):
                pe.wait_ge(kh_done, n)
            for g in range(GROUPS):
                m = pe.transpose(ps_kt[:, g, :], khat[:, t, g * P:(g + 1) * P], ident[:, :])
            m.then_inc(kt_done, 1)

        def pe_scores(pe, b, bp, pair, c):
            if pair == 0:
                pe.wait_ge(kl_done, b * KT + min(4 * c + 4, KT))
            if pair == 0 and c == 0:
                pe.wait_ge(qs_in, 16 * b + 16)
                pe.wait_ge(dk_in, 32 * b + 32)
            pe.wait_ge(s_copied, (b * PAIRS + pair) * NCH + c + 1)
            o, w = CH[c]
            g = pair // 2
            out = ps_s[:, c % 2, 0:w]
            for a, (qpart, kpart) in enumerate([(0, kh), (1, kh), (0, kl)]):
                m = pe.matmul(out, qs[:, bp, pair, qpart, :], kpart[:, bp, g, o:o + w],
                              start=(a == 0), stop=(a == 2))
            m.then_inc(s_done, 1)

        def tiles_of(g):
            return range(4 * g, min(4 * g + 4, KT))

        def pe_pt(pe, b, pair, g):
            m0 = b * PAIRS + pair
            if g == 0:
                pe.wait_ge(exp_done, m0 + 1)
            if g == NCH - 1:
                pe.wait_ge(fd_done, m0 + 1)
            pe.wait_ge(ptl_done, m0 * NCH + g + 1)
            for k in tiles_of(g):
                m = pe.transpose(ps_t[:, g % 2, (k % 4) * P:(k % 4 + 1) * P],
                                 p[:, pair % 2, k * P:(k + 1) * P], ident[:, :])
            m.then_inc(pt_done, 1)

        def pe_pv(pe, b, bp, pair, g):
            m0 = b * PAIRS + pair
            if g == 0:
                pe.wait_ge(o_done, m0 + 1)
                if pair == 0:
                    pe.wait_ge(dv_in, 16 * b + 16)
                    pe.wait_ge(vl_done, b * KT + KT)
            pe.wait_ge(ptl_done, m0 * NCH + g + 3)
            for k in tiles_of(g):
                for a, (ppart, vpart) in enumerate([(pth, 0), (ptl, 0), (pth, 1)]):
                    m = pe.matmul(o_reg, ppart[:, pair % 2, k, :], v[:, bp, k, pair, vpart, :],
                                  start=(k == 0 and a == 0), stop=(k == KT - 1 and a == 2))
            if g == NCH - 1:
                m.then_inc(pv_done, 1)

        def act_yh(act, nb, i, t):
            n = nb * KT + i
            r = rows(i)
            if i == 0:
                act.wait_ge(y_a, 16 * nb + 16)
            if i == YA:
                act.wait_ge(y_b, 16 * nb + 16)
            if not (isinstance(n, int) and n < 2):
                act.wait_ge(v_done, n - 1)
            act.activation(yh[:, t, :, 0:r], y[:, :, i * P:i * P + r], ACT.Copy).then_inc(yh_done, 1)

        def act_sq(act, nb, i, t):
            n = nb * KT + i
            r = rows(i)
            act.wait_ge(kc_done, n + 1)
            if not (isinstance(n, int) and n == 0):
                act.wait_ge(red_done, n)
            act.activation(sq[0:r, :], kc[0:r, t, :], ACT.Square, scale=SCALE).then_inc(sq_done, 1)

        def act_vh(act, nb, i, bp):
            n = nb * KT + i
            r = rows(i)
            act.wait_ge(v_done, n + 1)
            act.activation(v[0:r, bp, i, :, 0, :], ps_v[0:r, :].rearrange("p (a d) -> p a d", d=64),
                           ACT.Copy).then_inc(vh_done, 1)

        def act_kf(act, nb, i, t, bp):
            n = nb * KT + i
            r = rows(i)
            act.wait_ge(kt_done, n + 1)
            if not (isinstance(n, int) and n < 2):
                act.wait_ge(kl_done, n - 1)
            act.activation(kf[:, t, :, 0:r], ps_kt[:, :, 0:r], ACT.Identity, bias=kb_col,
                           scale=kw_col).then_inc(kf_done, 1)
            act.activation(kh[:, bp, :, i * P:i * P + r], ps_kt[:, :, 0:r], ACT.Identity, bias=kb_col,
                           scale=kw_col).then_inc(kh_done, 1)

        def act_pth(act, b, pair, g):
            act.wait_ge(pt_done, (b * PAIRS + pair) * NCH + g + 1)
            k = tiles_of(g)
            act.activation(pth[:, pair % 2, k[0]:k[-1] + 1, :], ps_t[:, g % 2, 0:len(k) * P].rearrange(
                "p (k n) -> p k n", n=P), ACT.Copy).then_inc(pth_done, 1)

        def act_exp(act, b, pair):
            act.wait_ge(nm_done, b * PAIRS + pair + 1)
            a = pair % 2
            act.activation(p[:, a, 0:MAIN], p[:, a, 0:MAIN], ACT.Exp, scale=-1.0, bias=nm[:, a, 0:1],
                           accum_out=lsum[:, a, 0:1])
            act.activation(p[:, a, DC0:KEYS], p[:, a, DC0:KEYS], ACT.Exp, scale=-1.0,
                           bias=nm[:, a, 1:2], accum_out=lsum[:, a, 1:2]).then_inc(exp_done, 1)

        def dve_yl(dve, nb, i, t):
            n = nb * KT + i
            r = rows(i)
            dve.wait_ge(yh_done, n + 1)
            dve.tensor_tensor(yl[:, t, :, 0:r], y[:, :, i * P:i * P + r], yh[:, t, :, 0:r].bitcast(F32), ALU.subtract)\
               .then_inc(yl_done, 1)

        def dve_red(dve, nb, i, t):
            r = rows(i)
            dve.wait_ge(sq_done, nb * KT + i + 1)
            dve.tensor_reduce(var[0:r, t, :], sq[0:r, :].rearrange("p (h d) -> p h d", d=HD), AX.X, ALU.add)\
               .then_inc(red_done, 1)

        def dve_kc(dve, nb, i, t):
            n = nb * KT + i
            r = rows(i)
            dve.wait_ge(k_done, n + 1)
            if not (isinstance(n, int) and n < 2):
                dve.wait_ge(hat_done, n - 1)
            dve.tensor_copy(kc[0:r, t, :], ps_k[0:r, :]).then_inc(kc_done, 1)

        def dve_vl(dve, nb, i, bp):
            n = nb * KT + i
            r = rows(i)
            dve.wait_ge(vh_done, n + 1)
            dve.tensor_tensor(v[0:r, bp, i, :, 1, :], ps_v[0:r, :].rearrange("p (a d) -> p a d", d=64),
                              v[0:r, bp, i, :, 0, :], ALU.subtract).then_inc(vl_done, 1)

        def dve_scores(dve, b, pair, c):
            m0 = b * PAIRS + pair
            a = pair % 2
            o, w = CH[c]
            dve.wait_ge(s_done, m0 * NCH + c + 1)
            if c < NCH - 1:
                dve.tensor_scalar(p[:, a, o:o + w], ps_s[:, c % 2, 0:w], -1.0, None, ALU.mult, ALU.min,
                                  accum_out=nm4[:, a, c:c + 1]).then_inc(s_copied, 1)
                return
            wm = MAIN - o
            dve.tensor_scalar(p[:, a, o:MAIN], ps_s[:, c % 2, 0:wm], -1.0, None, ALU.mult, ALU.min,
                              accum_out=nm4[:, a, c:c + 1])
            dve.tensor_scalar(p[:, a, DC0:KEYS], ps_s[:, c % 2, DC0 - o:w], -1.0, None, ALU.mult, ALU.min,
                              accum_out=nm[:, a, 1:2]).then_inc(s_copied, 1)
            dve.wait_ge(s_copied, m0 * NCH + c + 3)
            dve.tensor_reduce(nm[:, a, 0:1], nm4[:, a, 0:NCH], AX.X, ALU.min).then_inc(nm_done, 1)

        def dve_norm(dve, b, pair):
            m0 = b * PAIRS + pair
            a = pair % 2
            dve.wait_ge(exp_done, m0 + 1)
            dve.reciprocal(rl[:, a, :], lsum[:, a, :]).then_inc(rl_done, 1)
            dve.wait_ge(rl_done, m0 + 1)
            dve.tensor_tensor(fd[:, a, :], lsum[:, a, 0:1], rl[:, a, 1:2], ALU.mult).then_inc(fd1_done, 1)
            dve.wait_ge(fd1_done, m0 + 1)
            dve.tensor_scalar(p[:, a, DC0:KEYS], p[:, a, DC0:KEYS], fd[:, a, :], None, ALU.mult)\
               .then_inc(fd_done, 1)

        def dve_ptl(dve, b, pair, g):
            dve.wait_ge(pth_done, (b * PAIRS + pair) * NCH + g + 1)
            k = tiles_of(g)
            dve.tensor_tensor(ptl[:, pair % 2, k[0]:k[-1] + 1, :],
                              ps_t[:, g % 2, 0:len(k) * P].rearrange("p (k n) -> p k n", n=P),
                              pth[:, pair % 2, k[0]:k[-1] + 1, :], ALU.subtract).then_inc(ptl_done, 1)

        def dve_o(dve, b, pair):
            m0 = b * PAIRS + pair
            a = pair % 2
            dve.wait_ge(pv_done, m0 + 1)
            for par in range(2):
                q = slice(64 * par, 64 * par + 64)
                t = dve.tensor_scalar(ob[q, b, pair * HD:(pair + 1) * HD], o_reg[q, HD * par:HD * par + HD],
                                      rl[q, a, 0:1], None, ALU.mult)
            t.then_inc(o_done, 1)

        def pool_hat(pool, nb, i, t):
            n = nb * KT + i
            r = rows(i)
            pool.wait_ge(red_done, n + 1)
            pool.tensor_tensor(var[0:r, t, :], var[0:r, t, :], eps[0:r, :], ALU.add).then_inc(eps_done, 1)
            pool.wait_ge(eps_done, n + 1)
            pool.tensor_tensor(rstd[0:r, :], var[0:r, t, :], half[0:r, :], ALU.pow).then_inc(rstd_done, 1)
            pool.wait_ge(rstd_done, n + 1)
            if not (isinstance(n, int) and n < 2):
                pool.wait_ge(kt_done, n - 1)
            pool.tensor_tensor(khat[0:r, t, :].rearrange("p (h d) -> p h d", d=HD),
                               kc[0:r, t, :].rearrange("p (h d) -> p h d", d=HD),
                               rstd[0:r, :].unsqueeze(2).broadcast_to([r, H, HD]), ALU.mult)\
                .then_inc(hat_done, 1)

        def pool_kl(pool, nb, i, t, bp):
            n = nb * KT + i
            r = rows(i)
            pool.wait_ge(kh_done, n + 1)
            pool.tensor_tensor(kl[:, bp, :, i * P:i * P + r], kf[:, t, :, 0:r], kh[:, bp, :, i * P:i * P + r],
                               ALU.subtract).then_inc(kl_done, 1)


        def steps_of(b, nb):
            return [x for x in STEPS if (nb if x[0] in TILE_STEPS else b) is not None]

        def tile_par(nbp, i):
            return (nbp * KT + i) % 2

        def pe_batch(pe, b, bp, nb, nbp):
            for kind, i, c in steps_of(b, nb):
                if kind in ("k", "v"):
                    pe_proj(pe, nb, i, tile_par(nbp, i), kind)
                elif kind == "kt":
                    pe_kt(pe, nb, i, tile_par(nbp, i))
                elif kind == "s":
                    pe_scores(pe, b, bp, i, c)
                elif kind == "pt":
                    pe_pt(pe, b, i, c)
                elif kind == "pv":
                    pe_pv(pe, b, bp, i, c)

        def act_batch(act, b, bp, nb, nbp):
            for kind, i, c in steps_of(b, nb):
                if kind == "y":
                    act_yh(act, nb, i, tile_par(nbp, i))
                elif kind == "k":
                    act_sq(act, nb, i, tile_par(nbp, i))
                elif kind == "v":
                    act_vh(act, nb, i, nbp)
                elif kind == "kt":
                    act_kf(act, nb, i, tile_par(nbp, i), nbp)
                elif kind == "exp":
                    act_exp(act, b, i)
                elif kind == "pt":
                    act_pth(act, b, i, c)

        def dve_batch(dve, b, bp, nb, nbp):
            for kind, i, c in steps_of(b, nb):
                if kind == "y":
                    dve_yl(dve, nb, i, tile_par(nbp, i))
                elif kind == "k":
                    dve_kc(dve, nb, i, tile_par(nbp, i))
                elif kind == "v":
                    dve_red(dve, nb, i, tile_par(nbp, i))
                    dve_vl(dve, nb, i, nbp)
                elif kind == "s":
                    dve_scores(dve, b, i, c)
                elif kind == "norm":
                    dve_norm(dve, b, i)
                elif kind == "pt":
                    dve_ptl(dve, b, i, c)
                elif kind == "o":
                    dve_o(dve, b, i)

        def pool_batch(pool, b, bp, nb, nbp):
            for kind, i, c in steps_of(b, nb):
                if kind == "v":
                    pool_hat(pool, nb, i, tile_par(nbp, i))
                elif kind == "kt":
                    pool_kl(pool, nb, i, tile_par(nbp, i), nbp)

        def batches(eng, step):
            step(eng, None, None, 0, 0)
            with eng.Fori(0, B // 2 - 1) as turn:
                step(eng, 2 * turn, 0, 2 * turn + 1, 1)
                step(eng, 2 * turn + 1, 1, 2 * turn + 2, 0)
            step(eng, B - 2, 0, B - 1, 1)
            step(eng, B - 1, 1, None, None)

        vd_rows = vd_dram.rearrange("t (b k) a l d -> (t b) k a l d", k=DCA)
        with nc.Block() as block:

            @block.sync
            def _(sp):
                def load_a(b):
                    sp.dma_start(y[:, :, 0:YA * P], ctx_dram[b, :, :, 0:YA * P]).then_inc(y_a, 16)

                def load_b(b):
                    sp.dma_start(y[:, :, YA * P:MAIN], ctx_dram[b, :, :, YA * P:MAIN]).then_inc(y_b, 16)

                def load_attn(b, bp, wait):
                    if wait:
                        sp.wait_ge(s_done, (b - 1) * PAIRS * NCH + 1)
                    sp.dma_start(qs[:, bp].rearrange("p a l q -> p (a l q)"), qs_dram[b]).then_inc(qs_in, 16)
                    for part, buf in enumerate((kh, kl)):
                        sp.dma_start(buf[:, bp, :, DC0:KEYS], kd_dram[part, :, :, b, :]).then_inc(dk_in, 16)
                    if wait:
                        sp.wait_ge(pv_done, (b - 1) * PAIRS + 1)
                    sp.dma_start(v[DROW:DROW + DCA, bp, KT - 1], vd_rows[b]).then_inc(dv_in, 16)

                load_a(0)
                load_b(0)
                sp.wait_ge(const_ok, 5)
                load_attn(0, 0, False)
                sp.wait_ge(yl_done, YA)
                load_a(1)
                sp.wait_ge(yl_done, KT)
                load_b(1)
                sp.wait_ge(pv_done, 1)
                load_attn(1, 1, False)
                with sp.Fori(0, B // 2 - 1) as turn:
                    for u in range(2):
                        b = 2 * turn + u
                        sp.wait_ge(yl_done, (b + 1) * KT + YA)
                        load_a(b + 2)
                        sp.wait_ge(yl_done, (b + 1) * KT + KT)
                        load_b(b + 2)
                        load_attn(b + 2, u, True)

            @block.gpsimd
            def _(pool):
                pool.memset(half[:, :], -0.5).then_inc(const_ok, 1)
                pool.memset(eps[:, :], HEAD_EPS).then_inc(const_ok, 1)
                pool.memset(v[:, :, KT - 1], 0.0).then_inc(const_ok, 1)
                if DC0 > MAIN:
                    for buf in (kh, kl):
                        pool.memset(buf[:, :, :, MAIN:DC0], 0.0).then_inc(const_ok, 1)
                pool.wait_ge(const_ok, 5)
                batches(pool, pool_batch)

            @block.scalar
            def _(act):
                act.preload_act_table(ACT.Exp)
                batches(act, act_batch)

            @block.vector
            def _(dve):
                dve.sem_inc(s_copied, 2)
                dve.sem_inc(ptl_done, 2)
                dve.sem_inc(o_done, 1)
                dve.memset(p[:, :, MAIN:KPAD], 0.0).then_inc(min_done, 1)
                batches(dve, dve_batch)

            @block.tensor
            def _(pe):
                pe.wait_ge(min_done, 1)
                pe.wait_ge(const_ok, 5)
                batches(pe, pe_batch)
        nc.clear_and_free_semaphores(sems)
        nc.all_engine_barrier()


def prepare_context_attention(nc, env, raw, x_src, qs_dram, kd_dram, vd_dram, wk, wv, bk2, kw_col, kb_col):
    with ExitStack() as ctx:
        pre = env.prefix
        sb = lambda name, shape, dt=F32: ctx.enter_context(nc.sbuf_tensor(pre + name, shape, dt))
        sems = []

        def sem(name):
            s = ctx.enter_context(nc.semaphore(pre + name))
            sems.append(s)
            return s

        two = range(2)
        bank = [[ctx.enter_context(nc.psum_tensor(f"{pre}bank{u}{k}", [P, 512], F32)) for k in range(3)]
                for u in two]
        wk32 = sb("wk32", [P, KC * H, HD])
        wv32 = sb("wv32", [P, KC * D])
        wq32 = sb("wq32", [P, 4 * H, HD])
        dw32 = sb("dw32", [P, KC, 2 * H, HD])
        bq32 = sb("bq32", [P, H, HD])
        bd32 = sb("bd32", [P, H, HD])
        bk32 = sb("bk32", [2, H, HD])
        sums = sb("sums", [P, 9 * H])
        bsum = sb("bsum", [2, H])
        bkh = sb("bkh", [2, D], F32R)
        bkl = sb("bkl", [2, D])
        bkm = sb("bkm", [2, D])
        cols = sb("cols", [P, 6])
        qcol = sb("qcol", [P, 2])
        cbs = sb("cbs", [P, 2, 4])
        yd = sb("yd", [P, KC, B * DCA])
        half = sb("half", [P, H])
        eps = sb("eps", [P, H + 1])
        xs = [sb(f"xs{u}", [P, D]) for u in two]
        xn = [sb(f"xn{u}", [P, D]) for u in two]
        xt = [sb(f"xt{u}", [P, 4, P]) for u in two]
        stats = [sb(f"stats{u}", [P, 6]) for u in two]
        mv = [sb(f"mv{u}", [P, 2]) for u in two]
        rs = [sb(f"rs{u}", [P, 1]) for u in two]
        qc = [sb(f"qc{u}", [P, D]) for u in two]
        sq = [sb(f"sq{u}", [P, D]) for u in two]
        var = [sb(f"var{u}", [P, H]) for u in two]
        rh = [sb(f"rh{u}", [P, H]) for u in two]
        hat = [sb(f"hat{u}", [P, D]) for u in two]
        qf = [sb(f"qf{u}", [P, 4, P]) for u in two]
        qsb = [sb(f"qsb{u}", [P, 2, 4, 2, 2, 2, 64], F16) for u in two]
        kdb = sb("kdb", [P, 2, 2, 4, P], F16)
        vdb = sb("vdb", [P, 2, PAIRS, 2, 64], F16)

        names = ("seen wk_in wv_in wq_in dw_in bias_in col_in cb_in yd_in x_in0 x_in1 const sum1 sum2 cen bias_h bias_l bias_m w_ok "
                 "stat aggr eps rstd xn_done tr1 xt_done proj vproj vd_h vd_ok qc_done sq_done red eps2 rstd2 hat_done tr2 "
                 "qf_done qh_done ql_done q_out0 q_out1 kd_out").split()
        g = {name: sem(name) for name in names}
        ident = env.ident

        with nc.Block() as block:

            @block.sync
            def _(sp):
                def load_x(n, u):
                    sp.dma_start(xs[u][:, :], x_src[n]).then_inc(g[f"x_in{u}"], 16)

                load_x(0, 0)
                load_x(1, 1)
                sp.dma_start(wq32[:, :, :].rearrange("p a d -> p (a d)"), raw["wq"]).then_inc(g["wq_in"], 16)
                sp.dma_start(bq32[:, :, :].rearrange("p a d -> p (a d)"), raw["bq"]).then_inc(g["bias_in"], 16)
                sp.dma_start(bd32[:, :, :].rearrange("p a d -> p (a d)"), raw["bd"]).then_inc(g["bias_in"], 16)
                sp.dma_start(bk32[:, :, :].rearrange("p a d -> p (a d)"), raw["bk"]).then_inc(g["bias_in"], 16)
                sp.dma_start(cols[:, :], raw["cols"]).then_inc(g["col_in"], 16)
                sp.dma_start(cbs[:, :, :].rearrange("p a d -> p (a d)"), raw["cb"]).then_inc(g["cb_in"], 16)
                sp.dma_start(dw32[:, :, :, :].rearrange("p k a d -> p (k a d)"), raw["dw"]).then_inc(g["dw_in"], 16)
                sp.dma_start(yd[:, :, :].rearrange("p k n -> p (k n)"), raw["yd"]).then_inc(g["yd_in"], 16)
                sp.dma_start(wk32[:, :, :].rearrange("p a d -> p (a d)"), raw["wk"]).then_inc(g["wk_in"], 16)
                sp.dma_start(wv32[:, :], raw["wv"]).then_inc(g["wv_in"], 16)

                def store_q(n, u):
                    sp.wait_ge(g["ql_done"], n + 1)
                    for b in range(2):
                        sp.dma_start(qs_dram[2 * n + b], qsb[u][:, b].rearrange("p g r l a q -> p (g r l a q)"))\
                            .then_inc(g[f"q_out{u}"], 16)

                with sp.Fori(0, TT // 2 - 1) as turn:
                    for u in two:
                        sp.wait_ge(g["xn_done"], 2 * turn + u + 1)
                        load_x(2 * turn + 2 + u, u)
                    for u in two:
                        store_q(2 * turn + u, u)
                for u in two:
                    store_q(TT - 2 + u, u)
                for t in range(2):
                    sp.wait_ge(g["ql_done"], TT + t + 1)
                    for part in range(2):
                        sp.dma_start(kd_dram[part, :, :, 8 * t:8 * t + 8, :],
                                     kdb[:, t, part].rearrange("p g (b k) -> p g b k", k=DCA)).then_inc(g["kd_out"], 16)
                    sp.wait_ge(g["vd_ok"], t + 1)
                    sp.dma_start(vd_dram[t], vdb[:, t]).then_inc(g["kd_out"], 16)
                for u in two:
                    sp.wait_ge(g[f"q_out{u}"], 32 + 16 * B // 2)
                sp.wait_ge(g["kd_out"], 16 * 6)

            @block.gpsimd
            def _(pool):
                pool.memset(half[:, :], -0.5).then_inc(g["const"], 1)
                for u in two:
                    pool.memset(qsb[u][:, :, :, :, :, :, :], 0.0).then_inc(g["const"], 1)
                pool.memset(eps[:, 0:H], HEAD_EPS).then_inc(g["const"], 1)
                pool.memset(eps[:, H:H + 1], LN_EPS).then_inc(g["const"], 1)
                pool.wait_ge(g["const"], 5)

                def normalise(n, u):
                    pool.wait_ge(g["red"], n + 1)
                    pool.tensor_tensor(var[u][:, :], var[u][:, :], eps[:, 0:H], ALU.add).then_inc(g["eps2"], 1)
                    pool.wait_ge(g["eps2"], n + 1)
                    pool.tensor_tensor(rh[u][:, :], var[u][:, :], half[:, :], ALU.pow).then_inc(g["rstd2"], 1)
                    pool.wait_ge(g["rstd2"], n + 1)
                    pool.tensor_tensor(hat[u][:, :].rearrange("p (h d) -> p h d", d=HD),
                                       qc[u][:, :].rearrange("p (h d) -> p h d", d=HD),
                                       rh[u][:, :].unsqueeze(2).broadcast_to([P, H, HD]), ALU.mult)\
                        .then_inc(g["hat_done"], 1)

                with pool.Fori(0, TT // 2) as turn:
                    for u in two:
                        n = 2 * turn + u
                        pool.wait_ge(g["aggr"], n + 1)
                        pool.tensor_tensor(mv[u][:, 1:2], mv[u][:, 1:2], eps[:, H:H + 1], ALU.add).then_inc(g["eps"], 1)
                        pool.wait_ge(g["eps"], n + 1)
                        pool.tensor_tensor(rs[u][:, :], mv[u][:, 1:2], half[:, 0:1], ALU.pow).then_inc(g["rstd"], 1)
                    for u in two:
                        normalise(2 * turn + u, u)
                for t in range(2):
                    normalise(TT + t, t)

            @block.vector
            def _(dve):
                def centre(w, heads, o, k):
                    s = sums[:, o:o + heads]
                    dve.tensor_reduce(s, w, AX.X, ALU.add).then_inc(g["sum1"], 1)
                    dve.wait_ge(g["sum1"], k + 1)
                    dve.tensor_scalar(s, s, -1.0 / HD, None, ALU.mult).then_inc(g["sum2"], 1)
                    dve.wait_ge(g["sum2"], k + 1)
                    dve.tensor_tensor(w, w, s.unsqueeze(2).broadcast_to([P, heads, HD]), ALU.add).then_inc(g["cen"], 1)

                dve.wait_ge(g["wq_in"], 16)
                centre(wq32[:, :, :], 4 * H, 0, 0)
                dve.wait_ge(g["bias_in"], 48)
                centre(bq32[:, :, :], H, 4 * H, 1)
                dve.wait_ge(g["col_in"], 16)
                dve.tensor_scalar(qcol[:, :], cols[:, 0:2], SCALE, None, ALU.mult).then_inc(g["w_ok"], 1)

                def q_part(n, u, dca):
                    dve.wait_ge(g["proj"], n + 1)
                    dve.tensor_tensor(qc[u][:, :].rearrange("p (h d) -> p h d", d=HD),
                                      bank[u][1][:, :].rearrange("p (h d) -> p h d", d=HD),
                                      (bd32 if dca else bq32)[:, :, :], ALU.add).then_inc(g["qc_done"], 1)

                def red_part(n, u):
                    dve.wait_ge(g["sq_done"], n + 1)
                    dve.tensor_reduce(var[u][:, :], sq[u][:, :].rearrange("p (h d) -> p h d", d=HD), AX.X, ALU.add)\
                        .then_inc(g["red"], 1)

                with dve.Fori(0, TT // 2) as turn:
                    for u in two:
                        n = 2 * turn + u
                        dve.wait_ge(g[f"x_in{u}"], 16 * turn + 16)
                        dve.bn_stats(stats[u][:, :], xs[u][:, :]).then_inc(g["stat"], 1)
                    for u in two:
                        n = 2 * turn + u
                        dve.wait_ge(g["stat"], n + 1)
                        dve.sem_inc(g["seen"], 1)
                        dve.bn_aggr(mv[u][:, :], stats[u][:, :]).then_inc(g["aggr"], 1)
                    for u in two:
                        n = 2 * turn + u
                        dve.wait_ge(g["rstd"], n + 1)
                        dve.tensor_scalar(xn[u][:, :], xs[u][:, :], mv[u][:, 0:1], rs[u][:, 0:1], ALU.subtract,
                                          ALU.mult).then_inc(g["xn_done"], 1)
                    dve.wait_ge(g["cen"], 2)
                    for u in two:
                        q_part(2 * turn + u, u, False)
                    for u in two:
                        red_part(2 * turn + u, u)
                    for u in two:
                        n = 2 * turn + u
                        dve.wait_ge(g["qf_done"], n + 1)
                        dve.wait_ge(g["qh_done"], n + 1)
                        for r4 in range(4):
                            rows = slice(32 * r4, 32 * r4 + 32)
                            q4 = qf[u][rows, :, :].rearrange("p g (b q) -> p b g q", b=2)
                            dst = qsb[u][rows, :, :, r4 // 2, :, r4 % 2, :]
                            for b in range(2):
                                t = dve.tensor_tensor(dst[:, b, :, 1, :], q4[:, b], dst[:, b, :, 0, :], ALU.subtract)
                        t.then_inc(g["ql_done"], 1)
                dve.wait_ge(g["dw_in"], 16)
                for k in range(KC):
                    centre(dw32[:, k, 0:H, :], H, (5 + k) * H, 2 + k)
                centre(bd32[:, :, :], H, 7 * H, 4)
                for t in range(2):
                    q_part(TT + t, t, True)
                for t in range(2):
                    red_part(TT + t, t)
                for t in range(2):
                    dve.wait_ge(g["vd_h"], t + 1)
                    dve.tensor_tensor(vdb[:, t, :, 1, :], bank[t][0][:, :].rearrange("p (a d) -> p a d", d=64),
                                      vdb[:, t, :, 0, :], ALU.subtract).then_inc(g["vd_ok"], 1)
                for t in range(2):
                    dve.wait_ge(g["qf_done"], TT + t + 1)
                    dve.wait_ge(g["qh_done"], TT + t + 1)
                    dve.tensor_tensor(kdb[:, t, 1], qf[t][:, :, :], kdb[:, t, 0], ALU.subtract).then_inc(g["ql_done"], 1)
                dve.wait_ge(g["wk_in"], 16)
                dve.tensor_reduce(sums[:, 0:KC * H], wk32[:, :, :], AX.X, ALU.add).then_inc(g["sum1"], 1)
                dve.tensor_reduce(bsum[:, :], bk32[:, :, :], AX.X, ALU.add).then_inc(g["sum1"], 1)
                dve.wait_ge(g["sum1"], 7)
                dve.tensor_scalar(sums[:, 0:KC * H], sums[:, 0:KC * H], -1.0 / HD, None, ALU.mult).then_inc(g["sum2"], 1)
                dve.tensor_scalar(bsum[:, :], bsum[:, :], -1.0 / HD, None, ALU.mult).then_inc(g["sum2"], 1)
                dve.wait_ge(g["sum2"], 7)
                dve.tensor_tensor(wk32[:, :, :], wk32[:, :, :], sums[:, 0:KC * H].unsqueeze(2)
                                  .broadcast_to([P, KC * H, HD]), ALU.add).then_inc(g["cen"], 1)
                dve.tensor_tensor(bk32[:, :, :], bk32[:, :, :], bsum[:, :].unsqueeze(2).broadcast_to([2, H, HD]), ALU.add)\
                    .then_inc(g["cen"], 1)
                dve.wait_ge(g["cen"], 7)
                dve.wait_ge(g["wv_in"], 16)
                wkf = wk32[:, :, :].rearrange("p (k a) d -> p k (a d)", k=KC)
                wvf = wv32[:, :].rearrange("p (k n) -> p k n", k=KC)
                bkf = bk32[:, :, :].rearrange("p a d -> p (a d)")
                dve.tensor_copy(bkh[:, :], bkf).then_inc(g["bias_h"], 1)
                dve.tensor_copy(wk[:, 0], wkf).then_inc(g["bias_h"], 1)
                dve.tensor_copy(wv[:, 0], wvf).then_inc(g["bias_h"], 1)
                dve.wait_ge(g["bias_h"], 3)
                dve.tensor_tensor(bkl[:, :], bkf, bkh[:, :].bitcast(F32), ALU.subtract).then_inc(g["bias_l"], 1)
                dve.tensor_scalar(bkm[:, :], bkh[:, :].bitcast(F32), ident[0:2, 0:1], None, ALU.mult)\
                    .then_inc(g["bias_m"], 1)
                dve.tensor_tensor(wk[:, 1], wkf, wk[:, 0].bitcast(F32), ALU.subtract)
                dve.tensor_tensor(wv[:, 1], wvf, wv[:, 0].bitcast(F32), ALU.subtract)
                dve.wait_ge(g["bias_l"], 1)
                dve.wait_ge(g["bias_m"], 1)
                dve.scalar_tensor_tensor(out=bk2[:, :], in0=bkl[:, :], scalar=ident[0:2, 1:2], in1=bkm[:, :],
                                         op0=ALU.mult, op1=ALU.add)
                dve.wait_ge(g["cb_in"], 16)
                dve.tensor_tensor(env.cb_x[:, :], cbs[:, 0, :], cbs[:, 1, :], ALU.add)
                dve.tensor_copy(kw_col, cols[:, 2:3])
                dve.tensor_copy(kb_col, cols[:, 3:4])

            @block.scalar
            def _(act):
                act.preload_act_table(ACT.Exp)
                for u in two:
                    act.sem_inc(g[f"q_out{u}"], 32)
                act.wait_ge(g["w_ok"], 1)
                act.wait_ge(g["const"], 3)

                def square(n, u):
                    act.wait_ge(g["qc_done"], n + 1)
                    act.activation(sq[u][:, :], qc[u][:, :], ACT.Square, scale=SCALE).then_inc(g["sq_done"], 1)

                with act.Fori(0, TT // 2) as turn:
                    for u in two:
                        n = 2 * turn + u
                        act.wait_ge(g["tr1"], n + 1)
                        act.activation(xt[u][:, :, :], bank[u][0][:, :].rearrange("p (c n) -> p c n", c=4),
                                       ACT.Copy).then_inc(g["xt_done"], 1)
                    for u in two:
                        square(2 * turn + u, u)
                    for u in two:
                        n = 2 * turn + u
                        act.wait_ge(g["tr2"], n + 1)
                        src = bank[u][2][:, :].rearrange("p (c n) -> p c n", c=4)
                        act.activation(qf[u][:, :, :], src, ACT.Identity, bias=qcol[:, 1:2], scale=qcol[:, 0:1])\
                            .then_inc(g["qf_done"], 1)
                        act.wait_ge(g[f"q_out{u}"], 32 * turn + 32)
                        for r4 in range(4):
                            rows = slice(32 * r4, 32 * r4 + 32)
                            s4 = src[rows].rearrange("p g (b q) -> p b g q", b=2)
                            for b in range(2):
                                t = act.activation(qsb[u][rows, b, :, r4 // 2, 0, r4 % 2, :], s4[:, b], ACT.Identity,
                                                   bias=qcol[rows, 1:2], scale=qcol[rows, 0:1])
                        t.then_inc(g["qh_done"], 1)
                for t in range(2):
                    act.wait_ge(g["vproj"], t + 1)
                    act.activation(vdb[:, t, :, 0, :], bank[t][0][:, :].rearrange("p (a d) -> p a d", d=64), ACT.Copy)\
                        .then_inc(g["vd_h"], 1)
                for t in range(2):
                    square(TT + t, t)
                for t in range(2):
                    act.wait_ge(g["tr2"], TT + t + 1)
                    src = bank[t][2][:, :].rearrange("p (c n) -> p c n", c=4)
                    act.activation(qf[t][:, :, :], src, ACT.Identity, bias=cols[:, 5:6], scale=cols[:, 4:5])\
                        .then_inc(g["qf_done"], 1)
                    act.activation(kdb[:, t, 0], src, ACT.Identity, bias=cols[:, 5:6], scale=cols[:, 4:5])\
                        .then_inc(g["qh_done"], 1)

            @block.tensor
            def _(pe):
                def transpose4(src, out, done):
                    for k in range(4):
                        t = pe.transpose(out[:, k * P:(k + 1) * P], src[:, k * P:(k + 1) * P], ident[:, :])
                    t.then_inc(done, 1)

                with pe.Fori(0, TT // 2) as turn:
                    for u in two:
                        pe.wait_ge(g["xn_done"], 2 * turn + u + 1)
                        transpose4(xn[u], bank[u][0], g["tr1"])
                    pe.wait_ge(g["cen"], 2)
                    for u in two:
                        pe.wait_ge(g["xt_done"], 2 * turn + u + 1)
                        for k in range(4):
                            t = pe.matmul(bank[u][1][:, :], xt[u][:, k, :],
                                          wq32[:, k * H:(k + 1) * H, :].rearrange("p h d -> p (h d)"),
                                          start=(k == 0), stop=(k == 3))
                        t.then_inc(g["proj"], 1)
                    for u in two:
                        pe.wait_ge(g["hat_done"], 2 * turn + u + 1)
                        transpose4(hat[u], bank[u][2], g["tr2"])
                pe.wait_ge(g["yd_in"], 16)
                pe.wait_ge(g["cen"], 5)
                for t in range(2):
                    for k in range(KC):
                        m = pe.matmul(bank[t][0][:, :], yd[:, k, t * P:(t + 1) * P],
                                      dw32[:, k, H:2 * H, :].rearrange("p h d -> p (h d)"),
                                      start=(k == 0), stop=(k == KC - 1))
                    m.then_inc(g["vproj"], 1)
                for t in range(2):
                    for k in range(KC):
                        m = pe.matmul(bank[t][1][:, :], yd[:, k, t * P:(t + 1) * P],
                                      dw32[:, k, 0:H, :].rearrange("p h d -> p (h d)"),
                                      start=(k == 0), stop=(k == KC - 1))
                    m.then_inc(g["proj"], 1)
                for t in range(2):
                    pe.wait_ge(g["hat_done"], TT + t + 1)
                    transpose4(hat[t], bank[t][2], g["tr2"])
        nc.clear_and_free_semaphores(sems)
        nc.all_engine_barrier()


def self_attention(nc, env, layer, raw, x_src):
    rope = layer == 1
    kvw = 128 if rope else D
    with ExitStack() as ctx:
        sb = lambda name, shape, dt=F32: ctx.enter_context(nc.sbuf_tensor(pre + name, shape, dt))
        pre = env.prefix
        sems = []

        def sem(name):
            s = ctx.enter_context(nc.semaphore(pre + name))
            sems.append(s)
            return s

        two = range(2)
        bank = [[ctx.enter_context(nc.psum_tensor(f"{pre}bank{u}{k}", [P, 512], F32)) for k in range(4)]
                for u in two]
        o = [sb(f"o{u}", [P, 2, 256]) for u in two]
        ct = [sb(f"ct{u}", [P, 2, 2, P]) for u in two]
        xs = [sb(f"xs{u}", [P, D]) for u in two]
        xn = [sb(f"xn{u}", [P, D]) for u in two]
        xt = [sb(f"xt{u}", [P, 4, P]) for u in two]
        q32 = [sb(f"q32{u}", [P, D]) for u in two]
        k32 = [sb(f"k32{u}", [P, D]) for u in two]
        v32 = [sb(f"v32{u}", [P, D]) for u in two]
        rt = [sb(f"rt{u}", [P, 2, 256]) for u in two] if rope else None
        kr = [sb(f"kr{u}", [P, kvw]) for u in two] if rope else None
        qb = [sb(f"qb{u}", [P, 4, 2, 2, 64]) for u in two]
        kt = [sb(f"kt{u}", [P, 4, P]) for u in two]
        pr = [sb(f"pr{u}", [P, 4, 2, 2, 64]) for u in two]
        pt = [sb(f"pt{u}", [P, 8, P]) for u in two]
        stats = [sb(f"stats{u}", [P, 6]) for u in two]
        mv = [sb(f"mv{u}", [P, 2]) for u in two]
        rs = [sb(f"rs{u}", [P, 1]) for u in two]
        half1 = sb("half1", [P, 1])
        eps1 = sb("eps1", [P, 1])
        mx = [sb(f"mx{u}", [P, 4, 2, 2]) for u in two]
        ls = [sb(f"ls{u}", [P, 4, 2, 2]) for u in two]
        rl = [sb(f"rl{u}", [P, 4, 2, 2]) for u in two]

        W, loads = {}, {}
        for k, shape in ([("wo_x", (4, D)), ("bo_x", (D,)), ("wq", (4, D)), ("wk", (4, kvw)), ("wv", (4, kvw)), ("wo", (4, D))]
                         + ([("cos", (16,)), ("sin", (16,)), ("sink", (4, 2))] if rope else
                            [("bq", (D,)), ("bk", (D,)), ("cb", (4,)), ("bo", (D,))])):
            t = sb(k, [P] + list(shape))
            if len(shape) == 1:
                W[k] = loads[k] = t[:, :]
            else:
                W[k], loads[k] = t[:, :, :], t[:, :, :].rearrange("p a b -> p (a b)")
        W["cb_x"] = env.cb_x[:, :]

        names = ("seen const sink_ok o_in xs_in tr1 ct1 y1 res1 stat aggr eps rstd xn_done xs2 tr2 xt_done q_done k_done v_done "
                 "q32_done k32_done v32_done rope_a rope_b rope_c tr3 tr4 qb_done kt_done sc_done z_done mx_done "
                 "sub_done exp_done ls_done rl_done tr5 pt_done pv_done o_done tr6 ct2 y2 x_done").split()
        names += [f"load_{k}" for k in loads] + [f"x_in{n}" for n in range(TT)]
        g = {name: sem(name) for name in names}
        x, ob, ident, mask = env.x, env.ob, env.ident, env.parity_mask


        def tiles(eng, body):
            with eng.Fori(0, TT // 2) as turn:
                body(turn)

        with nc.Block() as block:

            @block.sync
            def _(sp):
                for n in range(2):
                    sp.dma_start(x[:, n, :], x_src[n]).then_inc(g[f"x_in{n}"], 16)
                for k in ("wo_x", "bo_x"):
                    sp.dma_start(loads[k], raw[k]).then_inc(g[f"load_{k}"], 16)
                for k in loads:
                    if k not in ("wo_x", "bo_x"):
                        sp.dma_start(loads[k], raw[k]).then_inc(g[f"load_{k}"], 16)
                for n in range(2, TT):
                    sp.dma_start(x[:, n, :], x_src[n]).then_inc(g[f"x_in{n}"], 16)

            @block.gpsimd
            def _(pool):
                pool.memset(half1[:, :], -0.5).then_inc(g["const"], 1)
                pool.memset(eps1[:, :], LN_EPS).then_inc(g["const"], 1)

                def body(turn):
                    for u in two:
                        n = 2 * turn + u
                        pool.wait_ge(g["x_done"], n + 1)
                        pool.tensor_tensor(xs[u][:, :], x[:, n, :], W["bo_x"], ALU.add).then_inc(g["xs_in"], 1)
                    for u in two:
                        n = 2 * turn + u
                        pool.wait_ge(g["aggr"], n + 1)
                        pool.tensor_tensor(mv[u][:, 1:2], mv[u][:, 1:2], eps1[:, :], ALU.add).then_inc(g["eps"], 1)
                        pool.wait_ge(g["eps"], n + 1)
                        pool.tensor_tensor(rs[u][:, :], mv[u][:, 1:2], half1[:, :], ALU.pow).then_inc(g["rstd"], 1)
                    if not rope:
                        for u in two:
                            n = 2 * turn + u
                            pool.wait_ge(g["xn_done"], n + 1)
                            pool.tensor_tensor(xs[u][:, :], xs[u][:, :], W["bo"], ALU.add).then_inc(g["xs2"], 1)
                pool.wait_ge(g["const"], 2)
                pool.wait_ge(g["load_bo_x"], 16)
                if not rope:
                    pool.wait_ge(g["load_bo"], 16)
                for n in range(TT):
                    pool.wait_ge(g[f"x_in{n}"], 16)
                tiles(pool, body)

            @block.scalar
            def _(act):
                act.preload_act_table(ACT.Exp)

                def ctx_evac(u, bank_, cb, done):
                    src = bank_[:, :].rearrange("p (b g a q) -> p b g a q", b=2, g=2, a=2)
                    for a in range(2):
                        for h in range(2):
                            t = act.activation(ct[u][:, a, h, :].rearrange("p (b q) -> p b q", b=2),
                                               src[:, :, h, a, :], ACT.Identity,
                                               bias=cb[:, 2 * a + h:2 * a + h + 1] if cb is not None else 0.0)
                    t.then_inc(done, 1)

                def body(turn):
                    for u in two:
                        n = 2 * turn + u
                        act.wait_ge(g["x_done"], n + 1)
                        act.activation(o[u][:, :, :], ob[:, bass.ds(n * 2, 2), :], ACT.Copy).then_inc(g["o_in"], 1)
                    for u in two:
                        n = 2 * turn + u
                        act.wait_ge(g["tr1"], n + 1)
                        ctx_evac(u, bank[u][0], W["cb_x"], g["ct1"])
                    for u in two:
                        n = 2 * turn + u
                        act.wait_ge(g["tr2"], n + 1)
                        act.activation(xt[u][:, :, :], bank[u][0][:, :].rearrange("p (c n) -> p c n", c=4),
                                       ACT.Copy).then_inc(g["xt_done"], 1)
                    for u in two:
                        n = 2 * turn + u
                        act.wait_ge(g["v_done"], n + 1)
                        if rope:
                            act.activation(v32[u][:, :].rearrange("p (k j d) -> p k j d", k=4, j=4),
                                           bank[u][1][:, 0:kvw].rearrange("p (k d) -> p k d", k=4)
                                           .unsqueeze(2).broadcast_to([P, 4, 4, HD]), ACT.Copy)\
                                .then_inc(g["v32_done"], 1)
                        else:
                            act.activation(v32[u][:, :], bank[u][1][:, :], ACT.Copy).then_inc(g["v32_done"], 1)
                    for u in two:
                        n = 2 * turn + u
                        act.wait_ge(g["tr4"], n + 1)
                        act.activation(kt[u][:, :, :], bank[u][2][:, :].rearrange("p (c n) -> p c n", c=4),
                                       ACT.Copy).then_inc(g["kt_done"], 1)
                    for u in two:
                        n = 2 * turn + u
                        act.wait_ge(g["sub_done"], n + 1)
                        act.activation(pr[u][:, :, :, :, :], pr[u][:, :, :, :, :], ACT.Exp,
                                       scale=SCALE).then_inc(g["exp_done"], 1)
                    for u in two:
                        n = 2 * turn + u
                        for j, k in enumerate((0, 2)):
                            act.wait_ge(g["tr5"], 2 * n + j + 1)
                            act.activation(pt[u][:, 4 * j:4 * j + 4, :],
                                           bank[u][k][:, :].rearrange("p (c n) -> p c n", c=4),
                                           ACT.Copy).then_inc(g["pt_done"], 1)
                    for u in two:
                        n = 2 * turn + u
                        act.wait_ge(g["tr6"], n + 1)
                        ctx_evac(u, bank[u][0], W.get("cb"), g["ct2"])
                if not rope:
                    act.wait_ge(g["load_cb"], 16)
                tiles(act, body)

            @block.vector
            def _(dve):
                dve.sem_inc(g["x_done"], 2)
                for k in ("sink", "cos", "sin") if rope else ("bq", "bk"):
                    dve.wait_ge(g[f"load_{k}"], 16)
                if rope:
                    dve.tensor_scalar(W["sink"], W["sink"], 1.0 / SCALE, None, ALU.mult).then_inc(g["sink_ok"], 1)
                    dve.wait_ge(g["sink_ok"], 1)

                def body(turn):
                    for u in two:
                        n = 2 * turn + u
                        dve.wait_ge(g["y1"], n + 1)
                        dve.wait_ge(g["xs_in"], n + 1)
                        dve.tensor_tensor(xs[u][:, :], bank[u][1][:, :], xs[u][:, :], ALU.add).then_inc(g["res1"], 1)
                    for u in two:
                        n = 2 * turn + u
                        dve.wait_ge(g["res1"], n + 1)
                        dve.bn_stats(stats[u][:, :], xs[u][:, :]).then_inc(g["stat"], 1)
                    for u in two:
                        n = 2 * turn + u
                        dve.wait_ge(g["stat"], n + 1)
                        dve.sem_inc(g["seen"], 1)
                        dve.bn_aggr(mv[u][:, :], stats[u][:, :]).then_inc(g["aggr"], 1)
                    for u in two:
                        n = 2 * turn + u
                        dve.wait_ge(g["rstd"], n + 1)
                        dve.tensor_scalar(xn[u][:, :], xs[u][:, :], mv[u][:, 0:1], rs[u][:, 0:1], ALU.subtract,
                                          ALU.mult).then_inc(g["xn_done"], 1)
                    for u in two:
                        n = 2 * turn + u
                        if not rope:
                            dve.wait_ge(g["q_done"], n + 1)
                            dve.tensor_tensor(q32[u][:, :], bank[u][2][:, :], W["bq"], ALU.add)\
                                .then_inc(g["q32_done"], 1)
                            dve.wait_ge(g["k_done"], n + 1)
                            dve.tensor_tensor(k32[u][:, :], bank[u][3][:, :], W["bk"], ALU.add)\
                                .then_inc(g["k32_done"], 1)
                            continue
                        for which, (src, w, dst) in enumerate(((bank[u][2], D, q32[u]), (bank[u][3], kvw, kr[u]))):
                            dve.wait_ge(g["k_done" if which else "q_done"], n + 1)
                            hs = w // HD
                            s4 = src[:, 0:w].rearrange("p (h f e) -> p h f e", h=hs, e=2)
                            d4 = dst[:, :].rearrange("p (h f e) -> p h f e", h=hs, e=2)
                            cos = W["cos"].unsqueeze(1).broadcast_to([P, hs, 16])
                            sin = W["sin"].unsqueeze(1).broadcast_to([P, hs, 16])
                            ta = rt[u][:, 0, 0:w // 2].rearrange("p (h f) -> p h f", h=hs)
                            tb = rt[u][:, 1, 0:w // 2].rearrange("p (h f) -> p h f", h=hs)
                            base = 2 * (2 * n + which)
                            for e, (ca, cb, op) in enumerate(((cos, sin, ALU.subtract), (sin, cos, ALU.add))):
                                if e:
                                    dve.wait_ge(g["rope_c"], base + 1)
                                dve.tensor_tensor(ta, s4[:, :, :, 0], ca, ALU.mult).then_inc(g["rope_a"], 1)
                                dve.tensor_tensor(tb, s4[:, :, :, 1], cb, ALU.mult).then_inc(g["rope_b"], 1)
                                dve.wait_ge(g["rope_a"], base + e + 1)
                                dve.wait_ge(g["rope_b"], base + e + 1)
                                dve.tensor_tensor(d4[:, :, :, e], ta, tb, op).then_inc(g["rope_c"], 1)
                            dve.wait_ge(g["rope_c"], base + 2)
                            if which:
                                dve.tensor_copy(k32[u][:, :].rearrange("p (k j d) -> p k j d", k=4, j=4),
                                                kr[u][:, :].rearrange("p (k d) -> p k d", k=4).unsqueeze(2)
                                                .broadcast_to([P, 4, 4, HD])).then_inc(g["k32_done"], 1)
                    for u in two:
                        n = 2 * turn + u
                        dve.wait_ge(g["tr3"], n + 1)
                        for a in range(2):
                            t = dve.tensor_scalar(qb[u][:, :, :, a, :], bank[u][0][:, :].rearrange(
                                "p (g b q) -> p g b q", g=4, b=2), mask[:, a:a + 1], None, ALU.mult)
                        t.then_inc(g["qb_done"], 1)
                    for u in two:
                        n = 2 * turn + u
                        for r in range(2):
                            dve.wait_ge(g["sc_done"], 2 * n + r + 1)
                            s = bank[u][2 + r][:, :].rearrange("p (g b k) -> p g b k", g=4, b=2)
                            dst = pr[u][:, :, r, :, :]
                            m = mx[u][:, :, r, :]
                            if rope:
                                dve.tensor_tensor(dst.rearrange("p g b k -> p g (b k)"),
                                                  s.rearrange("p g b k -> p g (b k)"),
                                                  W["sink"][:, :, r:r + 1].broadcast_to([P, 4, P]), ALU.add)\
                                    .then_inc(g["z_done"], 1)
                                dve.wait_ge(g["z_done"], 2 * n + r + 1)
                                s = dst
                            dve.tensor_reduce(m, s, AX.X, ALU.max).then_inc(g["mx_done"], 1)
                            dve.wait_ge(g["mx_done"], 2 * n + r + 1)
                            t = dve.tensor_tensor(dst, s, m.unsqueeze(3).broadcast_to([P, 4, 2, 64]), ALU.subtract)
                        t.then_inc(g["sub_done"], 1)
                    for u in two:
                        n = 2 * turn + u
                        dve.wait_ge(g["exp_done"], n + 1)
                        dve.tensor_reduce(ls[u][:, :, :, :], pr[u][:, :, :, :, :], AX.X, ALU.add).then_inc(g["ls_done"], 1)
                    for u in two:
                        n = 2 * turn + u
                        dve.wait_ge(g["ls_done"], n + 1)
                        dve.reciprocal(rl[u][:, :, :, :], ls[u][:, :, :, :]).then_inc(g["rl_done"], 1)
                    for u in two:
                        n = 2 * turn + u
                        dve.wait_ge(g["rl_done"], n + 1)
                        dve.wait_ge(g["pv_done"], n + 1)
                        for b in range(2):
                            src = bank[u][1 + 2 * b][:, :].rearrange("p (a n d) -> p a n d", a=8, n=2)
                            for a in range(2):
                                rows = slice(64 * a, 64 * a + 64)
                                t = dve.tensor_tensor(
                                    o[u][rows, b, :].rearrange("p (a d) -> p a d", a=8), src[rows, :, a, :],
                                    rl[u][rows, :, :, b].rearrange("p g r -> p (g r)").unsqueeze(2)
                                    .broadcast_to([64, 8, HD]), ALU.mult)
                        t.then_inc(g["o_done"], 1)
                    for u in two:
                        n = 2 * turn + u
                        dve.wait_ge(g["y2"], n + 1)
                        if not rope:
                            dve.wait_ge(g["xs2"], n + 1)
                        dve.tensor_tensor(x[:, n, :], bank[u][2][:, :], xs[u][:, :], ALU.add).then_inc(g["x_done"], 1)
                tiles(dve, body)

            @block.tensor
            def _(pe):
                def out_product(n, u, w, out, done):
                    for k in range(4):
                        t = pe.matmul(out[:, :], ct[u][:, k // 2, k % 2, :], w[:, k, :], start=(k == 0), stop=(k == 3))
                    t.then_inc(done, 1)

                def transpose4(src, out, done):
                    for k in range(4):
                        t = pe.transpose(out[:, k * P:(k + 1) * P], src[:, k * P:(k + 1) * P], ident[:, :])
                    t.then_inc(done, 1)

                def flat(t):
                    return t[:, :, :].rearrange("p b n -> p (b n)")

                def body(turn):
                    for u in two:
                        n = 2 * turn + u
                        pe.wait_ge(g["o_in"], n + 1)
                        transpose4(flat(o[u]), bank[u][0], g["tr1"])
                    for u in two:
                        n = 2 * turn + u
                        pe.wait_ge(g["ct1"], n + 1)
                        out_product(n, u, W["wo_x"], bank[u][1], g["y1"])
                    for u in two:
                        n = 2 * turn + u
                        pe.wait_ge(g["xn_done"], n + 1)
                        transpose4(xn[u], bank[u][0], g["tr2"])
                    for u in two:
                        n = 2 * turn + u
                        pe.wait_ge(g["xt_done"], n + 1)
                        for w, out, done, width in ((W["wq"], bank[u][2], "q_done", D), (W["wk"], bank[u][3], "k_done", kvw),
                                                    (W["wv"], bank[u][1], "v_done", kvw)):
                            for k in range(4):
                                t = pe.matmul(out[:, 0:width], xt[u][:, k, :], w[:, k, :], start=(k == 0), stop=(k == 3))
                            t.then_inc(g[done], 1)
                    for u in two:
                        n = 2 * turn + u
                        if rope:
                            pe.wait_ge(g["rope_c"], 4 * n + 2)
                        else:
                            pe.wait_ge(g["q32_done"], n + 1)
                        transpose4(q32[u], bank[u][0], g["tr3"])
                        pe.wait_ge(g["k32_done"], n + 1)
                        transpose4(k32[u], bank[u][2], g["tr4"])
                    for u in two:
                        n = 2 * turn + u
                        pe.wait_ge(g["qb_done"], n + 1)
                        pe.wait_ge(g["kt_done"], n + 1)
                        for r in range(2):
                            rows = slice(64 * r, 64 * r + 64)
                            for c in range(4):
                                for b in range(2):
                                    at = (c * 2 + b) * 64
                                    t = pe.matmul(bank[u][2 + r][:, at:at + 64],
                                                  qb[u][rows, c, b, :, :].rearrange("p a q -> p (a q)"),
                                                  kt[u][rows, c, 64 * b:64 * b + 64], start=True, stop=True)
                            t.then_inc(g["sc_done"], 1)
                    for u in two:
                        n = 2 * turn + u
                        pe.wait_ge(g["exp_done"], n + 1)
                        for j, k in enumerate((0, 2)):
                            for i in range(4):
                                pair = 4 * j + i
                                t = pe.transpose(bank[u][k][:, i * P:(i + 1) * P],
                                                 pr[u][:, pair // 2, pair % 2, :, :].rearrange("p b k -> p (b k)"),
                                                 ident[:, :])
                            t.then_inc(g["tr5"], 1)
                    for u in two:
                        n = 2 * turn + u
                        pe.wait_ge(g["pt_done"], 2 * n + 2)
                        pe.wait_ge(g["v32_done"], n + 1)
                        for b in range(2):
                            rows = slice(64 * b, 64 * b + 64)
                            for pair in range(8):
                                t = pe.matmul(bank[u][1 + 2 * b][:, pair * 64:(pair + 1) * 64], pt[u][rows, pair, :],
                                              v32[u][rows, pair * 64:(pair + 1) * 64], start=True, stop=True)
                        t.then_inc(g["pv_done"], 1)
                    for u in two:
                        n = 2 * turn + u
                        pe.wait_ge(g["o_done"], n + 1)
                        transpose4(flat(o[u]), bank[u][0], g["tr6"])
                    for u in two:
                        n = 2 * turn + u
                        pe.wait_ge(g["ct2"], n + 1)
                        out_product(n, u, W["wo"], bank[u][2], g["y2"])
                for k in ("wo_x", "wq", "wk", "wv", "wo"):
                    pe.wait_ge(g[f"load_{k}"], 16)
                tiles(pe, body)
        nc.clear_and_free_semaphores(sems)
        nc.all_engine_barrier()


E, TOPK, HID = 32, 4, 256
CAP = 2 * B * S * TOPK // E
SLOTS = E * CAP
ROUTE_STEPS = 34


class Steps:

    def __init__(self, eng, sem, turn, per):
        self.eng, self.sem, self.turn, self.per, self.n = eng, sem, turn, per, 0

    def link(self, ins):
        self.n += 1
        ins.then_inc(self.sem, 1)
        self.eng.wait_ge(self.sem, self.turn * self.per + self.n)


def moe_ffn(nc, env, raw, h_dram, slot_dram, eo_dram, x_out):
    with ExitStack() as outer:
        pre = env.prefix
        osb = lambda name, shape, dt=F32: outer.enter_context(nc.sbuf_tensor(pre + name, shape, dt))
        wts = osb("wts", [P, TT, TOPK])
        cidx = osb("cidx", [P, TT, TOPK], I32)
        x, ident = env.x, env.ident
        two = range(2)

        with ExitStack() as ctx:
            sb = lambda name, shape, dt=F32: ctx.enter_context(nc.sbuf_tensor(pre + name, shape, dt))
            sems = []

            def sem(name):
                s = ctx.enter_context(nc.semaphore(pre + name))
                sems.append(s)
                return s

            bank = [[ctx.enter_context(nc.psum_tensor(f"{pre}bank{u}{k}", [P, 512], F32)) for k in range(4)]
                    for u in two]
            gate = sb("gate", [P, 4 * E])
            sgu = sb("sgu", [P, 4, 2 * HID])
            sd = sb("sd", [P, 2, D])
            nw = sb("nw", [P, D])
            upper = sb("upper", [P, P])
            ones = sb("ones", [P, P])
            iota = sb("iota", [P, E])
            tok = sb("tok", [P, TT], I32)
            zero = sb("zero", [P, SLOTS // P], I32)
            half = sb("half", [P, 1])
            eps = sb("eps", [P, 2])
            acc = [sb(f"acc{u}", [P, E]) for u in two]
            h0 = [sb(f"h0{u}", [P, D]) for u in two]
            h = [sb(f"h{u}", [P, D]) for u in two]
            sq = [sb(f"sq{u}", [P, D]) for u in two]
            ht = [sb(f"ht{u}", [P, 4, P]) for u in two]
            stats = [sb(f"stats{u}", [P, 6]) for u in two]
            mv = [sb(f"mv{u}", [P, 2]) for u in two]
            rs = [sb(f"rs{u}", [P, 1]) for u in two]
            ms = [sb(f"ms{u}", [P, 1]) for u in two]
            r2 = [sb(f"r2{u}", [P, 1]) for u in two]
            lg = [sb(f"lg{u}", [P, E]) for u in two]
            top = [sb(f"top{u}", [P, 8]) for u in two]
            top_i = [sb(f"topi{u}", [P, 8], U32) for u in two]
            top_f = [sb(f"topf{u}", [P, 8]) for u in two]
            ntop = [sb(f"ntop{u}", [P, 1]) for u in two]
            ex = [sb(f"ex{u}", [P, TOPK]) for u in two]
            es = [sb(f"es{u}", [P, 1]) for u in two]
            er = [sb(f"er{u}", [P, 1]) for u in two]
            oh = [sb(f"oh{u}", [P, TOPK, E]) for u in two]
            oh2 = [sb(f"oh2{u}", [P, TOPK, E]) for u in two]
            cnt = [sb(f"cnt{u}", [P, E]) for u in two]
            pos = [sb(f"pos{u}", [P, E]) for u in two]
            pk = [sb(f"pk{u}", [P, TOPK]) for u in two]
            t1 = [sb(f"t1{u}", [P, TOPK]) for u in two]
            t2 = [sb(f"t2{u}", [P, TOPK]) for u in two]
            sidx = [sb(f"sidx{u}", [P, TOPK], I32) for u in two]
            tid = [sb(f"tid{u}", [P, 1], I32) for u in two]
            sg = [sb(f"sg{u}", [P, HID]) for u in two]
            sa = [sb(f"sa{u}", [P, 2, P]) for u in two]

            names = ("seen w_in const zero_in stat aggr eps rstd h0_done ms_done eps2 r2_done h_done xh_done h_out0 h_out1 "
                     "tr ht_done lg_done sh_done lgc_done top_done exp_done cnt_done acc_done pos_done posc_done route "
                     "sidx_done tid_done scat0 scat1 scat_done silu_done sa_done y_done x_done").split()
            g = {name: sem(name) for name in names}

            with nc.Block() as block:

                @block.sync
                def _(sp):
                    for dst, src in ((nw[:, :], "nw"), (gate[:, :], "gate"), (upper[:, :], "upper"), (iota[:, :], "iota"),
                                     (tok[:, :], "tok"), (sgu[:, :, :].rearrange("p k n -> p (k n)"), "sgu"),
                                     (sd[:, :, :].rearrange("p k n -> p (k n)"), "sd")):
                        sp.dma_start(dst, raw[src]).then_inc(g["w_in"], 16)
                    sp.wait_ge(g["const"], 1)
                    sp.dma_start(slot_dram.rearrange("(p s) o -> p (s o)", p=P), zero[:, :]).then_inc(g["zero_in"], 16)
                    with sp.Fori(0, TT // 2) as turn:
                        for u in two:
                            sp.wait_ge(g["h_done"], 2 * turn + u + 1)
                            sp.dma_start(h_dram[2 * turn + u], h[u][:, :]).then_inc(g[f"h_out{u}"], 16)
                    for u in two:
                        sp.wait_ge(g[f"h_out{u}"], 16 + 16 * (TT // 2))
                        sp.wait_ge(g[f"scat{u}"], 64 * (TT // 2))
                    sp.wait_ge(g["zero_in"], 16)

                @block.gpsimd
                def _(pool):
                    pool.memset(zero[:, :], 0).then_inc(g["const"], 1)
                    pool.memset(half[:, :], -0.5).then_inc(g["const"], 1)
                    pool.memset(ones[:, :], 1.0).then_inc(g["const"], 1)
                    pool.memset(acc[0][:, :], 0.0).then_inc(g["const"], 1)
                    pool.memset(eps[:, 0:1], LN_EPS).then_inc(g["const"], 1)
                    pool.memset(eps[:, 1:2], HEAD_EPS).then_inc(g["const"], 1)
                    pool.wait_ge(g["const"], 6)
                    pool.wait_ge(g["w_in"], 16 * 7)
                    pool.wait_ge(g["zero_in"], 16)
                    with pool.Fori(0, TT // 2) as turn:
                        for u in two:
                            n = 2 * turn + u
                            pool.wait_ge(g["aggr"], n + 1)
                            pool.tensor_tensor(mv[u][:, 1:2], mv[u][:, 1:2], eps[:, 0:1], ALU.add).then_inc(g["eps"], 1)
                            pool.wait_ge(g["eps"], n + 1)
                            pool.tensor_tensor(rs[u][:, :], mv[u][:, 1:2], half[:, :], ALU.pow).then_inc(g["rstd"], 1)
                        for u in two:
                            n = 2 * turn + u
                            pool.wait_ge(g["ms_done"], n + 1)
                            pool.tensor_tensor(ms[u][:, :], ms[u][:, :], eps[:, 1:2], ALU.add).then_inc(g["eps2"], 1)
                            pool.wait_ge(g["eps2"], n + 1)
                            pool.tensor_tensor(r2[u][:, :], ms[u][:, :], half[:, :], ALU.pow).then_inc(g["r2_done"], 1)
                        for u in two:
                            n = 2 * turn + u
                            pool.tensor_tensor(x[:, n, :], x[:, n, :], h0[u][:, :], ALU.add).then_inc(g["xh_done"], 1)
                            pool.sem_inc(g["seen"], 1)
                            pool.tensor_copy(tid[u][:, :], tok[:, bass.ds(n, 1)]).then_inc(g["tid_done"], 1)
                        for u in two:
                            n = 2 * turn + u
                            pool.wait_ge(g["tid_done"], n + 1)
                            pool.wait_ge(g["sidx_done"], n + 1)
                            pool.sem_inc(g["seen"], 1)
                            for k in range(TOPK):
                                pool.indirect_dma_start(slot_dram, bass.IndirectOffsetOnAxis(ap=sidx[u][:, k:k + 1], axis=0),
                                                        tid[u][:, 0:1], None, bounds_check=SLOTS - 1, oob_is_err=False)\
                                    .then_inc(g[f"scat{u}"], 16)
                        for u in two:
                            pool.wait_ge(g[f"scat{u}"], 64 * turn + 64)
                            pool.sem_inc(g["scat_done"], 1)

                @block.scalar
                def _(act):
                    for u in two:
                        act.sem_inc(g[f"h_out{u}"], 16)
                    with act.Fori(0, TT // 2) as turn:
                        for u in two:
                            n = 2 * turn + u
                            act.wait_ge(g["h0_done"], n + 1)
                            act.activation(sq[u][:, :], h0[u][:, :], ACT.Square, scale=float(D) ** -0.5,
                                           accum_out=ms[u][:, :]).then_inc(g["ms_done"], 1)
                        for u in two:
                            n = 2 * turn + u
                            act.wait_ge(g["tr"], n + 1)
                            act.activation(ht[u][:, :, :], bank[u][0][:, :].rearrange("p (c n) -> p c n", c=4), ACT.Copy)\
                                .then_inc(g["ht_done"], 1)
                        for u in two:
                            n = 2 * turn + u
                            act.wait_ge(g["sh_done"], n + 1)
                            act.activation(sg[u][:, :], bank[u][2][:, 0:HID], ACT.Silu).then_inc(g["silu_done"], 1)
                        for u in two:
                            n = 2 * turn + u
                            act.wait_ge(g["top_done"], n + 1)
                            act.activation(ex[u][:, :], top[u][:, 0:TOPK], ACT.Exp, bias=ntop[u][:, :],
                                           accum_out=es[u][:, :]).then_inc(g["exp_done"], 1)

                @block.vector
                def _(dve):
                    dve.wait_ge(g["w_in"], 16 * 7)
                    dve.wait_ge(g["const"], 4)
                    dve.sem_inc(g["scat_done"], 2)
                    with dve.Fori(0, TT // 2) as turn:
                        steps = Steps(dve, g["route"], turn, ROUTE_STEPS)
                        for u in two:
                            dve.bn_stats(stats[u][:, :], x[:, 2 * turn + u, :]).then_inc(g["stat"], 1)
                        for u in two:
                            dve.wait_ge(g["stat"], 2 * turn + u + 1)
                            dve.sem_inc(g["seen"], 1)
                            dve.bn_aggr(mv[u][:, :], stats[u][:, :]).then_inc(g["aggr"], 1)
                        for u in two:
                            n = 2 * turn + u
                            dve.wait_ge(g["rstd"], n + 1)
                            dve.tensor_scalar(h0[u][:, :], x[:, n, :], mv[u][:, 0:1], rs[u][:, 0:1], ALU.subtract,
                                              ALU.mult).then_inc(g["h0_done"], 1)
                        for u in two:
                            n = 2 * turn + u
                            dve.wait_ge(g["r2_done"], n + 1)
                            dve.wait_ge(g[f"h_out{u}"], 16 * turn + 16)
                            dve.scalar_tensor_tensor(out=h[u][:, :], in0=h0[u][:, :], scalar=r2[u][:, :], in1=nw[:, :],
                                                     op0=ALU.mult, op1=ALU.mult).then_inc(g["h_done"], 1)
                        for u in two:
                            n = 2 * turn + u
                            dve.wait_ge(g["lg_done"], n + 1)
                            steps.link(dve.tensor_copy(lg[u][:, :], bank[u][1][:, 0:E]))
                            dve.sem_inc(g["seen"], 1)
                            steps.link(dve.max(top[u][:, :], lg[u][:, :]))
                            dve.tensor_scalar(ntop[u][:, :], top[u][:, 0:1], -1.0, None, ALU.mult).then_inc(g["top_done"], 1)
                            dve.sem_inc(g["seen"], 1)
                            steps.link(dve.max_index(top_i[u][:, :], top[u][:, :], lg[u][:, :]))
                            steps.link(dve.tensor_copy(top_f[u][:, :], top_i[u][:, :]))
                            steps.link(dve.tensor_tensor(
                                oh[u][:, :, :], iota[:, :].unsqueeze(1).broadcast_to([P, TOPK, E]),
                                top_f[u][:, 0:TOPK].unsqueeze(2).broadcast_to([P, TOPK, E]), ALU.is_equal))
                            dve.tensor_reduce(cnt[u][:, :], oh[u][:, :, :].rearrange("p k e -> p e k"), AX.X, ALU.add)\
                                .then_inc(g["cnt_done"], 1)
                        dve.wait_ge(g["cnt_done"], 2 * turn + 1)
                        dve.tensor_tensor(acc[1][:, :], acc[0][:, :], cnt[0][:, :], ALU.add).then_inc(g["acc_done"], 1)
                        for u in two:
                            n = 2 * turn + u
                            dve.wait_ge(g["silu_done"], n + 1)
                            dve.tensor_tensor(sa[u][:, :, :], bank[u][2][:, HID:2 * HID].rearrange("p (c n) -> p c n", c=2),
                                              sg[u][:, :].rearrange("p (c n) -> p c n", c=2), ALU.mult)\
                                .then_inc(g["sa_done"], 1)
                        for u in two:
                            n = 2 * turn + u
                            dve.wait_ge(g["exp_done"], n + 1)
                            steps.link(dve.reciprocal(er[u][:, :], es[u][:, :]))
                            dve.tensor_scalar(wts[:, n, :], ex[u][:, :], er[u][:, :], None, ALU.mult)
                            dve.wait_ge(g["pos_done"], n + 1)
                            steps.link(dve.tensor_copy(pos[u][:, :], bank[u][1][:, 64:64 + E]))
                            steps.link(dve.tensor_tensor(oh2[u][:, :, :], oh[u][:, :, :],
                                                         pos[u][:, :].unsqueeze(1).broadcast_to([P, TOPK, E]), ALU.mult))
                            steps.link(dve.tensor_reduce(pk[u][:, :], oh2[u][:, :, :], AX.X, ALU.add))
                            f4 = top_f[u][:, 0:TOPK]
                            steps.link(dve.tensor_scalar(t1[u][:, :], pk[u][:, :], float(P), 1.0 - 2.0 * E * P,
                                                         ALU.is_ge, ALU.mult))
                            steps.link(dve.scalar_tensor_tensor(out=t2[u][:, :], in0=f4, scalar=2.0, in1=t1[u][:, :],
                                                                op0=ALU.mult, op1=ALU.add))
                            steps.link(dve.scalar_tensor_tensor(out=t1[u][:, :], in0=pk[u][:, :], scalar=2.0 * E,
                                                                in1=t2[u][:, :], op0=ALU.mult, op1=ALU.add))
                            steps.link(dve.tensor_scalar(t2[u][:, :], pk[u][:, :], float(CAP), 1e6, ALU.is_ge, ALU.mult))
                            steps.link(dve.tensor_tensor(t1[u][:, :], t1[u][:, :], t2[u][:, :], ALU.add))
                            dve.wait_ge(g["scat_done"], n + 1)
                            dve.tensor_copy(sidx[u][:, :], t1[u][:, :]).then_inc(g["sidx_done"], 1)
                            steps.link(dve.tensor_scalar(pk[u][:, :], pk[u][:, :], float(CAP - 1), None, ALU.min))
                            steps.link(dve.scalar_tensor_tensor(out=t2[u][:, :], in0=f4, scalar=float(CAP), in1=pk[u][:, :],
                                                                op0=ALU.mult, op1=ALU.add))
                            steps.link(dve.tensor_copy(cidx[:, n, :], t2[u][:, :]))
                        dve.wait_ge(g["cnt_done"], 2 * turn + 2)
                        dve.wait_ge(g["pos_done"], 2 * turn + 2)
                        dve.tensor_tensor(acc[0][:, :], acc[1][:, :], cnt[1][:, :], ALU.add).then_inc(g["acc_done"], 1)
                        for u in two:
                            n = 2 * turn + u
                            dve.wait_ge(g["y_done"], n + 1)
                            dve.wait_ge(g["xh_done"], n + 1)
                            dve.tensor_tensor(x[:, n, :], bank[u][3][:, :], x[:, n, :], ALU.add).then_inc(g["x_done"], 1)
                        assert steps.n == ROUTE_STEPS, steps.n

                @block.tensor
                def _(pe):
                    pe.wait_ge(g["w_in"], 16 * 7)
                    pe.wait_ge(g["const"], 4)
                    with pe.Fori(0, TT // 2) as turn:
                        for u in two:
                            pe.wait_ge(g["h_done"], 2 * turn + u + 1)
                            for k in range(4):
                                t = pe.transpose(bank[u][0][:, k * P:(k + 1) * P], h[u][:, k * P:(k + 1) * P], ident[:, :])
                            t.then_inc(g["tr"], 1)
                        for u in two:
                            pe.wait_ge(g["ht_done"], 2 * turn + u + 1)
                            for k in range(4):
                                t = pe.matmul(bank[u][1][:, 0:E], ht[u][:, k, :], gate[:, k * E:(k + 1) * E],
                                              start=(k == 0), stop=(k == 3))
                            t.then_inc(g["lg_done"], 1)
                        for u in two:
                            for c in range(4):
                                for k in range(4):
                                    t = pe.matmul(bank[u][2][:, c * P:(c + 1) * P], sgu[:, k, c * P:(c + 1) * P],
                                                  ht[u][:, k, :], start=(k == 0), stop=(k == 3))
                            t.then_inc(g["sh_done"], 1)
                        for u in two:
                            n = 2 * turn + u
                            pe.wait_ge(g["cnt_done"], n + 1)
                            if u:
                                pe.wait_ge(g["acc_done"], n)
                            out = bank[u][1][:, 64:64 + E]
                            pe.matmul(out, upper[:, :], cnt[u][:, :], start=True, stop=False)
                            pe.matmul(out, ones[:, :], acc[u][:, :], start=False, stop=True).then_inc(g["pos_done"], 1)
                        for u in two:
                            pe.wait_ge(g["sa_done"], 2 * turn + u + 1)
                            for k in range(2):
                                t = pe.matmul(bank[u][3][:, :], sa[u][:, k, :], sd[:, k, :], start=(k == 0), stop=(k == 1))
                            t.then_inc(g["y_done"], 1)
            nc.clear_and_free_semaphores(sems)
            nc.all_engine_barrier()

        with ExitStack() as ctx:
            pre = env.prefix + "e_"
            sb = lambda name, shape, dt=F32: ctx.enter_context(nc.sbuf_tensor(pre + name, shape, dt))
            sems = []

            def sem2(name):
                s = ctx.enter_context(nc.semaphore(pre + name))
                sems.append(s)
                return s

            bank = [ctx.enter_context(nc.psum_tensor(f"{pre}bank{k}", [P, 512], F32)) for k in range(6)]
            tab = sb("tab", [P, SLOTS // P], I32)
            idx = [[sb(f"idx{u}{j}", [P, 1], I32) for j in range(2)] for u in two]
            w13 = [sb(f"w13{u}", [P, 4, 2 * HID]) for u in two]
            w2 = [sb(f"w2{u}", [P, 2, D]) for u in two]
            rows = [sb(f"rows{u}", [P, 2, D]) for u in two]
            gt = [sb(f"gt{u}", [P, 4, CAP]) for u in two]
            sg = sb("sg", [P, 2 * CAP])
            aT = [sb(f"at{u}", [P, 2, CAP]) for u in two]
            eo = [sb(f"eo{u}", [P, 2, D]) for u in two]
            names = ("seen tab_in w13_in0 w13_in1 w2_in0 w2_in1 idx_done rows_in0 rows_in1 tr_done gt_a gt_b gu_done silu_done "
                     "act_done out_done eo_a eo_b eo_out0 eo_out1").split()
            g = {name: sem2(name) for name in names}
            PAIRS_E = E // 2
            eo_rows = eo_dram.rearrange("(e j p) d -> e p j d", e=E, p=P)

            with nc.Block() as block:

                @block.sync
                def _(sp):
                    def load(e, u):
                        sp.dma_start(w13[u][:, :, :].rearrange("p k n -> p (k n)"), raw["w13"][e]).then_inc(g[f"w13_in{u}"], 16)
                        sp.dma_start(w2[u][:, :, :].rearrange("p k n -> p (k n)"), raw["w2"][e]).then_inc(g[f"w2_in{u}"], 16)

                    def store(e, u):
                        sp.wait_ge(g["eo_a"], e + 1)
                        sp.wait_ge(g["eo_b"], e + 1)
                        sp.dma_start(eo_rows[e], eo[u][:, :, :]).then_inc(g[f"eo_out{u}"], 16)

                    sp.dma_start(tab[:, :], slot_dram.rearrange("(p s) o -> p (s o)", p=P)).then_inc(g["tab_in"], 16)
                    for u in two:
                        load(u, u)
                    with sp.Fori(0, PAIRS_E - 1) as turn:
                        for u in two:
                            e = 2 * turn + u
                            sp.wait_ge(g["out_done"], e + 1)
                            load(e + 2, u)
                            store(e, u)
                    for u in two:
                        store(E - 2 + u, u)
                    for u in two:
                        sp.wait_ge(g[f"eo_out{u}"], 16 + 16 * PAIRS_E)

                @block.gpsimd
                def _(pool):
                    pool.wait_ge(g["tab_in"], 16)

                    def gather(e, u, turn, first):
                        if not first:
                            pool.wait_ge(g[f"rows_in{u}"], 32 * turn)
                            pool.sem_inc(g["seen"], 1)
                        for j in range(2):
                            pool.tensor_copy(idx[u][j][:, :], tab[:, bass.ds(2 * e + j, 1)]).then_inc(g["idx_done"], 1)
                        if not first:
                            pool.wait_ge(g["tr_done"], e - 1)
                        pool.wait_ge(g["idx_done"], 2 * e + 2)
                        pool.sem_inc(g["seen"], 1)
                        for j in range(2):
                            pool.indirect_dma_start(rows[u][:, j, :], None, h_dram.rearrange("t p d -> (t p) d"),
                                                    bass.IndirectOffsetOnAxis(ap=idx[u][j][:, 0:1], axis=0),
                                                    bounds_check=B * S - 1, oob_is_err=False)\
                                .then_inc(g[f"rows_in{u}"], 16)

                    for u in two:
                        gather(u, u, 0, True)
                    with pool.Fori(1, PAIRS_E) as turn:
                        for u in two:
                            gather(2 * turn + u, u, turn, False)

                @block.scalar
                def _(act):
                    act.preload_act_table(ACT.Silu)
                    for u in two:
                        act.sem_inc(g[f"eo_out{u}"], 16)

                    def evac_t(e, u):
                        act.wait_ge(g["tr_done"], e + 1)
                        act.activation(gt[u][:, :, 0:P], bank[0][:, :].rearrange("p (c n) -> p c n", c=4), ACT.Copy)\
                            .then_inc(g["gt_a"], 1)

                    def rest(e, u, turn, last=False):
                        act.wait_ge(g["gu_done"], e + 1)
                        act.activation(sg[:, :], bank[2][:, :], ACT.Silu).then_inc(g["silu_done"], 1)
                        if not last:
                            evac_t(e + 1, 1 - u)
                        act.wait_ge(g["out_done"], e + 1)
                        act.wait_ge(g[f"eo_out{u}"], 16 * turn + 16)
                        act.activation(eo[u][:, 0, :], bank[4][:, :], ACT.Copy).then_inc(g["eo_a"], 1)

                    evac_t(0, 0)
                    with act.Fori(0, PAIRS_E - 1) as turn:
                        for u in two:
                            rest(2 * turn + u, u, turn)
                    rest(E - 2, 0, PAIRS_E - 1)
                    rest(E - 1, 1, PAIRS_E - 1, True)

                @block.vector
                def _(dve):
                    def evac_t(e, u):
                        dve.wait_ge(g["tr_done"], e + 1)
                        dve.tensor_copy(gt[u][:, :, P:2 * P], bank[1][:, :].rearrange("p (c n) -> p c n", c=4))\
                            .then_inc(g["gt_b"], 1)

                    def rest(e, u, turn, last=False):
                        dve.wait_ge(g["silu_done"], e + 1)
                        dve.tensor_tensor(aT[u][:, :, :].rearrange("p c n -> p (c n)"), bank[3][:, :], sg[:, :], ALU.mult)\
                            .then_inc(g["act_done"], 1)
                        if not last:
                            evac_t(e + 1, 1 - u)
                        dve.wait_ge(g["out_done"], e + 1)
                        dve.wait_ge(g[f"eo_out{u}"], 16 * turn + 16)
                        dve.tensor_copy(eo[u][:, 1, :], bank[5][:, :]).then_inc(g["eo_b"], 1)

                    evac_t(0, 0)
                    with dve.Fori(0, PAIRS_E - 1) as turn:
                        for u in two:
                            rest(2 * turn + u, u, turn)
                    rest(E - 2, 0, PAIRS_E - 1)
                    rest(E - 1, 1, PAIRS_E - 1, True)

                @block.tensor
                def _(pe):
                    def tr(e, u, turn):
                        pe.wait_ge(g[f"rows_in{u}"], 32 * turn + 32)
                        for j in range(2):
                            for k in range(4):
                                t = pe.transpose(bank[j][:, k * P:(k + 1) * P], rows[u][:, j, k * P:(k + 1) * P], ident[:, :])
                        t.then_inc(g["tr_done"], 1)

                    def rest(e, u, turn, last=False):
                        pe.wait_ge(g["gt_a"], e + 1)
                        pe.wait_ge(g["gt_b"], e + 1)
                        pe.wait_ge(g[f"w13_in{u}"], 16 * turn + 16)
                        for c in range(4):
                            for k in range(4):
                                t = pe.matmul(bank[2 + c // 2][:, (c % 2) * CAP:(c % 2 + 1) * CAP],
                                              w13[u][:, k, c * P:(c + 1) * P], gt[u][:, k, :], start=(k == 0), stop=(k == 3))
                        t.then_inc(g["gu_done"], 1)
                        if not last:
                            tr(e + 1, 1 - u, turn + u)
                        pe.wait_ge(g["act_done"], e + 1)
                        pe.wait_ge(g[f"w2_in{u}"], 16 * turn + 16)
                        if not (isinstance(e, int) and e == 0):
                            pe.wait_ge(g["eo_a"], e)
                            pe.wait_ge(g["eo_b"], e)
                        for j in range(2):
                            for k in range(2):
                                t = pe.matmul(bank[4 + j][:, :], aT[u][:, k, j * P:(j + 1) * P], w2[u][:, k, :],
                                              start=(k == 0), stop=(k == 1))
                        t.then_inc(g["out_done"], 1)

                    tr(0, 0, 0)
                    rest(0, 0, 0)
                    rest(1, 1, 0)
                    with pe.Fori(1, PAIRS_E - 1) as turn:
                        for u in two:
                            rest(2 * turn + u, u, turn)
                    rest(E - 2, 0, PAIRS_E - 1)
                    rest(E - 1, 1, PAIRS_E - 1, True)
            nc.clear_and_free_semaphores(sems)
            nc.all_engine_barrier()

        with ExitStack() as ctx:
            pre = env.prefix + "c_"
            sb = lambda name, shape, dt=F32: ctx.enter_context(nc.sbuf_tensor(pre + name, shape, dt))
            got = [sb(f"got{u}", [P, TOPK, D]) for u in two]
            idx = [[sb(f"idx{u}{k}", [P, 1], I32) for k in range(TOPK)] for u in two]
            wt = [sb(f"wt{u}", [P, TOPK]) for u in two]
            names = "seen got_in0 got_in1 idx_done wt_done add_done x_out".split()
            g = {name: ctx.enter_context(nc.semaphore(pre + name)) for name in names}

            with nc.Block() as block:

                @block.gpsimd
                def _(pool):
                    with pool.Fori(0, TT // 2) as turn:
                        for u in two:
                            n = 2 * turn + u
                            pool.wait_ge(g["add_done"], TOPK * n + TOPK)
                            pool.sem_inc(g["seen"], 1)
                            for k in range(TOPK):
                                pool.tensor_copy(idx[u][k][:, :], cidx[:, n, k:k + 1]).then_inc(g["idx_done"], 1)
                            pool.wait_ge(g["idx_done"], TOPK * n + TOPK)
                            pool.sem_inc(g["seen"], 1)
                            for k in range(TOPK):
                                pool.indirect_dma_start(got[u][:, k, :], None,
                                                        eo_dram,
                                                        bass.IndirectOffsetOnAxis(ap=idx[u][k][:, 0:1], axis=0),
                                                        bounds_check=SLOTS - 1, oob_is_err=False)\
                                    .then_inc(g[f"got_in{u}"], 16)

                @block.vector
                def _(dve):
                    dve.sem_inc(g["add_done"], 2 * TOPK)
                    with dve.Fori(0, TT // 2) as turn:
                        for u in two:
                            n = 2 * turn + u
                            dve.wait_ge(g["add_done"], TOPK * n + TOPK)
                            dve.tensor_copy(wt[u][:, :], wts[:, n, :]).then_inc(g["wt_done"], 1)
                        for u in two:
                            n = 2 * turn + u
                            dve.wait_ge(g["wt_done"], n + 1)
                            dve.wait_ge(g[f"got_in{u}"], 16 * TOPK * turn + 16 * TOPK)
                            for k in range(TOPK):
                                dve.wait_ge(g["add_done"], TOPK * n + 2 * TOPK + k)
                                dve.scalar_tensor_tensor(out=x[:, n, :], in0=got[u][:, k, :], scalar=wt[u][:, k:k + 1],
                                                         in1=x[:, n, :], op0=ALU.mult, op1=ALU.add).then_inc(g["add_done"], 1)

                @block.sync
                def _(sp):
                    with sp.Fori(0, TT) as n:
                        sp.wait_ge(g["add_done"], TOPK * n + 3 * TOPK)
                        sp.dma_start(x_out[n], x[:, n, :]).then_inc(g["x_out"], 16)
                    sp.wait_ge(g["x_out"], 16 * TT)
            nc.clear_and_free_semaphores(list(g.values()))
            nc.all_engine_barrier()


FH = int(2 * D * 4 / 3)
FC = -(-FH // P)
FTAIL = FH - (FC - 1) * P
HALF_T = B * S // 2


def ternary_ffn(nc, env, raw, out):
    with ExitStack() as ctx:
        pre = env.prefix
        sb = lambda name, shape, dt=F32: ctx.enter_context(nc.sbuf_tensor(pre + name, shape, dt))
        sems = []

        def sem(name):
            s = ctx.enter_context(nc.semaphore(pre + name))
            sems.append(s)
            return s

        two = range(2)
        bank = [ctx.enter_context(nc.psum_tensor(f"{pre}bank{k}", [P, 512], F32)) for k in range(8)]
        x, ident = env.x, env.ident
        raws = [sb(f"raw{i}", [P, 4 * FH]) for i in range(2)]
        rawt = sb("rawt", [P, D])
        q1 = sb("q1", [P, 4, FH], F16)
        q3 = sb("q3", [P, 4, FH], F16)
        q2 = sb("q2", [P, FC, D], F32R)
        neg = sb("neg", [P, FC * D], BF16)
        ones = sb("ones", [P, P])
        half = sb("half", [P, 1])
        eps = sb("eps", [P, 1])
        part = sb("part", [P, 3, FC])
        tot = sb("tot", [P, 3])
        size = sb("size", [P, 3])
        thr = sb("thr", [P, 3, 2])
        stats = [sb(f"stats{u}", [P, 6]) for u in two]
        mv = [sb(f"mv{u}", [P, 2]) for u in two]
        rs = [sb(f"rs{u}", [P, 1]) for u in two]
        h = [sb(f"h{u}", [P, D]) for u in two]
        hh = sb("hh", [P, 4, B * S], F16)
        hl = sb("hl", [P, 4, B * S], F16)
        sg = [sb(f"sg{u}", [P, HALF_T]) for u in two]
        gg = [sb(f"gg{u}", [P, HALF_T]) for u in two]
        gh = sb("gh", [P, FC, HALF_T], F32R)
        gl = sb("gl", [P, FC, HALF_T], F32R)
        o = h

        names = ("seen w1_in w3_in w2_in const part_done tot_done size_done s1 thr_done neg_done q_done stat aggr eps_done rstd h_done "
                 "tr hh_done hl_done p1_done p3_done silu_done gg_done gh_done gl_done y_done o_done o_out0 o_out1").split()
        g = {name: sem(name) for name in names}

        with nc.Block() as block:

            @block.sync
            def _(sp):
                sp.dma_start(raws[0][:, :], raw["w1"]).then_inc(g["w1_in"], 16)
                sp.dma_start(raws[1][:, 0:4 * FH], raw["w3"]).then_inc(g["w3_in"], 16)
                sp.wait_ge(g["q_done"], 1)
                sp.dma_start(raws[0][:, 0:(FC - 1) * D].rearrange("p (c d) -> p c d", d=D), raw["w2"])\
                    .then_inc(g["w2_in"], 16)
                sp.wait_ge(g["const"], 4)
                sp.dma_start(rawt[0:FTAIL, :], raw["w2t"]).then_inc(g["w2_in"], 16)
                with sp.Fori(0, TT // 2) as turn:
                    for u in two:
                        sp.wait_ge(g["o_done"], 2 * turn + u + 3)
                        sp.dma_start(out[2 * turn + u], o[u][:, :]).then_inc(g[f"o_out{u}"], 16)
                for u in two:
                    sp.wait_ge(g[f"o_out{u}"], 16 + 16 * (TT // 2))

            @block.gpsimd
            def _(pool):
                pool.memset(ones[:, :], 1.0).then_inc(g["const"], 1)
                pool.memset(half[:, :], -0.5).then_inc(g["const"], 1)
                pool.memset(eps[:, :], LN_EPS).then_inc(g["const"], 1)
                pool.memset(rawt[:, :], 0.0).then_inc(g["const"], 1)
                pool.wait_ge(g["const"], 4)
                with pool.Fori(0, TT // 2) as turn:
                    for u in two:
                        n = 2 * turn + u
                        pool.wait_ge(g["aggr"], n + 1)
                        pool.tensor_tensor(mv[u][:, 1:2], mv[u][:, 1:2], eps[:, :], ALU.add).then_inc(g["eps_done"], 1)
                        pool.wait_ge(g["eps_done"], n + 1)
                        pool.tensor_tensor(rs[u][:, :], mv[u][:, 1:2], half[:, :], ALU.pow).then_inc(g["rstd"], 1)

            @block.vector
            def _(dve):
                dve.wait_ge(g["const"], 4)
                for name in ("gg_done", "gl_done", "o_done"):
                    dve.sem_inc(g[name], 2)
                with dve.Fori(0, TT // 2) as turn:
                    for u in two:
                        dve.bn_stats(stats[u][:, :], x[:, 2 * turn + u, :]).then_inc(g["stat"], 1)
                    for u in two:
                        dve.wait_ge(g["stat"], 2 * turn + u + 1)
                        dve.sem_inc(g["seen"], 1)
                        dve.bn_aggr(mv[u][:, :], stats[u][:, :]).then_inc(g["aggr"], 1)
                    for u in two:
                        n = 2 * turn + u
                        dve.wait_ge(g["rstd"], n + 1)
                        dve.tensor_scalar(h[u][:, :], x[:, n, :], mv[u][:, 0:1], rs[u][:, 0:1], ALU.subtract,
                                          ALU.mult).then_inc(g["h_done"], 1)
                    for u in two:
                        n = 2 * turn + u
                        dve.wait_ge(g["hh_done"], n + 1)
                        dve.tensor_tensor(hl[:, :, bass.ds(n * P, P)], bank[u][:, :].rearrange("p (c n) -> p c n", c=4),
                                          hh[:, :, bass.ds(n * P, P)], ALU.subtract).then_inc(g["hl_done"], 1)

                def sizes(i, pieces, part_k):
                    dve.wait_ge(g["part_done"], part_k)
                    dve.tensor_reduce(tot[:, i:i + 1], part[:, i, 0:pieces], AX.X, ALU.add).then_inc(g["tot_done"], 1)
                    dve.wait_ge(g["size_done"], i + 1)
                    dve.tensor_scalar(size[:, i:i + 1], bank[2 + i][:, 0:1], 1.0 / (FH * D), None, ALU.mult)\
                        .then_inc(g["s1"], 1)
                    dve.wait_ge(g["s1"], i + 1)
                    dve.tensor_scalar(thr[:, i, 0:1], size[:, i:i + 1], 0.5, None, ALU.mult)
                    dve.tensor_scalar(thr[:, i, 1:2], size[:, i:i + 1], -0.5, None, ALU.mult).then_inc(g["thr_done"], 1)
                    dve.wait_ge(g["thr_done"], i + 1)

                def quantise(i, w, dst, nb, k, last=True):
                    dve.tensor_scalar(nb, w, thr[:, i, 1:2], None, ALU.is_lt).then_inc(g["neg_done"], 1)
                    dve.wait_ge(g["neg_done"], k)
                    t = dve.scalar_tensor_tensor(out=dst, in0=w, scalar=thr[:, i, 0:1], in1=nb, op0=ALU.is_gt,
                                                 op1=ALU.subtract)
                    if last:
                        t.then_inc(g["q_done"], 1)

                for i, (done, dst) in enumerate((("w1_in", q1), ("w3_in", q3))):
                    dve.wait_ge(g[done], 16)
                    w = raws[i][:, 0:4 * FH]
                    dve.tensor_reduce(part[:, i, 0:4], w.rearrange("p (k n) -> p k n", k=4), AX.X, ALU.add,
                                      apply_absolute_value=True).then_inc(g["part_done"], 1)
                    sizes(i, 4, i + 1)
                    if i:
                        dve.wait_ge(g["q_done"], 1)
                    quantise(i, w, dst[:, :, :].rearrange("p k n -> p (k n)"), neg[:, 0:4 * FH], i + 1)
                dve.wait_ge(g["w2_in"], 32)
                m = (FC - 1) * D
                w, wt = raws[0][:, 0:m], rawt[:, :]
                dve.tensor_reduce(part[:, 2, 0:FC - 1], w.rearrange("p (k n) -> p k n", n=D), AX.X, ALU.add,
                                  apply_absolute_value=True).then_inc(g["part_done"], 1)
                dve.tensor_reduce(part[:, 2, FC - 1:FC], wt, AX.X, ALU.add, apply_absolute_value=True)\
                    .then_inc(g["part_done"], 1)
                sizes(2, FC, 4)
                dve.wait_ge(g["q_done"], 2)
                q2f = q2[:, :, :].rearrange("p k n -> p (k n)")
                quantise(2, w, q2f[:, 0:m], neg[:, 0:m], 3, False)
                quantise(2, wt, q2f[:, m:m + D], neg[:, m:m + D], 4)

                with dve.Fori(0, 2) as t:
                    for c in range(FC):
                        n = t * FC + c
                        r = P if c < FC - 1 else FTAIL
                        u = c % 2
                        dve.wait_ge(g["silu_done"], n + 1)
                        dve.wait_ge(g["p3_done"], n + 1)
                        dve.wait_ge(g["gl_done"], n + 1)
                        dve.scalar_tensor_tensor(out=gg[u][0:r, :], in0=bank[2 + u][0:r, :], scalar=size[0:r, 1:2],
                                                 in1=sg[u][0:r, :], op0=ALU.mult, op1=ALU.mult).then_inc(g["gg_done"], 1)
                        dve.wait_ge(g["gh_done"], n + 1)
                        dve.tensor_tensor(gl[0:r, c, :], gg[u][0:r, :], gh[0:r, c, :].bitcast(F32), ALU.subtract)\
                            .then_inc(g["gl_done"], 1)
                    for j in range(TT // 2):
                        n = t * (TT // 2) + j
                        u = j % 2
                        dve.wait_ge(g["y_done"], n + 1)
                        dve.wait_ge(g[f"o_out{u}"], 16 * (2 * t + j // 2) + 16)
                        dve.scalar_tensor_tensor(out=o[u][:, :], in0=bank[4 + u][:, :], scalar=size[:, 2:3],
                                                 in1=x[:, n, :], op0=ALU.mult, op1=ALU.add).then_inc(g["o_done"], 1)

            @block.scalar
            def _(act):
                act.preload_act_table(ACT.Silu)
                for u in two:
                    act.sem_inc(g[f"o_out{u}"], 16)
                with act.Fori(0, TT // 2) as turn:
                    for u in two:
                        n = 2 * turn + u
                        act.wait_ge(g["tr"], n + 1)
                        act.activation(hh[:, :, bass.ds(n * P, P)], bank[u][:, :].rearrange("p (c n) -> p c n", c=4),
                                       ACT.Copy).then_inc(g["hh_done"], 1)
                act.wait_ge(g["s1"], 3)
                with act.Fori(0, 2) as t:
                    for c in range(FC):
                        n = t * FC + c
                        r = P if c < FC - 1 else FTAIL
                        u = c % 2
                        act.wait_ge(g["p1_done"], n + 1)
                        act.activation(sg[u][0:r, :], bank[u][0:r, :], ACT.Silu, scale=size[0:r, 0:1])\
                            .then_inc(g["silu_done"], 1)
                        act.wait_ge(g["gg_done"], n + 3)
                        act.activation(gh[0:r, c, :], gg[u][0:r, :], ACT.Copy).then_inc(g["gh_done"], 1)

            @block.tensor
            def _(pe):
                with pe.Fori(0, TT // 2) as turn:
                    for u in two:
                        n = 2 * turn + u
                        pe.wait_ge(g["h_done"], n + 1)
                        for k in range(4):
                            t = pe.transpose(bank[u][:, k * P:(k + 1) * P], h[u][:, k * P:(k + 1) * P], ident[:, :])
                        t.then_inc(g["tr"], 1)
                pe.wait_ge(g["const"], 4)
                for i in range(3):
                    pe.wait_ge(g["tot_done"], i + 1)
                    pe.matmul(bank[2 + i][:, 0:1], ones[:, :], tot[:, i:i + 1], start=True, stop=True)\
                        .then_inc(g["size_done"], 1)
                pe.wait_ge(g["hl_done"], TT)
                pe.wait_ge(g["q_done"], 3)
                with pe.Fori(0, 2) as t:
                    for c in range(FC):
                        r = P if c < FC - 1 else FTAIL
                        u = c % 2
                        n = t * FC + c
                        pe.wait_ge(g["gg_done"], n + 1)
                        for q, out_, done in ((q1, bank[u], "p1_done"), (q3, bank[2 + u], "p3_done")):
                            for k in range(4):
                                for a, part_ in enumerate((hh, hl)):
                                    m = pe.matmul(out_[0:r, :], q[:, k, c * P:c * P + r],
                                                  part_[:, k, bass.ds(t * HALF_T, HALF_T)],
                                                  start=(k == 0 and a == 0), stop=(k == 3 and a == 1))
                            m.then_inc(g[done], 1)
                    pe.wait_ge(g["gl_done"], FC * t + FC + 2)
                    for j in range(TT // 2):
                        n = t * (TT // 2) + j
                        u = j % 2
                        pe.wait_ge(g["o_done"], n + 1)
                        for c in range(FC):
                            r = P if c < FC - 1 else FTAIL
                            for a, part_ in enumerate((gh, gl)):
                                m = pe.matmul(bank[4 + u][:, :], part_[0:r, c, j * P:(j + 1) * P], q2[0:r, c, :],
                                              start=(c == 0 and a == 0), stop=(c == FC - 1 and a == 1))
                        m.then_inc(g["y_done"], 1)
        nc.clear_and_free_semaphores(sems)
        nc.all_engine_barrier()


def layout(a):
    f = np.float32
    P = 128

    def rows(w):
        k, n = w.shape[0] // P, w.shape[1]
        return w.reshape(k, P, n).transpose(1, 0, 2).reshape(P, k * n)

    def equal(v, n=P):
        return np.broadcast_to(v[None, :], (n, v.shape[0]))

    def head_out(w):
        return w.reshape(2, 4, 2, 32, -1).transpose(1, 3, 2, 0, 4).reshape(P, -1)

    def head_cols(v):
        return v.reshape(2, 4, 2, 32).transpose(1, 3, 2, 0).reshape(P, 4)

    out = {"x": a["x"].reshape(8, P, 512)}
    ctx = a["ctx_1024"]
    out["ctx"] = ctx.transpose(0, 2, 1).reshape(16, 2, P, 1601).transpose(0, 2, 1, 3)
    for L in range(2):
        g = lambda n: a[f"L{L}_xattn_{n}"]
        w = np.concatenate([g("Wk"), g("Wv")], 1).reshape(256, 16, 2, 32)
        b = np.concatenate([g("bk"), g("bv")]).reshape(16, 2, 32)
        x = f"L{L}x_"
        out[x + "wk"] = rows(w[:, :, 0].reshape(256, 512))
        out[x + "wv"] = rows(w[:, :, 1].reshape(256, 512))
        out[x + "wq"] = rows(g("Wq"))
        out[x + "dw"] = rows(g("Wkv_dca"))
        out[x + "bq"] = equal(g("bq"))
        out[x + "bd"] = equal(g("bkv_dca")[:512])
        out[x + "bk"] = equal(b[:, 0].reshape(512), 2)
        out[x + "cols"] = np.stack([np.tile(g(n), 4) for n in ("qn_w", "qn_b", "kn_w", "kn_b", "kn_dca_w", "kn_dca_b")], 1)
        out[x + "cb"] = np.concatenate([head_cols(b[:, 1]), head_cols(g("bkv_dca")[512:])], 1)
        out[x + "yd"] = rows(ctx[:, -16:].reshape(256, 256).T)
        s = f"L{L}s_"
        out[s + "wo_x"] = head_out(g("Wo"))
        out[s + "bo_x"] = equal(g("bo"))
        if L == 0:
            h = lambda n: a["L0_attn_" + n]
            out[s + "wq"], out[s + "wk"], out[s + "wv"] = rows(h("Wq")), rows(h("Wk")), rows(h("Wv"))
            out[s + "wo"] = head_out(h("Wo"))
            out[s + "bq"], out[s + "bk"], out[s + "bo"] = equal(h("bq")), equal(h("bk")), equal(h("bo"))
            out[s + "cb"] = head_cols(h("bv"))
        else:
            h = lambda n: a["L1_attn_" + n]
            out[s + "wq"], out[s + "wk"], out[s + "wv"] = rows(h("wq")), rows(h("wk")), rows(h("wv"))
            out[s + "wo"] = head_out(h("wo"))
            inv = f(1.0) / f(10000.0) ** (np.arange(16, dtype=f) / f(16))
            angle = (np.arange(P) % 64).astype(f)[:, None] * inv[None, :]
            out[s + "cos"], out[s + "sin"] = np.cos(angle), np.sin(angle)
            sink = h("sink").reshape(8, 2)
            out[s + "sink"] = np.repeat(sink.T, 64, 0)
    w = lambda n: a["L0_ffn_" + n]
    out["m_nw"] = equal(w("norm_w"))
    out["m_gate"] = rows(w("gate_w").T)
    out["m_upper"] = np.triu(np.ones((P, P), f), 1)
    out["m_iota"] = np.broadcast_to(np.arange(32, dtype=f), (P, 32))
    out["m_tok"] = np.arange(8 * P, dtype=np.int32).reshape(8, P).T
    out["m_sgu"] = rows(np.concatenate([w("shared_gate_w"), w("shared_up_w")], 1))
    out["m_sd"] = rows(w("shared_down_w"))
    out["m_w13"] = w("w13").reshape(32, 4, P, 512).transpose(0, 2, 1, 3).reshape(32, P, 2048)
    out["m_w2"] = w("w2").reshape(32, 2, P, 512).transpose(0, 2, 1, 3).reshape(32, P, 1024)
    w = lambda n: a["L1_ffn_" + n]
    out["f_w1"], out["f_w3"] = rows(w("w1").T), rows(w("w3").T)
    main = 1365 // P * P
    out["f_w2"] = w("w2").T[:main].reshape(-1, P, 512).transpose(1, 0, 2)
    out["f_w2t"] = w("w2").T[main:]
    out["ident"] = np.eye(P, dtype=f)
    par = (np.arange(P) // 32) % 2
    out["pm"] = np.stack([par == 0, par == 1], 1).astype(f)
    return {k: np.ascontiguousarray(v) for k, v in out.items()}


class Env:
    pass


LAYERS = 2


def perceiver(nc, arrays, out):
    with ExitStack() as outer:
        dram = lambda name, shape, dt=F32: nc.dram_tensor(name, shape, dt).ap()
        qs_dram = dram("qs_dram", [B, P, PAIRS * 2 * P], F16)
        kd_dram = dram("kd_dram", [2, P, GROUPS, B, DCA], F16)
        vd_dram = dram("vd_dram", [B * DCA // P, P, PAIRS, 2, 64], F16)
        h_dram = dram("h_dram", [TT, P, D])
        slot_dram = dram("slot_dram", [SLOTS, 1], I32)
        eo_dram = dram("eo_dram", [SLOTS, D])
        x1_dram = dram("x1_dram", [TT, P, D])
        env = Env()
        sb = lambda name, shape, dt=F32: outer.enter_context(nc.sbuf_tensor(name, shape, dt))
        env.ident = sb("ident", [P, P])
        env.parity_mask = sb("parity_mask", [P, 2])
        env.ones2 = sb("ones2", [2, P], F32R)
        env.cb_x = sb("cb_x", [P, 4])
        ones32 = sb("ones32", [2, P])
        loaded = outer.enter_context(nc.semaphore("loaded"))
        made = outer.enter_context(nc.semaphore("made"))
        with nc.Block() as block:

            @block.sync
            def _(sp):
                sp.dma_start(env.ident[:, :], arrays["ident"]).then_inc(loaded, 16)
                sp.dma_start(env.parity_mask[:, :], arrays["pm"]).then_inc(loaded, 16)
                sp.wait_ge(loaded, 32)

            @block.vector
            def _(dve):
                dve.memset(ones32[:, :], 1.0).then_inc(made, 1)
                dve.wait_ge(made, 1)
                dve.tensor_copy(env.ones2[:, :], ones32[:, :])
        nc.all_engine_barrier()

        for layer in range(LAYERS):
            x_src = arrays["x"] if layer == 0 else x1_dram
            part = lambda kind: {name[len(kind):]: a for name, a in arrays.items() if name.startswith(kind)}
            with ExitStack() as ctx:
                sb = lambda name, shape, dt=F32: ctx.enter_context(nc.sbuf_tensor(f"l{layer}_{name}", shape, dt))
                env.ob = sb("ob", [P, B, PAIRS * HD])
                with ExitStack() as weights:
                    wsb = lambda name, shape, dt=F32R: weights.enter_context(
                        nc.sbuf_tensor(f"l{layer}_{name}", shape, dt))
                    wk, wv = wsb("wk", [P, 2, KC, D]), wsb("wv", [P, 2, KC, D])
                    bk2, kcol = wsb("bk2", [2, D]), wsb("kcol", [P, 2], F32)
                    env.prefix = f"p{layer}_"
                    prepare_context_attention(nc, env, part(f"L{layer}x_"), x_src, qs_dram, kd_dram, vd_dram, wk, wv,
                                              bk2, kcol[:, 0:1], kcol[:, 1:2])
                    env.prefix = f"a{layer}_"
                    context_attention(nc, env, arrays["ctx"], qs_dram, kd_dram, vd_dram, wk, wv, bk2, kcol[:, 0:1],
                                      kcol[:, 1:2])
                env.x = sb("x", [P, TT, D])
                env.prefix = f"s{layer}_"
                self_attention(nc, env, layer, part(f"L{layer}s_"), x_src)
                env.prefix = f"f{layer}_"
                if layer == 0:
                    moe_ffn(nc, env, part("m_"), h_dram, slot_dram, eo_dram, x1_dram)
                else:
                    ternary_ffn(nc, env, part("f_"), out)


def kernel(**inputs):
    import numpy as _np
    import concourse.bacc as _bacc
    from concourse import mybir as _mybir
    from concourse.bass_utils import run_bass_kernel_spmd as _run

    arrays = layout({name: _np.asarray(a) for name, a in inputs.items()})
    nc = _bacc.Bacc("TRN2", target_bir_lowering=False, num_devices=1)
    aps = {name: nc.dram_tensor(f"in_{name}", a.shape, _mybir.dt.from_np(a.dtype), kind="ExternalInput").ap()
           for name, a in arrays.items()}
    out = nc.dram_tensor("out", (TT, P, D), _mybir.dt.float32, kind="ExternalOutput").ap()
    perceiver(nc, aps, out)
    r = _run(nc, [{f"in_{name}": a for name, a in arrays.items()}], core_ids=[0])
    return r.results[0]["out"].reshape(B, S, D)
```

```python
from contextlib import ExitStack

import numpy as np
import concourse.bass as bass
from concourse import mybir

F32 = mybir.dt.float32
F32R = mybir.dt.float32r
F16 = mybir.dt.float16
BF16 = mybir.dt.bfloat16
I32 = mybir.dt.int32
U32 = mybir.dt.uint32
ALU = mybir.AluOpType
ACT = mybir.ActivationFunctionType
AX = mybir.AxisListType

P = 128
B, S, D = 16, 64, 512
H, HD = 16, 32
PAIRS = H // 2
GROUPS = D // P
TT = B * S // P
CTX, KD, DCA = 1601, 256, 16
MAIN = CTX - DCA
DC0 = MAIN + MAIN % 2
KEYS = DC0 + DCA
KC = KD // P
KT = -(-MAIN // P)
TAIL = MAIN - (KT - 1) * P
DROW = DC0 - (KT - 1) * P
KPAD = KT * P
CH = [(c * 512, min(512, KEYS - c * 512)) for c in range(-(-KEYS // 512))]
NCH = len(CH)
YA = 6
LN_EPS, HEAD_EPS = 1e-5, 1e-6
SCALE = float(HD) ** -0.5

ORDER = """
    s0.0 s0.1 y0 s0.2 s0.3 y1 exp0 k0 s1.0 norm0 v0 pt0.0 pt0.1 s1.1 k1 s1.2 s1.3 y2 v1 pt0.2 pt0.3 pv0.0
    pv0.1 y3 exp1 k2 pv0.2 pv0.3 o0 kt0 norm1 v2 pt1.0 pt1.1 s2.0 s2.1 kt1 pt1.2 k3 s2.2 pv1.0 pv1.1 pt1.3
    s2.3 v3 y4 y5 kt2 exp2 pv1.2 pv1.3 o1 s3.0 s3.1 k4 norm2 v4 pt2.0 pt2.1 kt3 k5 s3.2 s3.3 y6 pt2.2 v5 pt2.3
    pv2.0 y7 exp3 pv2.1 k6 pv2.2 pv2.3 o2 s4.0 kt4 s4.1 norm3 pt3.0 pt3.1 v6 s4.2 y8 s4.3 pt3.2 pt3.3 kt5
    pv3.0 exp4 pv3.1 k7 pv3.2 pv3.3 o3 v7 s5.0 kt6 norm4 s5.1 pt4.0 y9 pt4.1 k8 s5.2 v8 y10 pv4.0 s5.3 pt4.2
    pt4.3 kt7 exp5 k9 pv4.1 pv4.2 pv4.3 o4 s6.0 v9 pt5.0 y11 pt5.1 kt8 k10 norm5 v10 pt5.2 pv5.0 pt5.3 pv5.1
    s6.1 s6.2 y12 kt9 s6.3 exp6 pv5.2 pv5.3 o5 k11 s7.0 v11 s7.1 pt6.0 kt10 s7.2 s7.3 pt6.1 pt6.2 exp7 k12
    norm6 v12 pv6.0 pt6.3 pv6.1 norm7 pv6.2 pt7.0 kt11 pv6.3 o6 pt7.1 pt7.2 pv7.0 pt7.3 pv7.1 pv7.2 pv7.3 kt12
    o7
"""


PAIRS_ORDER = """
    s0.0 s0.1 s0.2 s0.3 s1.0 exp0 s1.1 s1.2 norm0 pt0.0 pt0.1 s1.3 pt0.2 pv0.0 pt0.3 pv0.1 pv0.2 pv0.3 o0 exp1
    s2.0 norm1 pt1.0 s2.1 s2.2 pt1.1 pt1.2 pv1.0 s2.3 pt1.3 pv1.1 pv1.2 pv1.3 o1 s3.0 exp2 s3.1 norm2 pt2.0
    pt2.1 s3.2 pt2.2 pt2.3 pv2.0 pv2.1 s3.3 exp3 pv2.2 pv2.3 o2 s4.0 s4.1 norm3 s4.2 pt3.0 pt3.1 s4.3 pt3.2
    pt3.3 exp4 pv3.0 pv3.1 pv3.2 pv3.3 o3 s5.0 norm4 pt4.0 pt4.1 s5.1 s5.2 pt4.2 pv4.0 pt4.3 s5.3 pv4.1 pv4.2
    pv4.3 o4 s6.0 s6.1 exp5 norm5 s6.2 pt5.0 pt5.1 s6.3 pt5.2 pv5.0 pt5.3 exp6 pv5.1 pv5.2 pv5.3 o5 s7.0 s7.1
    pt6.0 s7.2 s7.3 pt6.1 pt6.2 pv6.0 pv6.1 norm6 exp7 norm7 pt6.3 pt7.0 pv6.2 pv6.3 o6 pt7.1 pt7.2 pv7.0
    pt7.3 pv7.1 pv7.2 pv7.3 o7
"""


def steps_in(order):
    steps = []
    for name in order.split():
        kind = name.rstrip("0123456789.")
        number, _, chunk = name[len(kind):].partition(".")
        steps.append((kind, int(number), int(chunk or 0)))
    return steps


def tile_steps():
    steps = [("y", 0, 0), ("y", 1, 0)]
    for i in range(KT + 2):
        if i < KT:
            steps += [("k", i, 0), ("v", i, 0)]
        if i + 2 < KT:
            steps.append(("y", i + 2, 0))
        if i >= 2:
            steps.append(("kt", i - 2, 0))
    return steps




def context_attention(nc, env, ctx_dram, qs_dram, kd_dram, vd_dram, wk, wv, bk, kw_col, kb_col):
    with ExitStack() as ctx:
        sb = lambda name, shape, dt: ctx.enter_context(nc.sbuf_tensor(name, shape, dt))
        ps = lambda name, shape, dt: ctx.enter_context(nc.psum_tensor(name, shape, dt))
        pre = env.prefix
        sems = []

        def sem(name):
            s = ctx.enter_context(nc.semaphore(pre + name))
            sems.append(s)
            return s

        y = sb(pre + "y", [P, KC, MAIN], F32)
        yh = sb(pre + "yh", [P, 2, KC, P], F32R)
        yl = sb(pre + "yl", [P, 2, KC, P], F32R)
        kh = sb(pre + "kh", [P, 2, GROUPS, KEYS], F16)
        kl = sb(pre + "kl", [P, 2, GROUPS, KEYS], F16)
        v = sb(pre + "v", [P, 2, KT, PAIRS, 2, 64], F16)
        qs = sb(pre + "qs", [P, 2, PAIRS, 2, P], F16)
        p = sb(pre + "p", [P, 2, KPAD], F32)
        pth = sb(pre + "pth", [P, 2, KT, P], F16)
        ptl = sb(pre + "ptl", [P, 2, KT, P], F16)
        sq = sb(pre + "sq", [P, D], F32)
        kc = sb(pre + "kc", [P, 2, D], F32)
        khat = sb(pre + "khat", [P, 2, D], F32)
        kf = sb(pre + "kf", [P, 2, GROUPS, P], F32)
        var = sb(pre + "var", [P, 2, H], F32)
        rstd = sb(pre + "rstd", [P, 2, H], F32)
        half = sb(pre + "half", [P, H], F32)
        eps = sb(pre + "eps", [P, H], F32)
        nm4 = sb(pre + "nm4", [P, 2, NCH + 1], F32)
        nm = sb(pre + "nm", [P, 2, 2], F32)
        lsum = sb(pre + "lsum", [P, 2, 2], F32)
        rl = sb(pre + "rl", [P, 2, 2], F32)
        o_lo = sb(pre + "o_lo", [P, HD], F32)
        fd = sb(pre + "fd", [P, 2, 1], F32)

        ps_s = ps(pre + "ps_s", [P, 2, 512], F32)
        ps_t = ps(pre + "ps_t", [P, 2, 512], F32)
        ps_o = ps(pre + "ps_o", [P, 512], F32)
        ps_k = ps(pre + "ps_k", [P, 512], F32)
        ps_v = ps(pre + "ps_v", [P, 512], F32)
        ps_kt = ps(pre + "ps_kt", [P, GROUPS, P], F32)
        o_reg = ps_o[:, 0:P]

        y_a, y_b = sem("y_a"), sem("y_b")
        qs_in, dk_in, dv_in = sem("qs_in"), sem("dk_in"), sem("dv_in")
        const_ok = sem("const_ok")
        yh_done, yl_done = sem("yh_done"), sem("yl_done")
        k_done, v_done = sem("k_done"), sem("v_done")
        kc_done, sq_done, red_done, rstd_done, hat_done = sem("kc_done"), sem("sq_done"), sem("red_done"), sem("rstd_done"), sem("hat_done")
        kt_done, kf_done, kh_done, kl_done = sem("kt_done"), sem("kf_done"), sem("kh_done"), sem("kl_done")
        vh_done, vl_done = sem("vh_done"), sem("vl_done")
        s_done, s_copied = sem("s_done"), sem("s_copied")
        min_done, nm_done, exp_done = sem("min_done"), sem("nm_done"), sem("exp_done")
        rl_done, fd1_done, fd_done = sem("rl_done"), sem("fd1_done"), sem("fd_done")
        pt_done, pth_done, ptl_done = sem("pt_done"), sem("pth_done"), sem("ptl_done")
        pv_done, olo_done, o_done = sem("pv_done"), sem("olo_done"), sem("o_done")
        eps_done = sem("eps_done")

        ident = env.ident
        ob = env.ob

        def rows(i):
            return P if i < KT - 1 else TAIL


        def pe_proj(pe, nb, i, t, which):
            n = nb * KT + i
            r = rows(i)
            first = isinstance(n, int) and n == 0
            if which == "k":
                pe.wait_ge(yh_done, n + 1)
                pe.wait_ge(yl_done, n + 1)
                if not first:
                    pe.wait_ge(kc_done, n)
                w, out, done = wk, ps_k, k_done
            else:
                if not first:
                    pe.wait_ge(vl_done, n)
                w, out, done = wv, ps_v, v_done
            steps = [(yh, 0), (yl, 0), (yh, 1)]
            for c in range(KC):
                for a, (part, wpart) in enumerate(steps):
                    m = pe.matmul(out[0:r, :], part[:, t, c, 0:r], w[:, wpart, c, :],
                                  start=(c == 0 and a == 0),
                                  stop=(c == KC - 1 and a == 2))
            m.then_inc(done, 1)

        def pe_kt(pe, nb, i, t):
            n = nb * KT + i
            r = rows(i)
            pe.wait_ge(hat_done, n + 1)
            if not (isinstance(n, int) and n == 0):
                pe.wait_ge(kh_done, n)
            for g in range(GROUPS):
                m = pe.transpose(ps_kt[:, g, :], khat[:, t, g * P:(g + 1) * P], ident[:, :])
            m.then_inc(kt_done, 1)

        def pe_scores(pe, b, bp, pair, c):
            if pair == 0:
                pe.wait_ge(kl_done, b * KT + min(4 * c + 4, KT))
            if pair == 0 and c == 0:
                pe.wait_ge(qs_in, 16 * b + 16)
                pe.wait_ge(dk_in, 32 * b + 32)
            pe.wait_ge(s_copied, (b * PAIRS + pair) * NCH + c + 1)
            o, w = CH[c]
            g = pair // 2
            out = ps_s[:, c % 2, 0:w]
            for a, (qpart, kpart) in enumerate([(0, kh), (1, kh), (0, kl)]):
                m = pe.matmul(out, qs[:, bp, pair, qpart, :], kpart[:, bp, g, o:o + w],
                              start=(a == 0), stop=(a == 2))
            m.then_inc(s_done, 1)

        def tiles_of(g):
            return range(4 * g, min(4 * g + 4, KT))

        def pe_pt(pe, b, pair, g):
            m0 = b * PAIRS + pair
            if g == 0:
                pe.wait_ge(exp_done, m0 + 1)
            if g == NCH - 1:
                pe.wait_ge(fd_done, m0 + 1)
            pe.wait_ge(ptl_done, m0 * NCH + g + 1)
            for k in tiles_of(g):
                m = pe.transpose(ps_t[:, g % 2, (k % 4) * P:(k % 4 + 1) * P],
                                 p[:, pair % 2, k * P:(k + 1) * P], ident[:, :])
            m.then_inc(pt_done, 1)

        def pe_pv(pe, b, bp, pair, g):
            m0 = b * PAIRS + pair
            if g == 0:
                pe.wait_ge(o_done, m0 + 1)
                if pair == 0:
                    pe.wait_ge(dv_in, 16 * b + 16)
                    pe.wait_ge(vl_done, b * KT + KT)
            pe.wait_ge(ptl_done, m0 * NCH + g + 3)
            for k in tiles_of(g):
                pe.matmul(o_reg, pth[:, pair % 2, k, :], v[:, bp, k, pair, :, :].rearrange("p l d -> p (l d)"),
                          start=(k == 0), stop=False)
                m = pe.matmul(o_reg[:, 0:64], ptl[:, pair % 2, k, :], v[:, bp, k, pair, 0, :],
                              start=False, stop=(k == KT - 1))
            if g == NCH - 1:
                m.then_inc(pv_done, 1)

        def act_yh(act, nb, i, t):
            n = nb * KT + i
            r = rows(i)
            if i == 0:
                act.wait_ge(y_a, 16 * nb + 16)
            if i == YA:
                act.wait_ge(y_b, 16 * nb + 16)
            if not (isinstance(n, int) and n < 2):
                act.wait_ge(v_done, n - 1)
            act.activation(yh[:, t, :, 0:r], y[:, :, i * P:i * P + r], ACT.Copy).then_inc(yh_done, 1)

        def act_sq(act, nb, i, t):
            n = nb * KT + i
            r = rows(i)
            act.wait_ge(kc_done, n + 1)
            if not (isinstance(n, int) and n == 0):
                act.wait_ge(red_done, n)
            act.activation(sq[0:r, :], kc[0:r, t, :], ACT.Square, scale=SCALE).then_inc(sq_done, 1)

        def act_vh(act, nb, i, bp):
            n = nb * KT + i
            r = rows(i)
            act.wait_ge(v_done, n + 1)
            act.activation(v[0:r, bp, i, :, 0, :], ps_v[0:r, :].rearrange("p (a d) -> p a d", d=64),
                           ACT.Copy).then_inc(vh_done, 1)

        def act_kf(act, nb, i, t, bp):
            n = nb * KT + i
            r = rows(i)
            act.wait_ge(kt_done, n + 1)
            if not (isinstance(n, int) and n < 2):
                act.wait_ge(kl_done, n - 1)
            act.activation(kf[:, t, :, 0:r], ps_kt[:, :, 0:r], ACT.Identity, bias=kb_col,
                           scale=kw_col).then_inc(kf_done, 1)
            act.activation(kh[:, bp, :, i * P:i * P + r], ps_kt[:, :, 0:r], ACT.Identity, bias=kb_col,
                           scale=kw_col).then_inc(kh_done, 1)

        def act_pth(act, b, pair, g):
            act.wait_ge(pt_done, (b * PAIRS + pair) * NCH + g + 1)
            k = tiles_of(g)
            act.activation(pth[:, pair % 2, k[0]:k[-1] + 1, :], ps_t[:, g % 2, 0:len(k) * P].rearrange(
                "p (k n) -> p k n", n=P), ACT.Copy).then_inc(pth_done, 1)

        def act_exp(act, b, pair):
            act.wait_ge(nm_done, b * PAIRS + pair + 1)
            a = pair % 2
            act.activation(p[:, a, 0:MAIN], p[:, a, 0:MAIN], ACT.Exp, scale=-1.0, bias=nm[:, a, 0:1],
                           accum_out=lsum[:, a, 0:1])
            act.activation(p[:, a, DC0:KEYS], p[:, a, DC0:KEYS], ACT.Exp, scale=-1.0,
                           bias=nm[:, a, 1:2], accum_out=lsum[:, a, 1:2]).then_inc(exp_done, 1)

        def dve_yl(dve, nb, i, t):
            n = nb * KT + i
            r = rows(i)
            dve.wait_ge(yh_done, n + 1)
            dve.tensor_tensor(yl[:, t, :, 0:r], y[:, :, i * P:i * P + r], yh[:, t, :, 0:r].bitcast(F32), ALU.subtract)\
               .then_inc(yl_done, 1)

        def dve_red(dve, nb, i, t):
            r = rows(i)
            dve.wait_ge(sq_done, nb * KT + i + 1)
            dve.tensor_reduce(var[0:r, t, :], sq[0:r, :].rearrange("p (h d) -> p h d", d=HD), AX.X, ALU.add)\
               .then_inc(red_done, 1)

        def dve_kc(dve, nb, i, t):
            n = nb * KT + i
            r = rows(i)
            dve.wait_ge(k_done, n + 1)
            if not (isinstance(n, int) and n < 2):
                dve.wait_ge(hat_done, n - 1)
            dve.tensor_tensor(kc[0:r, t, :], ps_k[0:r, :], bk[0:r, :], ALU.add).then_inc(kc_done, 1)

        def dve_vl(dve, nb, i, bp):
            n = nb * KT + i
            r = rows(i)
            dve.wait_ge(vh_done, n + 1)
            dve.tensor_tensor(v[0:r, bp, i, :, 1, :], ps_v[0:r, :].rearrange("p (a d) -> p a d", d=64),
                              v[0:r, bp, i, :, 0, :], ALU.subtract).then_inc(vl_done, 1)

        def dve_scores(dve, b, pair, c):
            m0 = b * PAIRS + pair
            a = pair % 2
            o, w = CH[c]
            dve.wait_ge(s_done, m0 * NCH + c + 1)
            if c < NCH - 1:
                dve.tensor_scalar(p[:, a, o:o + w], ps_s[:, c % 2, 0:w], -1.0, None, ALU.mult, ALU.min,
                                  accum_out=nm4[:, a, c:c + 1]).then_inc(s_copied, 1)
                return
            wm = MAIN - o
            dve.tensor_scalar(p[:, a, o:MAIN], ps_s[:, c % 2, 0:wm], -1.0, None, ALU.mult, ALU.min,
                              accum_out=nm4[:, a, c:c + 1])
            dve.tensor_scalar(p[:, a, DC0:KEYS], ps_s[:, c % 2, DC0 - o:w], -1.0, None, ALU.mult, ALU.min,
                              accum_out=nm[:, a, 1:2]).then_inc(s_copied, 1)
            dve.wait_ge(s_copied, m0 * NCH + c + 3)
            dve.tensor_reduce(nm[:, a, 0:1], nm4[:, a, 0:NCH], AX.X, ALU.min).then_inc(nm_done, 1)

        def dve_norm(dve, b, pair):
            m0 = b * PAIRS + pair
            a = pair % 2
            dve.wait_ge(exp_done, m0 + 1)
            dve.reciprocal(rl[:, a, :], lsum[:, a, :]).then_inc(rl_done, 1)
            dve.wait_ge(rl_done, m0 + 1)
            dve.tensor_tensor(fd[:, a, :], lsum[:, a, 0:1], rl[:, a, 1:2], ALU.mult).then_inc(fd1_done, 1)
            dve.wait_ge(fd1_done, m0 + 1)
            dve.tensor_scalar(p[:, a, DC0:KEYS], p[:, a, DC0:KEYS], fd[:, a, :], None, ALU.mult)\
               .then_inc(fd_done, 1)

        def dve_ptl(dve, b, pair, g):
            dve.wait_ge(pth_done, (b * PAIRS + pair) * NCH + g + 1)
            k = tiles_of(g)
            dve.tensor_tensor(ptl[:, pair % 2, k[0]:k[-1] + 1, :],
                              ps_t[:, g % 2, 0:len(k) * P].rearrange("p (k n) -> p k n", n=P),
                              pth[:, pair % 2, k[0]:k[-1] + 1, :], ALU.subtract).then_inc(ptl_done, 1)

        def dve_o(dve, b, pair):
            m0 = b * PAIRS + pair
            a = pair % 2
            dve.wait_ge(pv_done, m0 + 1)
            for par in range(2):
                q = slice(64 * par, 64 * par + 64)
                lo = slice(64 + HD * par, 64 + HD * par + HD)
                t = dve.tensor_scalar(o_lo[q, :], o_reg[q, lo], rl[q, a, 0:1], None, ALU.mult)
            t.then_inc(olo_done, 1)
            dve.wait_ge(olo_done, m0 + 1)
            for par in range(2):
                q = slice(64 * par, 64 * par + 64)
                t = dve.scalar_tensor_tensor(out=ob[q, b, pair * HD:(pair + 1) * HD],
                                             in0=o_reg[q, HD * par:HD * par + HD], scalar=rl[q, a, 0:1],
                                             in1=o_lo[q, :], op0=ALU.mult, op1=ALU.add)
            t.then_inc(o_done, 1)

        def pool_rstd(pool, nb, i, t):
            n = nb * KT + i
            r = rows(i)
            pool.wait_ge(red_done, n + 1)
            pool.tensor_tensor(var[0:r, t, :], var[0:r, t, :], eps[0:r, :], ALU.add).then_inc(eps_done, 1)
            pool.wait_ge(eps_done, n + 1)
            if not (isinstance(n, int) and n < 2):
                pool.wait_ge(hat_done, n - 1)
            pool.tensor_tensor(rstd[0:r, t, :], var[0:r, t, :], half[0:r, :], ALU.pow).then_inc(rstd_done, 1)

        def hat(eng, nb, i, t):
            n = nb * KT + i
            r = rows(i)
            eng.wait_ge(rstd_done, n + 1)
            if not (isinstance(n, int) and n < 2):
                eng.wait_ge(kt_done, n - 1)
            eng.tensor_tensor(khat[0:r, t, :].rearrange("p (h d) -> p h d", d=HD),
                              kc[0:r, t, :].rearrange("p (h d) -> p h d", d=HD),
                              rstd[0:r, t, :].unsqueeze(2).broadcast_to([r, H, HD]), ALU.mult)\
                .then_inc(hat_done, 1)

        def k_low(eng, nb, i, t, bp):
            n = nb * KT + i
            r = rows(i)
            eng.wait_ge(kh_done, n + 1)
            eng.tensor_tensor(kl[:, bp, :, i * P:i * P + r], kf[:, t, :, 0:r], kh[:, bp, :, i * P:i * P + r],
                              ALU.subtract).then_inc(kl_done, 1)


        def steps_of(b, nb):
            if b is None:
                return tile_steps()
            return steps_in(PAIRS_ORDER if nb is None else ORDER)

        def tile_par(nbp, i):
            return (nbp * KT + i) % 2

        def pe_batch(pe, b, bp, nb, nbp):
            for kind, i, c in steps_of(b, nb):
                if kind in ("k", "v"):
                    pe_proj(pe, nb, i, tile_par(nbp, i), kind)
                elif kind == "kt":
                    pe_kt(pe, nb, i, tile_par(nbp, i))
                elif kind == "s":
                    pe_scores(pe, b, bp, i, c)
                elif kind == "pt":
                    pe_pt(pe, b, i, c)
                elif kind == "pv":
                    pe_pv(pe, b, bp, i, c)

        def act_batch(act, b, bp, nb, nbp):
            for kind, i, c in steps_of(b, nb):
                if kind == "y":
                    act_yh(act, nb, i, tile_par(nbp, i))
                elif kind == "k":
                    act_sq(act, nb, i, tile_par(nbp, i))
                elif kind == "v":
                    act_vh(act, nb, i, nbp)
                elif kind == "kt":
                    act_kf(act, nb, i, tile_par(nbp, i), nbp)
                elif kind == "exp":
                    act_exp(act, b, i)
                elif kind == "pt":
                    act_pth(act, b, i, c)

        def dve_batch(dve, b, bp, nb, nbp):
            for kind, i, c in steps_of(b, nb):
                if kind == "y":
                    dve_yl(dve, nb, i, tile_par(nbp, i))
                elif kind == "k":
                    dve_kc(dve, nb, i, tile_par(nbp, i))
                elif kind == "v":
                    dve_red(dve, nb, i, tile_par(nbp, i))
                    if b is None and i:
                        hat(dve, nb, i - 1, tile_par(nbp, i - 1))
                    dve_vl(dve, nb, i, nbp)
                elif kind == "s":
                    dve_scores(dve, b, i, c)
                elif kind == "norm":
                    dve_norm(dve, b, i)
                elif kind == "pt":
                    dve_ptl(dve, b, i, c)
                elif kind == "o":
                    dve_o(dve, b, i)
                elif b is None and kind == "kt":
                    if i:
                        k_low(dve, nb, i - 1, tile_par(nbp, i - 1), nbp)
                    if i == KT - 1:
                        hat(dve, nb, i, tile_par(nbp, i))
            if b is None:
                k_low(dve, nb, KT - 1, tile_par(nbp, KT - 1), nbp)

        def pool_batch(pool, b, bp, nb, nbp):
            for kind, i, c in steps_of(b, nb):
                if kind == "v":
                    pool_rstd(pool, nb, i, tile_par(nbp, i))
                    if b is not None:
                        hat(pool, nb, i, tile_par(nbp, i))
                elif b is not None and kind == "kt":
                    k_low(pool, nb, i, tile_par(nbp, i), nbp)

        def batches(eng, step):
            step(eng, None, None, 0, 0)
            with eng.Fori(0, B // 2 - 1) as turn:
                step(eng, 2 * turn, 0, 2 * turn + 1, 1)
                step(eng, 2 * turn + 1, 1, 2 * turn + 2, 0)
            step(eng, B - 2, 0, B - 1, 1)
            step(eng, B - 1, 1, None, None)

        vd_rows = vd_dram.rearrange("t (b k) a l d -> (t b) k a l d", k=DCA)
        with nc.Block() as block:

            @block.sync
            def _(sp):
                def load_a(b):
                    sp.dma_start(y[:, :, 0:YA * P], ctx_dram[b, :, :, 0:YA * P]).then_inc(y_a, 16)

                def load_b(b):
                    sp.dma_start(y[:, :, YA * P:MAIN], ctx_dram[b, :, :, YA * P:MAIN]).then_inc(y_b, 16)

                def load_attn(b, bp, wait):
                    if wait:
                        sp.wait_ge(s_done, (b - 1) * PAIRS * NCH + 1)
                    sp.dma_start(qs[:, bp].rearrange("p a l q -> p (a l q)"), qs_dram[b]).then_inc(qs_in, 16)
                    for part, buf in enumerate((kh, kl)):
                        sp.dma_start(buf[:, bp, :, DC0:KEYS], kd_dram[part, :, :, b, :]).then_inc(dk_in, 16)
                    if wait:
                        sp.wait_ge(pv_done, (b - 1) * PAIRS + 1)
                    sp.dma_start(v[DROW:DROW + DCA, bp, KT - 1], vd_rows[b]).then_inc(dv_in, 16)

                load_a(0)
                load_b(0)
                sp.wait_ge(const_ok, 5)
                load_attn(0, 0, False)
                sp.wait_ge(yl_done, YA)
                load_a(1)
                sp.wait_ge(yl_done, KT)
                load_b(1)
                sp.wait_ge(pv_done, 1)
                load_attn(1, 1, False)
                with sp.Fori(0, B // 2 - 1) as turn:
                    for u in range(2):
                        b = 2 * turn + u
                        sp.wait_ge(yl_done, (b + 1) * KT + YA)
                        load_a(b + 2)
                        sp.wait_ge(yl_done, (b + 1) * KT + KT)
                        load_b(b + 2)
                        load_attn(b + 2, u, True)

            @block.gpsimd
            def _(pool):
                pool.memset(half[:, :], -0.5).then_inc(const_ok, 1)
                pool.memset(eps[:, :], HEAD_EPS).then_inc(const_ok, 1)
                pool.memset(v[:, :, KT - 1], 0.0).then_inc(const_ok, 1)
                if DC0 > MAIN:
                    for buf in (kh, kl):
                        pool.memset(buf[:, :, :, MAIN:DC0], 0.0).then_inc(const_ok, 1)
                pool.wait_ge(const_ok, 5)
                batches(pool, pool_batch)

            @block.scalar
            def _(act):
                act.preload_act_table(ACT.Exp)
                batches(act, act_batch)

            @block.vector
            def _(dve):
                dve.sem_inc(s_copied, 2)
                dve.sem_inc(ptl_done, 2)
                dve.sem_inc(o_done, 1)
                dve.memset(p[:, :, MAIN:KPAD], 0.0).then_inc(min_done, 1)
                batches(dve, dve_batch)

            @block.tensor
            def _(pe):
                pe.wait_ge(min_done, 1)
                pe.wait_ge(const_ok, 5)
                batches(pe, pe_batch)
        nc.clear_and_free_semaphores(sems)
        nc.all_engine_barrier()


def prepare_context_attention(nc, env, raw, x_src, qs_dram, kd_dram, vd_dram, wk, wv, bk32, kw_col, kb_col):
    with ExitStack() as ctx:
        pre = env.prefix
        sb = lambda name, shape, dt=F32: ctx.enter_context(nc.sbuf_tensor(pre + name, shape, dt))
        sems = []

        def sem(name):
            s = ctx.enter_context(nc.semaphore(pre + name))
            sems.append(s)
            return s

        ways = range(TT)
        bank = [ctx.enter_context(nc.psum_tensor(f"{pre}bank{u}", [P, 512], F32)) for u in ways]
        wk32 = sb("wk32", [P, KC * H, HD])
        wv32 = sb("wv32", [P, KC * D])
        wq32 = sb("wq32", [P, 4 * H, HD])
        dw32 = sb("dw32", [P, KC, 2 * H, HD])
        bq32 = sb("bq32", [P, H, HD])
        bd32 = sb("bd32", [P, H, HD])
        sums = sb("sums", [P, 9 * H])
        bsum = sb("bsum", [P, H])
        cols = sb("cols", [P, 6])
        qcol = sb("qcol", [P, 2])
        cbs = sb("cbs", [P, 2, 4])
        yd = sb("yd", [P, KC, B * DCA])
        half = sb("half", [P, H])
        eps = sb("eps", [P, H + 1])
        xs = [sb(f"xs{u}", [P, D]) for u in ways]
        xn = [sb(f"xn{u}", [P, D]) for u in ways]
        xt = [sb(f"xt{u}", [P, 4, P]) for u in ways]
        stats = [sb(f"stats{u}", [P, 6]) for u in ways]
        mv = [sb(f"mv{u}", [P, 2]) for u in ways]
        rs = [sb(f"rs{u}", [P, 1]) for u in ways]
        qc = [sb(f"qc{u}", [P, D]) for u in ways]
        sq = xs
        var = [sb(f"var{u}", [P, H]) for u in ways]
        rh = [sb(f"rh{u}", [P, H]) for u in ways]
        hat = xn
        qf = xt
        qsb = [sb(f"qsb{u}", [P, 2, 4, 2, 2, 2, 64], F16) for u in ways]
        kdb = sb("kdb", [P, 2, 2, 4, P], F16)
        vdb = sb("vdb", [P, 2, PAIRS, 2, 64], F16)

        names = ("zeroed wk_in wv_in wq_in dw_in bias_in col_in cb_in yd_in const sum1 sum2 cen hi_done w_ok "
                 "stat aggr eps rstd xn_done tr1 xt_done proj vproj vd_h vd_ok qc_done sq_done red eps2 rstd2 hat_done tr2 "
                 "qf_done qh_done ql_done kd_out").split()
        names += [f"{name}{u}" for name in ("x_in", "q_out") for u in ways]
        g = {name: sem(name) for name in names}
        ident = env.ident

        with nc.Block() as block:

            @block.sync
            def _(sp):
                def load_x(n, u):
                    sp.dma_start(xs[u][:, :], x_src[n]).then_inc(g[f"x_in{u}"], 16)

                for u in ways:
                    load_x(u, u)
                sp.dma_start(wq32[:, :, :].rearrange("p a d -> p (a d)"), raw["wq"]).then_inc(g["wq_in"], 16)
                sp.dma_start(bq32[:, :, :].rearrange("p a d -> p (a d)"), raw["bq"]).then_inc(g["bias_in"], 16)
                sp.dma_start(bd32[:, :, :].rearrange("p a d -> p (a d)"), raw["bd"]).then_inc(g["bias_in"], 16)
                sp.dma_start(bk32, raw["bk"]).then_inc(g["bias_in"], 16)
                sp.dma_start(cols[:, :], raw["cols"]).then_inc(g["col_in"], 16)
                sp.dma_start(cbs[:, :, :].rearrange("p a d -> p (a d)"), raw["cb"]).then_inc(g["cb_in"], 16)
                sp.dma_start(dw32[:, :, :, :].rearrange("p k a d -> p (k a d)"), raw["dw"]).then_inc(g["dw_in"], 16)
                sp.dma_start(yd[:, :, :].rearrange("p k n -> p (k n)"), raw["yd"]).then_inc(g["yd_in"], 16)
                sp.dma_start(wk32[:, :, :].rearrange("p a d -> p (a d)"), raw["wk"]).then_inc(g["wk_in"], 16)
                sp.dma_start(wv32[:, :], raw["wv"]).then_inc(g["wv_in"], 16)

                def store_q(n, u):
                    sp.wait_ge(g["ql_done"], n + 1)
                    for b in range(2):
                        sp.dma_start(qs_dram[2 * n + b], qsb[u][:, b].rearrange("p g r l a q -> p (g r l a q)"))\
                            .then_inc(g[f"q_out{u}"], 16)

                for n in range(TT):
                    store_q(n, n)
                for t in range(2):
                    sp.wait_ge(g["ql_done"], TT + t + 1)
                    for part in range(2):
                        sp.dma_start(kd_dram[part, :, :, 8 * t:8 * t + 8, :],
                                     kdb[:, t, part].rearrange("p g (b k) -> p g b k", k=DCA)).then_inc(g["kd_out"], 16)
                    sp.wait_ge(g["vd_ok"], t + 1)
                    sp.dma_start(vd_dram[t], vdb[:, t]).then_inc(g["kd_out"], 16)
                for u in ways:
                    sp.wait_ge(g[f"q_out{u}"], 32 + 16 * B // TT)
                sp.wait_ge(g["kd_out"], 16 * 6)

            @block.gpsimd
            def _(pool):
                pool.memset(half[:, :], -0.5).then_inc(g["const"], 1)
                pool.memset(eps[:, 0:H], HEAD_EPS).then_inc(g["const"], 1)
                pool.memset(eps[:, H:H + 1], LN_EPS).then_inc(g["const"], 1)
                pool.wait_ge(g["const"], 3)

                def normalise(n, u):
                    pool.wait_ge(g["red"], n + 1)
                    pool.tensor_tensor(var[u][:, :], var[u][:, :], eps[:, 0:H], ALU.add).then_inc(g["eps2"], 1)
                    pool.wait_ge(g["eps2"], n + 1)
                    pool.tensor_tensor(rh[u][:, :], var[u][:, :], half[:, :], ALU.pow).then_inc(g["rstd2"], 1)
                    pool.wait_ge(g["rstd2"], n + 1)
                    pool.tensor_tensor(hat[u][:, :].rearrange("p (h d) -> p h d", d=HD),
                                       qc[u][:, :].rearrange("p (h d) -> p h d", d=HD),
                                       rh[u][:, :].unsqueeze(2).broadcast_to([P, H, HD]), ALU.mult)\
                        .then_inc(g["hat_done"], 1)

                for turn in range(TT // len(ways)):
                    for u in ways:
                        n = TT * turn + u
                        pool.wait_ge(g["aggr"], n + 1)
                        pool.tensor_tensor(mv[u][:, 1:2], mv[u][:, 1:2], eps[:, H:H + 1], ALU.add).then_inc(g["eps"], 1)
                        pool.wait_ge(g["eps"], n + 1)
                        pool.tensor_tensor(rs[u][:, :], mv[u][:, 1:2], half[:, 0:1], ALU.pow).then_inc(g["rstd"], 1)
                    for u in ways:
                        normalise(TT * turn + u, u)
                for t in range(2):
                    normalise(TT + t, t)

            @block.vector
            def _(dve):
                def centre(w, heads, o, k):
                    s = sums[:, o:o + heads]
                    dve.tensor_reduce(s, w, AX.X, ALU.add).then_inc(g["sum1"], 1)
                    dve.wait_ge(g["sum1"], k + 1)
                    dve.tensor_scalar(s, s, -1.0 / HD, None, ALU.mult).then_inc(g["sum2"], 1)
                    dve.wait_ge(g["sum2"], k + 1)
                    dve.tensor_tensor(w, w, s.unsqueeze(2).broadcast_to([P, heads, HD]), ALU.add).then_inc(g["cen"], 1)

                def q_part(n, u, dca):
                    dve.wait_ge(g["proj"], n + 1)
                    dve.tensor_tensor(qc[u][:, :].rearrange("p (h d) -> p h d", d=HD),
                                      bank[u][:, :].rearrange("p (h d) -> p h d", d=HD),
                                      (bd32 if dca else bq32)[:, :, :], ALU.add).then_inc(g["qc_done"], 1)

                def red_part(n, u):
                    dve.wait_ge(g["sq_done"], n + 1)
                    dve.tensor_reduce(var[u][:, :], sq[u][:, :].rearrange("p (h d) -> p h d", d=HD), AX.X, ALU.add)\
                        .then_inc(g["red"], 1)

                for turn in range(TT // len(ways)):
                    for u in ways:
                        n = TT * turn + u
                        dve.wait_ge(g[f"x_in{u}"], 16 * turn + 16)
                        dve.bn_stats(stats[u][:, :], xs[u][:, :]).then_inc(g["stat"], 1)
                    for u in ways:
                        n = TT * turn + u
                        dve.wait_ge(g["stat"], n + 1)
                        dve.bn_aggr(mv[u][:, :], stats[u][:, :]).then_inc(g["aggr"], 1)
                    dve.wait_ge(g["wq_in"], 16)
                    centre(wq32[:, :, :], 4 * H, 0, 0)
                    dve.wait_ge(g["bias_in"], 48)
                    centre(bq32[:, :, :], H, 4 * H, 1)
                    dve.wait_ge(g["col_in"], 16)
                    dve.tensor_scalar(qcol[:, :], cols[:, 0:2], SCALE, None, ALU.mult).then_inc(g["w_ok"], 1)
                    for u in ways:
                        n = TT * turn + u
                        dve.wait_ge(g["rstd"], n + 1)
                        dve.tensor_scalar(xn[u][:, :], xs[u][:, :], mv[u][:, 0:1], rs[u][:, 0:1], ALU.subtract,
                                          ALU.mult).then_inc(g["xn_done"], 1)
                    dve.wait_ge(g["cen"], 2)
                    for u in ways:
                        q_part(TT * turn + u, u, False)
                        dve.memset(qsb[u][:, :, :, :, :, :, :].rearrange("p b g r l a q -> p (b g r l a q)")
                                   .bitcast(F32), 0.0).then_inc(g["zeroed"], 1)
                    for u in ways:
                        red_part(TT * turn + u, u)
                    for u in ways:
                        n = TT * turn + u
                        dve.wait_ge(g["qf_done"], n + 1)
                        dve.wait_ge(g["qh_done"], n + 1)
                        for r4 in range(4):
                            rows = slice(32 * r4, 32 * r4 + 32)
                            q4 = qf[u][rows, :, :].rearrange("p g (b q) -> p b g q", b=2)
                            dst = qsb[u][rows, :, :, r4 // 2, :, r4 % 2, :]
                            for b in range(2):
                                t = dve.tensor_tensor(dst[:, b, :, 1, :], q4[:, b], dst[:, b, :, 0, :], ALU.subtract)
                        t.then_inc(g["ql_done"], 1)
                dve.wait_ge(g["dw_in"], 16)
                for k in range(KC):
                    centre(dw32[:, k, 0:H, :], H, (5 + k) * H, 2 + k)
                centre(bd32[:, :, :], H, 7 * H, 4)
                for t in range(2):
                    q_part(TT + t, t, True)
                for t in range(2):
                    red_part(TT + t, t)
                for t in range(2):
                    dve.wait_ge(g["vd_h"], t + 1)
                    dve.tensor_tensor(vdb[:, t, :, 1, :], bank[2 + t][:, :].rearrange("p (a d) -> p a d", d=64),
                                      vdb[:, t, :, 0, :], ALU.subtract).then_inc(g["vd_ok"], 1)
                for t in range(2):
                    dve.wait_ge(g["qf_done"], TT + t + 1)
                    dve.wait_ge(g["qh_done"], TT + t + 1)
                    dve.tensor_tensor(kdb[:, t, 1], qf[t][:, :, :], kdb[:, t, 0], ALU.subtract).then_inc(g["ql_done"], 1)
                dve.wait_ge(g["wk_in"], 16)
                dve.tensor_reduce(sums[:, 0:KC * H], wk32[:, :, :], AX.X, ALU.add).then_inc(g["sum1"], 1)
                bk3 = bk32.rearrange("p (h d) -> p h d", d=HD)
                dve.tensor_reduce(bsum[:, :], bk3, AX.X, ALU.add).then_inc(g["sum1"], 1)
                dve.wait_ge(g["sum1"], 7)
                dve.tensor_scalar(sums[:, 0:KC * H], sums[:, 0:KC * H], -1.0 / HD, None, ALU.mult).then_inc(g["sum2"], 1)
                dve.tensor_scalar(bsum[:, :], bsum[:, :], -1.0 / HD, None, ALU.mult).then_inc(g["sum2"], 1)
                dve.wait_ge(g["sum2"], 7)
                dve.tensor_tensor(wk32[:, :, :], wk32[:, :, :], sums[:, 0:KC * H].unsqueeze(2)
                                  .broadcast_to([P, KC * H, HD]), ALU.add).then_inc(g["cen"], 1)
                dve.tensor_tensor(bk3, bk3, bsum[:, :].unsqueeze(2).broadcast_to([P, H, HD]), ALU.add)\
                    .then_inc(g["cen"], 1)
                dve.wait_ge(g["cen"], 7)
                dve.wait_ge(g["wv_in"], 16)
                wkf = wk32[:, :, :].rearrange("p (k a) d -> p k (a d)", k=KC)
                wvf = wv32[:, :].rearrange("p (k n) -> p k n", k=KC)
                dve.tensor_copy(wk[:, 0], wkf).then_inc(g["hi_done"], 1)
                dve.tensor_copy(wv[:, 0], wvf).then_inc(g["hi_done"], 1)
                dve.wait_ge(g["hi_done"], 2)
                dve.tensor_tensor(wk[:, 1], wkf, wk[:, 0].bitcast(F32), ALU.subtract)
                dve.tensor_tensor(wv[:, 1], wvf, wv[:, 0].bitcast(F32), ALU.subtract)
                dve.wait_ge(g["cb_in"], 16)
                dve.tensor_tensor(env.cb_x[:, :], cbs[:, 0, :], cbs[:, 1, :], ALU.add)
                dve.tensor_copy(kw_col, cols[:, 2:3])
                dve.tensor_copy(kb_col, cols[:, 3:4])

            @block.scalar
            def _(act):
                act.preload_act_table(ACT.Exp)
                for u in ways:
                    act.sem_inc(g[f"q_out{u}"], 32)

                def square(n, u):
                    act.wait_ge(g["qc_done"], n + 1)
                    act.activation(sq[u][:, :], qc[u][:, :], ACT.Square, scale=SCALE).then_inc(g["sq_done"], 1)

                for turn in range(TT // len(ways)):
                    for u in ways:
                        n = TT * turn + u
                        act.wait_ge(g["tr1"], n + 1)
                        act.activation(xt[u][:, :, :], bank[u][:, :].rearrange("p (c n) -> p c n", c=4),
                                       ACT.Copy).then_inc(g["xt_done"], 1)
                    for u in ways:
                        square(TT * turn + u, u)
                    for u in ways:
                        n = TT * turn + u
                        act.wait_ge(g["tr2"], n + 1)
                        act.wait_ge(g["w_ok"], 1)
                        src = bank[u][:, :].rearrange("p (c n) -> p c n", c=4)
                        act.activation(qf[u][:, :, :], src, ACT.Identity, bias=qcol[:, 1:2], scale=qcol[:, 0:1])\
                            .then_inc(g["qf_done"], 1)
                        act.wait_ge(g["zeroed"], u + 1)
                        act.wait_ge(g[f"q_out{u}"], 32 * turn + 32)
                        for r4 in range(4):
                            rows = slice(32 * r4, 32 * r4 + 32)
                            s4 = src[rows].rearrange("p g (b q) -> p b g q", b=2)
                            for b in range(2):
                                t = act.activation(qsb[u][rows, b, :, r4 // 2, 0, r4 % 2, :], s4[:, b], ACT.Identity,
                                                   bias=qcol[rows, 1:2], scale=qcol[rows, 0:1])
                        t.then_inc(g["qh_done"], 1)
                for t in range(2):
                    act.wait_ge(g["vproj"], t + 1)
                    act.activation(vdb[:, t, :, 0, :], bank[2 + t][:, :].rearrange("p (a d) -> p a d", d=64), ACT.Copy)\
                        .then_inc(g["vd_h"], 1)
                for t in range(2):
                    square(TT + t, t)
                for t in range(2):
                    act.wait_ge(g["tr2"], TT + t + 1)
                    src = bank[t][:, :].rearrange("p (c n) -> p c n", c=4)
                    act.activation(qf[t][:, :, :], src, ACT.Identity, bias=cols[:, 5:6], scale=cols[:, 4:5])\
                        .then_inc(g["qf_done"], 1)
                    act.activation(kdb[:, t, 0], src, ACT.Identity, bias=cols[:, 5:6], scale=cols[:, 4:5])\
                        .then_inc(g["qh_done"], 1)

            @block.tensor
            def _(pe):
                def transpose4(src, out, done):
                    for k in range(4):
                        t = pe.transpose(out[:, k * P:(k + 1) * P], src[:, k * P:(k + 1) * P], ident[:, :])
                    t.then_inc(done, 1)

                for turn in range(TT // len(ways)):
                    for u in ways:
                        pe.wait_ge(g["xn_done"], TT * turn + u + 1)
                        transpose4(xn[u], bank[u], g["tr1"])
                    pe.wait_ge(g["cen"], 2)
                    for u in ways:
                        pe.wait_ge(g["xt_done"], TT * turn + u + 1)
                        for k in range(4):
                            t = pe.matmul(bank[u][:, :], xt[u][:, k, :],
                                          wq32[:, k * H:(k + 1) * H, :].rearrange("p h d -> p (h d)"),
                                          start=(k == 0), stop=(k == 3))
                        t.then_inc(g["proj"], 1)
                    for u in ways:
                        pe.wait_ge(g["hat_done"], TT * turn + u + 1)
                        transpose4(hat[u], bank[u], g["tr2"])
                pe.wait_ge(g["yd_in"], 16)
                pe.wait_ge(g["cen"], 5)
                for t in range(2):
                    for k in range(KC):
                        m = pe.matmul(bank[2 + t][:, :], yd[:, k, t * P:(t + 1) * P],
                                      dw32[:, k, H:2 * H, :].rearrange("p h d -> p (h d)"),
                                      start=(k == 0), stop=(k == KC - 1))
                    m.then_inc(g["vproj"], 1)
                for t in range(2):
                    for k in range(KC):
                        m = pe.matmul(bank[t][:, :], yd[:, k, t * P:(t + 1) * P],
                                      dw32[:, k, 0:H, :].rearrange("p h d -> p (h d)"),
                                      start=(k == 0), stop=(k == KC - 1))
                    m.then_inc(g["proj"], 1)
                for t in range(2):
                    pe.wait_ge(g["hat_done"], TT + t + 1)
                    pe.wait_ge(g["vd_ok"], t + 1)
                    transpose4(hat[t], bank[t], g["tr2"])
        nc.clear_and_free_semaphores(sems)
        nc.all_engine_barrier()


def self_attention(nc, env, layer, raw, x_src):
    rope = layer == 1
    kvw = 128 if rope else D
    with ExitStack() as ctx:
        sb = lambda name, shape, dt=F32: ctx.enter_context(nc.sbuf_tensor(pre + name, shape, dt))
        pre = env.prefix
        sems = []

        def sem(name):
            s = ctx.enter_context(nc.semaphore(pre + name))
            sems.append(s)
            return s

        two = range(2)
        bank = [[ctx.enter_context(nc.psum_tensor(f"{pre}bank{u}{k}", [P, 512], F32)) for k in range(4)]
                for u in two]
        o = [sb(f"o{u}", [P, 2, 256]) for u in two]
        ct = [sb(f"ct{u}", [P, 2, 2, P]) for u in two]
        ox = [sb(f"ox{u}", [P, 2, 256]) for u in two]
        cx = [sb(f"cx{u}", [P, 2, 2, P]) for u in two]
        xn = [sb(f"xn{u}", [P, D]) for u in two]
        xt = [sb(f"xt{u}", [P, 4, P]) for u in two]
        q32 = [sb(f"q32{u}", [P, D]) for u in two]
        k32 = [sb(f"k32{u}", [P, D]) for u in two]
        v32 = [sb(f"v32{u}", [P, D]) for u in two]
        rt = [sb(f"rt{u}", [P, 2, 256]) for u in two] if rope else None
        kr = [sb(f"kr{u}", [P, kvw]) for u in two] if rope else None
        qb = [sb(f"qb{u}", [P, 4, 2, 2, 64]) for u in two]
        kt = [sb(f"kt{u}", [P, 4, P]) for u in two]
        pr = [sb(f"pr{u}", [P, 4, 2, 2, 64]) for u in two]
        pt = [sb(f"pt{u}", [P, 8, P]) for u in two]
        stats = [sb(f"stats{u}", [P, 6]) for u in two]
        mv = [sb(f"mv{u}", [P, 2]) for u in two]
        rs = [sb(f"rs{u}", [P, 1]) for u in two]
        half1 = sb("half1", [P, 1])
        eps1 = sb("eps1", [P, 1])
        mx = [sb(f"mx{u}", [P, 4, 2, 2]) for u in two]
        ls = [sb(f"ls{u}", [P, 4, 2, 2]) for u in two]
        rl = [sb(f"rl{u}", [P, 4, 2, 2]) for u in two]

        W, loads = {}, {}
        for k, shape in ([("wo_x", (4, D)), ("bo_x", (D,)), ("wq", (4, D)), ("wk", (4, kvw)), ("wv", (4, kvw)), ("wo", (4, D))]
                         + ([("cos", (16,)), ("sin", (16,)), ("sink", (4, 2))] if rope else
                            [("bq", (D,)), ("bk", (D,)), ("cb", (4,)), ("bo", (D,))])):
            t = sb(k, [P] + list(shape))
            if len(shape) == 1:
                W[k] = loads[k] = t[:, :]
            else:
                W[k], loads[k] = t[:, :, :], t[:, :, :].rearrange("p a b -> p (a b)")
        W["cb_x"] = env.cb_x[:, :]

        names = ("seen seen_p const sink_ok o_in xs_in tr1 ct1 y1 res1 stat aggr eps rstd xn_done xs2 tr2 xt_done q_done k_done v_done "
                 "q32_done k32_done v32_done rope_a rope_b rope_c tr3 tr4 qb_done kt_done sc_done z_done mx_done "
                 "sub_done exp_done ls_done rl_done tr5 pt_done pv_done o_done tr6 ct2 y2").split()
        names += [f"load_{k}" for k in loads] + [f"x_in{n}" for n in range(TT)]
        g = {name: sem(name) for name in names}
        x, ob, ident, mask = env.x, env.ob, env.ident, env.parity_mask


        def slots(eng, *steps):
            def slot(n, u):
                for step in steps:
                    at = {"g": (n + 1, 1 - u), "f": (n, u), "b": (n - 1, 1 - u)}[step.__name__[0]]
                    if not (isinstance(n, int) and not 0 <= at[0] < TT):
                        step(*at)

            slot(-1, 1)
            slot(0, 0)
            with eng.Fori(0, TT // 2 - 1) as turn:
                slot(2 * turn + 1, 1)
                slot(2 * turn + 2, 0)
            slot(TT - 1, 1)
            slot(TT, 0)

        with nc.Block() as block:

            @block.sync
            def _(sp):
                for n in range(2):
                    sp.dma_start(x[:, n, :], x_src[n]).then_inc(g[f"x_in{n}"], 16)
                large = ["wo_x", "wq", "wk", "wv", "wo"]
                for k in large[:1] + [k for k in loads if k not in large] + large[1:]:
                    sp.dma_start(loads[k], raw[k]).then_inc(g[f"load_{k}"], 16)
                for n in range(2, TT):
                    sp.dma_start(x[:, n, :], x_src[n]).then_inc(g[f"x_in{n}"], 16)

            @block.gpsimd
            def _(pool):
                pool.memset(half1[:, :], -0.5).then_inc(g["const"], 1)
                pool.memset(eps1[:, :], LN_EPS).then_inc(g["const"], 1)

                def g_xs(n, u):
                    pool.tensor_tensor(x[:, n, :], x[:, n, :], W["bo_x"], ALU.add).then_inc(g["xs_in"], 1)
                    if isinstance(n, int) and n == 1:
                        for m in range(2, TT):
                            pool.wait_ge(g[f"x_in{m}"], 16)

                def g_rs(n, u):
                    pool.wait_ge(g["aggr"], n + 1)
                    pool.tensor_tensor(mv[u][:, 1:2], mv[u][:, 1:2], eps1[:, :], ALU.add).then_inc(g["eps"], 1)
                    pool.wait_ge(g["eps"], n + 1)
                    pool.tensor_tensor(rs[u][:, :], mv[u][:, 1:2], half1[:, :], ALU.pow).then_inc(g["rstd"], 1)

                def f_bo(n, u):
                    pool.wait_ge(g["xn_done"], n + 1)
                    pool.sem_inc(g["seen_p"], 1)
                    pool.tensor_tensor(x[:, n, :], x[:, n, :], W["bo"], ALU.add).then_inc(g["xs2"], 1)

                pool.wait_ge(g["const"], 2)
                pool.wait_ge(g["load_bo_x"], 16)
                if not rope:
                    pool.wait_ge(g["load_bo"], 16)
                for n in range(2):
                    pool.wait_ge(g[f"x_in{n}"], 16)
                slots(pool, *(([] if rope else [f_bo]) + [g_xs, g_rs]))

            @block.scalar
            def _(act):
                act.preload_act_table(ACT.Exp)

                def ctx_evac(dst, bank_, cb, done):
                    src = bank_[:, :].rearrange("p (b g a q) -> p b g a q", b=2, g=2, a=2)
                    for a in range(2):
                        for h in range(2):
                            t = act.activation(dst[:, a, h, :].rearrange("p (b q) -> p b q", b=2),
                                               src[:, :, h, a, :], ACT.Identity,
                                               bias=cb[:, 2 * a + h:2 * a + h + 1] if cb is not None else 0.0)
                    t.then_inc(done, 1)

                def g_o(n, u):
                    act.activation(ox[u][:, :, :], ob[:, bass.ds(n * 2, 2), :], ACT.Copy).then_inc(g["o_in"], 1)

                def g_ct(n, u):
                    act.wait_ge(g["tr1"], n + 1)
                    ctx_evac(cx[u], bank[u][2], W["cb_x"], g["ct1"])

                def f_xt(n, u):
                    act.wait_ge(g["tr2"], n + 1)
                    act.activation(xt[u][:, :, :], bank[u][0][:, :].rearrange("p (c n) -> p c n", c=4),
                                   ACT.Copy).then_inc(g["xt_done"], 1)

                def b_v(n, u):
                    act.wait_ge(g["v_done"], n + 1)
                    if rope:
                        act.activation(v32[u][:, :].rearrange("p (k j d) -> p k j d", k=4, j=4),
                                       bank[u][1][:, 0:kvw].rearrange("p (k d) -> p k d", k=4)
                                       .unsqueeze(2).broadcast_to([P, 4, 4, HD]), ACT.Copy)\
                            .then_inc(g["v32_done"], 1)
                    else:
                        act.activation(v32[u][:, :], bank[u][1][:, :], ACT.Copy).then_inc(g["v32_done"], 1)

                def f_kt(n, u):
                    act.wait_ge(g["tr4"], n + 1)
                    act.activation(kt[u][:, :, :], bank[u][2][:, :].rearrange("p (c n) -> p c n", c=4),
                                   ACT.Copy).then_inc(g["kt_done"], 1)

                def b_exp(n, u):
                    act.wait_ge(g["sub_done"], n + 1)
                    act.activation(pr[u][:, :, :, :, :], pr[u][:, :, :, :, :], ACT.Exp,
                                   scale=SCALE).then_inc(g["exp_done"], 1)

                def b_pt(n, u):
                    for j, k in enumerate((0, 2)):
                        act.wait_ge(g["tr5"], 2 * n + j + 1)
                        act.activation(pt[u][:, 4 * j:4 * j + 4, :],
                                       bank[u][k][:, :].rearrange("p (c n) -> p c n", c=4),
                                       ACT.Copy).then_inc(g["pt_done"], 1)

                def b_ct(n, u):
                    act.wait_ge(g["tr6"], n + 1)
                    ctx_evac(ct[u], bank[u][0], W.get("cb"), g["ct2"])

                if not rope:
                    act.wait_ge(g["load_cb"], 16)
                slots(act, g_o, f_xt, b_v, b_exp, b_pt, g_ct, b_ct, f_kt)

            @block.vector
            def _(dve):
                for k in ("sink", "cos", "sin") if rope else ("bq", "bk"):
                    dve.wait_ge(g[f"load_{k}"], 16)
                if rope:
                    dve.tensor_scalar(W["sink"], W["sink"], 1.0 / SCALE, None, ALU.mult).then_inc(g["sink_ok"], 1)
                    dve.wait_ge(g["sink_ok"], 1)

                def g_res(n, u):
                    dve.wait_ge(g["y1"], n + 1)
                    dve.wait_ge(g["xs_in"], n + 1)
                    dve.tensor_tensor(x[:, n, :], bank[u][1][:, :], x[:, n, :], ALU.add).then_inc(g["res1"], 1)

                def g_stat(n, u):
                    dve.wait_ge(g["res1"], n + 1)
                    dve.sem_inc(g["seen"], 1)
                    dve.bn_stats(stats[u][:, :], x[:, n, :]).then_inc(g["stat"], 1)

                def g_aggr(n, u):
                    dve.wait_ge(g["stat"], n + 1)
                    dve.sem_inc(g["seen"], 1)
                    dve.bn_aggr(mv[u][:, :], stats[u][:, :]).then_inc(g["aggr"], 1)

                def f_xn(n, u):
                    dve.wait_ge(g["rstd"], n + 1)
                    dve.tensor_scalar(xn[u][:, :], x[:, n, :], mv[u][:, 0:1], rs[u][:, 0:1], ALU.subtract,
                                      ALU.mult).then_inc(g["xn_done"], 1)

                def rotate(n, u, which, src, w, dst):
                    hs = w // HD
                    s4 = src[:, 0:w].rearrange("p (h f e) -> p h f e", h=hs, e=2)
                    d4 = dst[:, :].rearrange("p (h f e) -> p h f e", h=hs, e=2)
                    cos = W["cos"].unsqueeze(1).broadcast_to([P, hs, 16])
                    sin = W["sin"].unsqueeze(1).broadcast_to([P, hs, 16])
                    ta = rt[u][:, 0, 0:w // 2].rearrange("p (h f) -> p h f", h=hs)
                    tb = rt[u][:, 1, 0:w // 2].rearrange("p (h f) -> p h f", h=hs)
                    base = 2 * (2 * n + which)
                    for e, (ca, cb, op) in enumerate(((cos, sin, ALU.subtract), (sin, cos, ALU.add))):
                        if e:
                            dve.wait_ge(g["rope_c"], base + 1)
                        dve.tensor_tensor(ta, s4[:, :, :, 0], ca, ALU.mult).then_inc(g["rope_a"], 1)
                        dve.tensor_tensor(tb, s4[:, :, :, 1], cb, ALU.mult).then_inc(g["rope_b"], 1)
                        dve.wait_ge(g["rope_a"], base + e + 1)
                        dve.wait_ge(g["rope_b"], base + e + 1)
                        dve.tensor_tensor(d4[:, :, :, e], ta, tb, op).then_inc(g["rope_c"], 1)
                    dve.wait_ge(g["rope_c"], base + 2)

                def f_q(n, u):
                    dve.wait_ge(g["q_done"], n + 1)
                    if rope:
                        rotate(n, u, 0, bank[u][2], D, q32[u])
                    else:
                        dve.tensor_tensor(q32[u][:, :], bank[u][2][:, :], W["bq"], ALU.add).then_inc(g["q32_done"], 1)

                def f_k(n, u):
                    dve.wait_ge(g["k_done"], n + 1)
                    if rope:
                        rotate(n, u, 1, bank[u][3], kvw, kr[u])
                        dve.tensor_copy(k32[u][:, :].rearrange("p (k j d) -> p k j d", k=4, j=4),
                                        kr[u][:, :].rearrange("p (k d) -> p k d", k=4).unsqueeze(2)
                                        .broadcast_to([P, 4, 4, HD])).then_inc(g["k32_done"], 1)
                    else:
                        dve.tensor_tensor(k32[u][:, :], bank[u][3][:, :], W["bk"], ALU.add).then_inc(g["k32_done"], 1)

                def f_qb(n, u):
                    dve.wait_ge(g["tr3"], n + 1)
                    for a in range(2):
                        t = dve.tensor_scalar(qb[u][:, :, :, a, :], bank[u][0][:, :].rearrange(
                            "p (g b q) -> p g b q", g=4, b=2), mask[:, a:a + 1], None, ALU.mult)
                    t.then_inc(g["qb_done"], 1)

                def b_softmax(n, u):
                    for r in range(2):
                        dve.wait_ge(g["sc_done"], 2 * n + r + 1)
                        s = bank[u][2 + r][:, :].rearrange("p (g b k) -> p g b k", g=4, b=2)
                        dst = pr[u][:, :, r, :, :]
                        m = mx[u][:, :, r, :]
                        if rope:
                            dve.tensor_tensor(dst.rearrange("p g b k -> p g (b k)"),
                                              s.rearrange("p g b k -> p g (b k)"),
                                              W["sink"][:, :, r:r + 1].broadcast_to([P, 4, P]), ALU.add)\
                                .then_inc(g["z_done"], 1)
                            dve.wait_ge(g["z_done"], 2 * n + r + 1)
                            s = dst
                        dve.tensor_reduce(m, s, AX.X, ALU.max).then_inc(g["mx_done"], 1)
                        dve.wait_ge(g["mx_done"], 2 * n + r + 1)
                        t = dve.tensor_tensor(dst, s, m.unsqueeze(3).broadcast_to([P, 4, 2, 64]), ALU.subtract)
                    t.then_inc(g["sub_done"], 1)

                def b_ls(n, u):
                    dve.wait_ge(g["exp_done"], n + 1)
                    dve.tensor_reduce(ls[u][:, :, :, :], pr[u][:, :, :, :, :], AX.X, ALU.add).then_inc(g["ls_done"], 1)

                def b_rl(n, u):
                    dve.wait_ge(g["ls_done"], n + 1)
                    dve.reciprocal(rl[u][:, :, :, :], ls[u][:, :, :, :]).then_inc(g["rl_done"], 1)

                def b_o(n, u):
                    dve.wait_ge(g["rl_done"], n + 1)
                    dve.wait_ge(g["pv_done"], n + 1)
                    for b in range(2):
                        src = bank[u][1 + 2 * b][:, :].rearrange("p (a n d) -> p a n d", a=8, n=2)
                        for a in range(2):
                            rows = slice(64 * a, 64 * a + 64)
                            t = dve.tensor_tensor(
                                o[u][rows, b, :].rearrange("p (a d) -> p a d", a=8), src[rows, :, a, :],
                                rl[u][rows, :, :, b].rearrange("p g r -> p (g r)").unsqueeze(2)
                                .broadcast_to([64, 8, HD]), ALU.mult)
                    t.then_inc(g["o_done"], 1)

                def b_x(n, u):
                    dve.wait_ge(g["y2"], n + 1)
                    if not rope:
                        dve.wait_ge(g["xs2"], n + 1)
                    dve.tensor_tensor(x[:, n, :], bank[u][3][:, :], x[:, n, :], ALU.add)

                slots(dve, f_xn, b_softmax, b_ls, b_rl, f_q, f_k, b_o, f_qb, g_res, g_stat, g_aggr, b_x)

            @block.tensor
            def _(pe):
                def out_product(ct_, w, out, done):
                    for k in range(4):
                        t = pe.matmul(out[:, :], ct_[:, k // 2, k % 2, :], w[:, k, :], start=(k == 0), stop=(k == 3))
                    t.then_inc(done, 1)

                def transpose4(src, out, done):
                    for k in range(4):
                        t = pe.transpose(out[:, k * P:(k + 1) * P], src[:, k * P:(k + 1) * P], ident[:, :])
                    t.then_inc(done, 1)

                def flat(t):
                    return t[:, :, :].rearrange("p b n -> p (b n)")

                def g_tr1(n, u):
                    pe.wait_ge(g["o_in"], n + 1)
                    transpose4(flat(ox[u]), bank[u][2], g["tr1"])

                def g_out(n, u):
                    pe.wait_ge(g["ct1"], n + 1)
                    out_product(cx[u], W["wo_x"], bank[u][1], g["y1"])

                def f_tr2(n, u):
                    pe.wait_ge(g["xn_done"], n + 1)
                    transpose4(xn[u], bank[u][0], g["tr2"])

                def projection(n, u, w, out, done, width, ks=(0, 1, 2, 3)):
                    pe.wait_ge(g["xt_done"], n + 1)
                    for k in ks:
                        t = pe.matmul(out[:, 0:width], xt[u][:, k, :], w[:, k, :], start=(k == 0), stop=(k == 3))
                    if ks[-1] == 3:
                        t.then_inc(g[done], 1)

                def first(n, *weights):
                    if isinstance(n, int) and n == 0:
                        for k in weights:
                            pe.wait_ge(g[f"load_{k}"], 16)

                def f_q(n, u):
                    first(n, "wq")
                    projection(n, u, W["wq"], bank[u][2], "q_done", D)

                def f_k(n, u):
                    first(n, "wk")
                    projection(n, u, W["wk"], bank[u][3], "k_done", kvw)

                def b_va(n, u):
                    projection(n, u, W["wv"], bank[u][1], "v_done", kvw, (0, 1))

                def b_vb(n, u):
                    projection(n, u, W["wv"], bank[u][1], "v_done", kvw, (2, 3))

                def f_tr3(n, u):
                    if rope:
                        pe.wait_ge(g["rope_c"], 4 * n + 2)
                    else:
                        pe.wait_ge(g["q32_done"], n + 1)
                    transpose4(q32[u], bank[u][0], g["tr3"])

                def f_tr4(n, u):
                    pe.wait_ge(g["k32_done"], n + 1)
                    transpose4(k32[u], bank[u][2], g["tr4"])
                    first(n, "wv", "wo")

                def b_sc(n, u):
                    pe.wait_ge(g["qb_done"], n + 1)
                    pe.wait_ge(g["kt_done"], n + 1)
                    for r in range(2):
                        rows = slice(64 * r, 64 * r + 64)
                        for c in range(4):
                            for b in range(2):
                                at = (c * 2 + b) * 64
                                t = pe.matmul(bank[u][2 + r][:, at:at + 64],
                                              qb[u][rows, c, b, :, :].rearrange("p a q -> p (a q)"),
                                              kt[u][rows, c, 64 * b:64 * b + 64], start=True, stop=True)
                        t.then_inc(g["sc_done"], 1)

                def b_tr5(n, u):
                    pe.wait_ge(g["exp_done"], n + 1)
                    for j, k in enumerate((0, 2)):
                        for i in range(4):
                            pair = 4 * j + i
                            t = pe.transpose(bank[u][k][:, i * P:(i + 1) * P],
                                             pr[u][:, pair // 2, pair % 2, :, :].rearrange("p b k -> p (b k)"),
                                             ident[:, :])
                        t.then_inc(g["tr5"], 1)

                def b_pv(n, u):
                    pe.wait_ge(g["pt_done"], 2 * n + 2)
                    pe.wait_ge(g["v32_done"], n + 1)
                    for b in range(2):
                        rows = slice(64 * b, 64 * b + 64)
                        for pair in range(8):
                            t = pe.matmul(bank[u][1 + 2 * b][:, pair * 64:(pair + 1) * 64], pt[u][rows, pair, :],
                                          v32[u][rows, pair * 64:(pair + 1) * 64], start=True, stop=True)
                    t.then_inc(g["pv_done"], 1)

                def b_tr6(n, u):
                    pe.wait_ge(g["o_done"], n + 1)
                    transpose4(flat(o[u]), bank[u][0], g["tr6"])

                def b_out(n, u):
                    pe.wait_ge(g["ct2"], n + 1)
                    out_product(ct[u], W["wo"], bank[u][3], g["y2"])

                pe.wait_ge(g["load_wo_x"], 16)
                slots(pe, b_sc, b_va, f_tr2, b_vb, f_q, b_tr5, f_k, b_pv, f_tr3, g_tr1, f_tr4, b_tr6, g_out, b_out)
        nc.clear_and_free_semaphores(sems)
        nc.all_engine_barrier()


E, TOPK, HID = 32, 4, 256
CAP = 2 * B * S * TOPK // E
SLOTS = E * CAP
ROUTE_STEPS = 34


class Steps:

    def __init__(self, eng, sem, turn, per):
        self.eng, self.sem, self.turn, self.per, self.n = eng, sem, turn, per, 0

    def link(self, ins):
        self.n += 1
        ins.then_inc(self.sem, 1)
        self.eng.wait_ge(self.sem, self.turn * self.per + self.n)


def moe_ffn(nc, env, raw, h_dram, slot_dram, eo_dram, x_out):
    with ExitStack() as outer:
        pre = env.prefix
        osb = lambda name, shape, dt=F32: outer.enter_context(nc.sbuf_tensor(pre + name, shape, dt))
        wts = osb("wts", [P, TT, TOPK])
        cidx = osb("cidx", [P, TT, TOPK], I32)
        x, ident = env.x, env.ident
        two = range(2)

        with ExitStack() as ctx:
            sb = lambda name, shape, dt=F32: ctx.enter_context(nc.sbuf_tensor(pre + name, shape, dt))
            sems = []

            def sem(name):
                s = ctx.enter_context(nc.semaphore(pre + name))
                sems.append(s)
                return s

            bank = [[ctx.enter_context(nc.psum_tensor(f"{pre}bank{u}{k}", [P, 512], F32)) for k in range(4)]
                    for u in two]
            gate = sb("gate", [P, 4 * E])
            sgu = sb("sgu", [P, 4, 2 * HID])
            sd = sb("sd", [P, 2, D])
            nw = sb("nw", [P, D])
            upper = sb("upper", [P, P])
            ones = sb("ones", [P, P])
            iota = sb("iota", [P, E])
            tok = sb("tok", [P, TT], I32)
            zero = sb("zero", [P, SLOTS // P], I32)
            half = sb("half", [P, 1])
            eps = sb("eps", [P, 2])
            acc = [sb(f"acc{u}", [P, E]) for u in two]
            h0 = [sb(f"h0{u}", [P, D]) for u in two]
            h = [sb(f"h{u}", [P, D]) for u in two]
            sq = [sb(f"sq{u}", [P, D]) for u in two]
            ht = [sb(f"ht{u}", [P, 4, P]) for u in two]
            stats = [sb(f"stats{u}", [P, 6]) for u in two]
            mv = [sb(f"mv{u}", [P, 2]) for u in two]
            rs = [sb(f"rs{u}", [P, 1]) for u in two]
            ms = [sb(f"ms{u}", [P, 1]) for u in two]
            r2 = [sb(f"r2{u}", [P, 1]) for u in two]
            lg = [sb(f"lg{u}", [P, E]) for u in two]
            top = [sb(f"top{u}", [P, 8]) for u in two]
            top_i = [sb(f"topi{u}", [P, 8], U32) for u in two]
            top_f = [sb(f"topf{u}", [P, 8]) for u in two]
            ntop = [sb(f"ntop{u}", [P, 1]) for u in two]
            ex = [sb(f"ex{u}", [P, TOPK]) for u in two]
            es = [sb(f"es{u}", [P, 1]) for u in two]
            er = [sb(f"er{u}", [P, 1]) for u in two]
            oh = [sb(f"oh{u}", [P, TOPK, E]) for u in two]
            oh2 = [sb(f"oh2{u}", [P, TOPK, E]) for u in two]
            cnt = [sb(f"cnt{u}", [P, E]) for u in two]
            pos = [sb(f"pos{u}", [P, E]) for u in two]
            pk = [sb(f"pk{u}", [P, TOPK]) for u in two]
            t1 = [sb(f"t1{u}", [P, TOPK]) for u in two]
            t2 = [sb(f"t2{u}", [P, TOPK]) for u in two]
            sidx = [sb(f"sidx{u}", [P, TOPK], I32) for u in two]
            tid = [sb(f"tid{u}", [P, 1], I32) for u in two]
            sg = [sb(f"sg{u}", [P, HID]) for u in two]
            sa = [sb(f"sa{u}", [P, 2, P]) for u in two]

            names = ("seen w_in const zero_in stat aggr eps rstd h0_done ms_done eps2 r2_done h_done xh_done h_out0 h_out1 "
                     "tr ht_done lg_done sh_done lgc_done top_done exp_done cnt_done acc_done pos_done posc_done route "
                     "sidx_done tid_done scat0 scat1 scat_done silu_done sa_done y_done x_done").split()
            g = {name: sem(name) for name in names}

            with nc.Block() as block:

                @block.sync
                def _(sp):
                    for dst, src in ((nw[:, :], "nw"), (gate[:, :], "gate"), (upper[:, :], "upper"), (iota[:, :], "iota"),
                                     (tok[:, :], "tok"), (sgu[:, :, :].rearrange("p k n -> p (k n)"), "sgu"),
                                     (sd[:, :, :].rearrange("p k n -> p (k n)"), "sd")):
                        sp.dma_start(dst, raw[src]).then_inc(g["w_in"], 16)
                    sp.wait_ge(g["const"], 1)
                    sp.dma_start(slot_dram.rearrange("(p s) o -> p (s o)", p=P), zero[:, :]).then_inc(g["zero_in"], 16)
                    with sp.Fori(0, TT // 2) as turn:
                        for u in two:
                            sp.wait_ge(g["h_done"], 2 * turn + u + 1)
                            sp.dma_start(h_dram[2 * turn + u], h[u][:, :]).then_inc(g[f"h_out{u}"], 16)
                    for u in two:
                        sp.wait_ge(g[f"h_out{u}"], 16 + 16 * (TT // 2))
                        sp.wait_ge(g[f"scat{u}"], 64 * (TT // 2))
                    sp.wait_ge(g["zero_in"], 16)

                @block.gpsimd
                def _(pool):
                    pool.memset(zero[:, :], 0).then_inc(g["const"], 1)
                    pool.memset(half[:, :], -0.5).then_inc(g["const"], 1)
                    pool.memset(ones[:, :], 1.0).then_inc(g["const"], 1)
                    pool.memset(acc[0][:, :], 0.0).then_inc(g["const"], 1)
                    pool.memset(eps[:, 0:1], LN_EPS).then_inc(g["const"], 1)
                    pool.memset(eps[:, 1:2], HEAD_EPS).then_inc(g["const"], 1)
                    pool.wait_ge(g["const"], 6)
                    pool.wait_ge(g["w_in"], 16 * 7)
                    pool.wait_ge(g["zero_in"], 16)
                    with pool.Fori(0, TT // 2) as turn:
                        for u in two:
                            n = 2 * turn + u
                            pool.wait_ge(g["aggr"], n + 1)
                            pool.tensor_tensor(mv[u][:, 1:2], mv[u][:, 1:2], eps[:, 0:1], ALU.add).then_inc(g["eps"], 1)
                            pool.wait_ge(g["eps"], n + 1)
                            pool.tensor_tensor(rs[u][:, :], mv[u][:, 1:2], half[:, :], ALU.pow).then_inc(g["rstd"], 1)
                        for u in two:
                            n = 2 * turn + u
                            pool.wait_ge(g["ms_done"], n + 1)
                            pool.tensor_tensor(ms[u][:, :], ms[u][:, :], eps[:, 1:2], ALU.add).then_inc(g["eps2"], 1)
                            pool.wait_ge(g["eps2"], n + 1)
                            pool.tensor_tensor(r2[u][:, :], ms[u][:, :], half[:, :], ALU.pow).then_inc(g["r2_done"], 1)
                        for u in two:
                            n = 2 * turn + u
                            pool.tensor_tensor(x[:, n, :], x[:, n, :], h0[u][:, :], ALU.add).then_inc(g["xh_done"], 1)
                            pool.sem_inc(g["seen"], 1)
                            pool.tensor_copy(tid[u][:, :], tok[:, bass.ds(n, 1)]).then_inc(g["tid_done"], 1)
                        for u in two:
                            n = 2 * turn + u
                            pool.wait_ge(g["tid_done"], n + 1)
                            pool.wait_ge(g["sidx_done"], n + 1)
                            pool.sem_inc(g["seen"], 1)
                            for k in range(TOPK):
                                pool.indirect_dma_start(slot_dram, bass.IndirectOffsetOnAxis(ap=sidx[u][:, k:k + 1], axis=0),
                                                        tid[u][:, 0:1], None, bounds_check=SLOTS - 1, oob_is_err=False)\
                                    .then_inc(g[f"scat{u}"], 16)
                        for u in two:
                            pool.wait_ge(g[f"scat{u}"], 64 * turn + 64)
                            pool.sem_inc(g["scat_done"], 1)

                @block.scalar
                def _(act):
                    for u in two:
                        act.sem_inc(g[f"h_out{u}"], 16)
                    with act.Fori(0, TT // 2) as turn:
                        for u in two:
                            n = 2 * turn + u
                            act.wait_ge(g["h0_done"], n + 1)
                            act.activation(sq[u][:, :], h0[u][:, :], ACT.Square, scale=float(D) ** -0.5,
                                           accum_out=ms[u][:, :]).then_inc(g["ms_done"], 1)
                        for u in two:
                            n = 2 * turn + u
                            act.wait_ge(g["tr"], n + 1)
                            act.activation(ht[u][:, :, :], bank[u][0][:, :].rearrange("p (c n) -> p c n", c=4), ACT.Copy)\
                                .then_inc(g["ht_done"], 1)
                        for u in two:
                            n = 2 * turn + u
                            act.wait_ge(g["sh_done"], n + 1)
                            act.activation(sg[u][:, :], bank[u][2][:, 0:HID], ACT.Silu).then_inc(g["silu_done"], 1)
                        for u in two:
                            n = 2 * turn + u
                            act.wait_ge(g["top_done"], n + 1)
                            act.activation(ex[u][:, :], top[u][:, 0:TOPK], ACT.Exp, bias=ntop[u][:, :],
                                           accum_out=es[u][:, :]).then_inc(g["exp_done"], 1)

                @block.vector
                def _(dve):
                    dve.wait_ge(g["w_in"], 16 * 7)
                    dve.wait_ge(g["const"], 4)
                    dve.sem_inc(g["scat_done"], 2)
                    with dve.Fori(0, TT // 2) as turn:
                        steps = Steps(dve, g["route"], turn, ROUTE_STEPS)
                        for u in two:
                            dve.bn_stats(stats[u][:, :], x[:, 2 * turn + u, :]).then_inc(g["stat"], 1)
                        for u in two:
                            dve.wait_ge(g["stat"], 2 * turn + u + 1)
                            dve.sem_inc(g["seen"], 1)
                            dve.bn_aggr(mv[u][:, :], stats[u][:, :]).then_inc(g["aggr"], 1)
                        for u in two:
                            n = 2 * turn + u
                            dve.wait_ge(g["rstd"], n + 1)
                            dve.tensor_scalar(h0[u][:, :], x[:, n, :], mv[u][:, 0:1], rs[u][:, 0:1], ALU.subtract,
                                              ALU.mult).then_inc(g["h0_done"], 1)
                        for u in two:
                            n = 2 * turn + u
                            dve.wait_ge(g["r2_done"], n + 1)
                            dve.wait_ge(g[f"h_out{u}"], 16 * turn + 16)
                            dve.scalar_tensor_tensor(out=h[u][:, :], in0=h0[u][:, :], scalar=r2[u][:, :], in1=nw[:, :],
                                                     op0=ALU.mult, op1=ALU.mult).then_inc(g["h_done"], 1)
                        for u in two:
                            n = 2 * turn + u
                            dve.wait_ge(g["lg_done"], n + 1)
                            steps.link(dve.tensor_copy(lg[u][:, :], bank[u][1][:, 0:E]))
                            dve.sem_inc(g["seen"], 1)
                            steps.link(dve.max(top[u][:, :], lg[u][:, :]))
                            dve.tensor_scalar(ntop[u][:, :], top[u][:, 0:1], -1.0, None, ALU.mult).then_inc(g["top_done"], 1)
                            dve.sem_inc(g["seen"], 1)
                            steps.link(dve.max_index(top_i[u][:, :], top[u][:, :], lg[u][:, :]))
                            steps.link(dve.tensor_copy(top_f[u][:, :], top_i[u][:, :]))
                            steps.link(dve.tensor_tensor(
                                oh[u][:, :, :], iota[:, :].unsqueeze(1).broadcast_to([P, TOPK, E]),
                                top_f[u][:, 0:TOPK].unsqueeze(2).broadcast_to([P, TOPK, E]), ALU.is_equal))
                            dve.tensor_reduce(cnt[u][:, :], oh[u][:, :, :].rearrange("p k e -> p e k"), AX.X, ALU.add)\
                                .then_inc(g["cnt_done"], 1)
                        dve.wait_ge(g["cnt_done"], 2 * turn + 1)
                        dve.tensor_tensor(acc[1][:, :], acc[0][:, :], cnt[0][:, :], ALU.add).then_inc(g["acc_done"], 1)
                        for u in two:
                            n = 2 * turn + u
                            dve.wait_ge(g["silu_done"], n + 1)
                            dve.tensor_tensor(sa[u][:, :, :], bank[u][2][:, HID:2 * HID].rearrange("p (c n) -> p c n", c=2),
                                              sg[u][:, :].rearrange("p (c n) -> p c n", c=2), ALU.mult)\
                                .then_inc(g["sa_done"], 1)
                        for u in two:
                            n = 2 * turn + u
                            dve.wait_ge(g["exp_done"], n + 1)
                            steps.link(dve.reciprocal(er[u][:, :], es[u][:, :]))
                            dve.tensor_scalar(wts[:, n, :], ex[u][:, :], er[u][:, :], None, ALU.mult)
                            dve.wait_ge(g["pos_done"], n + 1)
                            steps.link(dve.tensor_copy(pos[u][:, :], bank[u][1][:, 64:64 + E]))
                            steps.link(dve.tensor_tensor(oh2[u][:, :, :], oh[u][:, :, :],
                                                         pos[u][:, :].unsqueeze(1).broadcast_to([P, TOPK, E]), ALU.mult))
                            steps.link(dve.tensor_reduce(pk[u][:, :], oh2[u][:, :, :], AX.X, ALU.add))
                            f4 = top_f[u][:, 0:TOPK]
                            steps.link(dve.tensor_scalar(t1[u][:, :], pk[u][:, :], float(P), 1.0 - 2.0 * E * P,
                                                         ALU.is_ge, ALU.mult))
                            steps.link(dve.scalar_tensor_tensor(out=t2[u][:, :], in0=f4, scalar=2.0, in1=t1[u][:, :],
                                                                op0=ALU.mult, op1=ALU.add))
                            steps.link(dve.scalar_tensor_tensor(out=t1[u][:, :], in0=pk[u][:, :], scalar=2.0 * E,
                                                                in1=t2[u][:, :], op0=ALU.mult, op1=ALU.add))
                            steps.link(dve.tensor_scalar(t2[u][:, :], pk[u][:, :], float(CAP), 1e6, ALU.is_ge, ALU.mult))
                            steps.link(dve.tensor_tensor(t1[u][:, :], t1[u][:, :], t2[u][:, :], ALU.add))
                            dve.wait_ge(g["scat_done"], n + 1)
                            dve.tensor_copy(sidx[u][:, :], t1[u][:, :]).then_inc(g["sidx_done"], 1)
                            steps.link(dve.tensor_scalar(pk[u][:, :], pk[u][:, :], float(CAP - 1), None, ALU.min))
                            steps.link(dve.scalar_tensor_tensor(out=t2[u][:, :], in0=f4, scalar=float(CAP), in1=pk[u][:, :],
                                                                op0=ALU.mult, op1=ALU.add))
                            steps.link(dve.tensor_copy(cidx[:, n, :], t2[u][:, :]))
                        dve.wait_ge(g["cnt_done"], 2 * turn + 2)
                        dve.wait_ge(g["pos_done"], 2 * turn + 2)
                        dve.tensor_tensor(acc[0][:, :], acc[1][:, :], cnt[1][:, :], ALU.add).then_inc(g["acc_done"], 1)
                        for u in two:
                            n = 2 * turn + u
                            dve.wait_ge(g["y_done"], n + 1)
                            dve.wait_ge(g["xh_done"], n + 1)
                            dve.tensor_tensor(x[:, n, :], bank[u][3][:, :], x[:, n, :], ALU.add).then_inc(g["x_done"], 1)
                        assert steps.n == ROUTE_STEPS, steps.n

                @block.tensor
                def _(pe):
                    pe.wait_ge(g["w_in"], 16 * 7)
                    pe.wait_ge(g["const"], 4)
                    with pe.Fori(0, TT // 2) as turn:
                        for u in two:
                            pe.wait_ge(g["h_done"], 2 * turn + u + 1)
                            for k in range(4):
                                t = pe.transpose(bank[u][0][:, k * P:(k + 1) * P], h[u][:, k * P:(k + 1) * P], ident[:, :])
                            t.then_inc(g["tr"], 1)
                        for u in two:
                            pe.wait_ge(g["ht_done"], 2 * turn + u + 1)
                            for k in range(4):
                                t = pe.matmul(bank[u][1][:, 0:E], ht[u][:, k, :], gate[:, k * E:(k + 1) * E],
                                              start=(k == 0), stop=(k == 3))
                            t.then_inc(g["lg_done"], 1)
                        for u in two:
                            for c in range(4):
                                for k in range(4):
                                    t = pe.matmul(bank[u][2][:, c * P:(c + 1) * P], sgu[:, k, c * P:(c + 1) * P],
                                                  ht[u][:, k, :], start=(k == 0), stop=(k == 3))
                            t.then_inc(g["sh_done"], 1)
                        for u in two:
                            n = 2 * turn + u
                            pe.wait_ge(g["cnt_done"], n + 1)
                            if u:
                                pe.wait_ge(g["acc_done"], n)
                            out = bank[u][1][:, 64:64 + E]
                            pe.matmul(out, upper[:, :], cnt[u][:, :], start=True, stop=False)
                            pe.matmul(out, ones[:, :], acc[u][:, :], start=False, stop=True).then_inc(g["pos_done"], 1)
                        for u in two:
                            pe.wait_ge(g["sa_done"], 2 * turn + u + 1)
                            for k in range(2):
                                t = pe.matmul(bank[u][3][:, :], sa[u][:, k, :], sd[:, k, :], start=(k == 0), stop=(k == 1))
                            t.then_inc(g["y_done"], 1)
            nc.clear_and_free_semaphores(sems)
            nc.all_engine_barrier()

        with ExitStack() as ctx:
            pre = env.prefix + "e_"
            sb = lambda name, shape, dt=F32: ctx.enter_context(nc.sbuf_tensor(pre + name, shape, dt))
            sems = []

            def sem2(name):
                s = ctx.enter_context(nc.semaphore(pre + name))
                sems.append(s)
                return s

            bank = [ctx.enter_context(nc.psum_tensor(f"{pre}bank{k}", [P, 512], F32)) for k in range(6)]
            tab = sb("tab", [P, SLOTS // P], I32)
            idx = [[sb(f"idx{u}{j}", [P, 1], I32) for j in range(2)] for u in two]
            w13 = [sb(f"w13{u}", [P, 4, 2 * HID]) for u in two]
            w2 = [sb(f"w2{u}", [P, 2, D]) for u in two]
            rows = [sb(f"rows{u}", [P, 2, D]) for u in two]
            gt = [sb(f"gt{u}", [P, 4, CAP]) for u in two]
            sg = sb("sg", [P, 2 * CAP])
            aT = [sb(f"at{u}", [P, 2, CAP]) for u in two]
            eo = [sb(f"eo{u}", [P, 2, D]) for u in two]
            names = ("seen tab_in w13_in0 w13_in1 w2_in0 w2_in1 idx_done rows_in0 rows_in1 tr_done gt_a gt_b gu_done silu_done "
                     "act_done out_done eo_a eo_b eo_out0 eo_out1").split()
            g = {name: sem2(name) for name in names}
            PAIRS_E = E // 2
            eo_rows = eo_dram.rearrange("(e j p) d -> e p j d", e=E, p=P)

            with nc.Block() as block:

                @block.sync
                def _(sp):
                    def load(e, u):
                        sp.dma_start(w13[u][:, :, :].rearrange("p k n -> p (k n)"), raw["w13"][e]).then_inc(g[f"w13_in{u}"], 16)
                        sp.dma_start(w2[u][:, :, :].rearrange("p k n -> p (k n)"), raw["w2"][e]).then_inc(g[f"w2_in{u}"], 16)

                    def store(e, u):
                        sp.wait_ge(g["eo_a"], e + 1)
                        sp.wait_ge(g["eo_b"], e + 1)
                        sp.dma_start(eo_rows[e], eo[u][:, :, :]).then_inc(g[f"eo_out{u}"], 16)

                    sp.dma_start(tab[:, :], slot_dram.rearrange("(p s) o -> p (s o)", p=P)).then_inc(g["tab_in"], 16)
                    for u in two:
                        load(u, u)
                    with sp.Fori(0, PAIRS_E - 1) as turn:
                        for u in two:
                            e = 2 * turn + u
                            sp.wait_ge(g["out_done"], e + 1)
                            load(e + 2, u)
                            store(e, u)
                    for u in two:
                        store(E - 2 + u, u)
                    for u in two:
                        sp.wait_ge(g[f"eo_out{u}"], 16 + 16 * PAIRS_E)

                @block.gpsimd
                def _(pool):
                    pool.wait_ge(g["tab_in"], 16)

                    def gather(e, u, turn, first):
                        if not first:
                            pool.wait_ge(g[f"rows_in{u}"], 32 * turn)
                            pool.sem_inc(g["seen"], 1)
                        for j in range(2):
                            pool.tensor_copy(idx[u][j][:, :], tab[:, bass.ds(2 * e + j, 1)]).then_inc(g["idx_done"], 1)
                        if not first:
                            pool.wait_ge(g["tr_done"], e - 1)
                        pool.wait_ge(g["idx_done"], 2 * e + 2)
                        pool.sem_inc(g["seen"], 1)
                        for j in range(2):
                            pool.indirect_dma_start(rows[u][:, j, :], None, h_dram.rearrange("t p d -> (t p) d"),
                                                    bass.IndirectOffsetOnAxis(ap=idx[u][j][:, 0:1], axis=0),
                                                    bounds_check=B * S - 1, oob_is_err=False)\
                                .then_inc(g[f"rows_in{u}"], 16)

                    for u in two:
                        gather(u, u, 0, True)
                    with pool.Fori(1, PAIRS_E) as turn:
                        for u in two:
                            gather(2 * turn + u, u, turn, False)

                @block.scalar
                def _(act):
                    act.preload_act_table(ACT.Silu)
                    for u in two:
                        act.sem_inc(g[f"eo_out{u}"], 16)

                    def evac_t(e, u):
                        act.wait_ge(g["tr_done"], e + 1)
                        act.activation(gt[u][:, :, 0:P], bank[0][:, :].rearrange("p (c n) -> p c n", c=4), ACT.Copy)\
                            .then_inc(g["gt_a"], 1)

                    def rest(e, u, turn, last=False):
                        act.wait_ge(g["gu_done"], e + 1)
                        act.activation(sg[:, :], bank[2][:, :], ACT.Silu).then_inc(g["silu_done"], 1)
                        if not last:
                            evac_t(e + 1, 1 - u)
                        act.wait_ge(g["out_done"], e + 1)
                        act.wait_ge(g[f"eo_out{u}"], 16 * turn + 16)
                        act.activation(eo[u][:, 0, :], bank[4][:, :], ACT.Copy).then_inc(g["eo_a"], 1)

                    evac_t(0, 0)
                    with act.Fori(0, PAIRS_E - 1) as turn:
                        for u in two:
                            rest(2 * turn + u, u, turn)
                    rest(E - 2, 0, PAIRS_E - 1)
                    rest(E - 1, 1, PAIRS_E - 1, True)

                @block.vector
                def _(dve):
                    def evac_t(e, u):
                        dve.wait_ge(g["tr_done"], e + 1)
                        dve.tensor_copy(gt[u][:, :, P:2 * P], bank[1][:, :].rearrange("p (c n) -> p c n", c=4))\
                            .then_inc(g["gt_b"], 1)

                    def rest(e, u, turn, last=False):
                        dve.wait_ge(g["silu_done"], e + 1)
                        dve.tensor_tensor(aT[u][:, :, :].rearrange("p c n -> p (c n)"), bank[3][:, :], sg[:, :], ALU.mult)\
                            .then_inc(g["act_done"], 1)
                        if not last:
                            evac_t(e + 1, 1 - u)
                        dve.wait_ge(g["out_done"], e + 1)
                        dve.wait_ge(g[f"eo_out{u}"], 16 * turn + 16)
                        dve.tensor_copy(eo[u][:, 1, :], bank[5][:, :]).then_inc(g["eo_b"], 1)

                    evac_t(0, 0)
                    with dve.Fori(0, PAIRS_E - 1) as turn:
                        for u in two:
                            rest(2 * turn + u, u, turn)
                    rest(E - 2, 0, PAIRS_E - 1)
                    rest(E - 1, 1, PAIRS_E - 1, True)

                @block.tensor
                def _(pe):
                    def tr(e, u, turn):
                        pe.wait_ge(g[f"rows_in{u}"], 32 * turn + 32)
                        for j in range(2):
                            for k in range(4):
                                t = pe.transpose(bank[j][:, k * P:(k + 1) * P], rows[u][:, j, k * P:(k + 1) * P], ident[:, :])
                        t.then_inc(g["tr_done"], 1)

                    def rest(e, u, turn, last=False):
                        pe.wait_ge(g["gt_a"], e + 1)
                        pe.wait_ge(g["gt_b"], e + 1)
                        pe.wait_ge(g[f"w13_in{u}"], 16 * turn + 16)
                        for c in range(4):
                            for k in range(4):
                                t = pe.matmul(bank[2 + c // 2][:, (c % 2) * CAP:(c % 2 + 1) * CAP],
                                              w13[u][:, k, c * P:(c + 1) * P], gt[u][:, k, :], start=(k == 0), stop=(k == 3))
                        t.then_inc(g["gu_done"], 1)
                        if not last:
                            tr(e + 1, 1 - u, turn + u)
                        pe.wait_ge(g["act_done"], e + 1)
                        pe.wait_ge(g[f"w2_in{u}"], 16 * turn + 16)
                        if not (isinstance(e, int) and e == 0):
                            pe.wait_ge(g["eo_a"], e)
                            pe.wait_ge(g["eo_b"], e)
                        for j in range(2):
                            for k in range(2):
                                t = pe.matmul(bank[4 + j][:, :], aT[u][:, k, j * P:(j + 1) * P], w2[u][:, k, :],
                                              start=(k == 0), stop=(k == 1))
                        t.then_inc(g["out_done"], 1)

                    tr(0, 0, 0)
                    rest(0, 0, 0)
                    rest(1, 1, 0)
                    with pe.Fori(1, PAIRS_E - 1) as turn:
                        for u in two:
                            rest(2 * turn + u, u, turn)
                    rest(E - 2, 0, PAIRS_E - 1)
                    rest(E - 1, 1, PAIRS_E - 1, True)
            nc.clear_and_free_semaphores(sems)
            nc.all_engine_barrier()

        with ExitStack() as ctx:
            pre = env.prefix + "c_"
            sb = lambda name, shape, dt=F32: ctx.enter_context(nc.sbuf_tensor(pre + name, shape, dt))
            got = [sb(f"got{u}", [P, TOPK, D]) for u in two]
            idx = [[sb(f"idx{u}{k}", [P, 1], I32) for k in range(TOPK)] for u in two]
            wt = [sb(f"wt{u}", [P, TOPK]) for u in two]
            names = "seen got_in0 got_in1 idx_done wt_done add_done x_out".split()
            g = {name: ctx.enter_context(nc.semaphore(pre + name)) for name in names}

            with nc.Block() as block:

                @block.gpsimd
                def _(pool):
                    with pool.Fori(0, TT // 2) as turn:
                        for u in two:
                            n = 2 * turn + u
                            pool.wait_ge(g["add_done"], TOPK * n + TOPK)
                            pool.sem_inc(g["seen"], 1)
                            for k in range(TOPK):
                                pool.tensor_copy(idx[u][k][:, :], cidx[:, n, k:k + 1]).then_inc(g["idx_done"], 1)
                            pool.wait_ge(g["idx_done"], TOPK * n + TOPK)
                            pool.sem_inc(g["seen"], 1)
                            for k in range(TOPK):
                                pool.indirect_dma_start(got[u][:, k, :], None,
                                                        eo_dram,
                                                        bass.IndirectOffsetOnAxis(ap=idx[u][k][:, 0:1], axis=0),
                                                        bounds_check=SLOTS - 1, oob_is_err=False)\
                                    .then_inc(g[f"got_in{u}"], 16)

                @block.vector
                def _(dve):
                    dve.sem_inc(g["add_done"], 2 * TOPK)
                    with dve.Fori(0, TT // 2) as turn:
                        for u in two:
                            n = 2 * turn + u
                            dve.wait_ge(g["add_done"], TOPK * n + TOPK)
                            dve.tensor_copy(wt[u][:, :], wts[:, n, :]).then_inc(g["wt_done"], 1)
                        for u in two:
                            n = 2 * turn + u
                            dve.wait_ge(g["wt_done"], n + 1)
                            dve.wait_ge(g[f"got_in{u}"], 16 * TOPK * turn + 16 * TOPK)
                            for k in range(TOPK):
                                dve.wait_ge(g["add_done"], TOPK * n + 2 * TOPK + k)
                                dve.scalar_tensor_tensor(out=x[:, n, :], in0=got[u][:, k, :], scalar=wt[u][:, k:k + 1],
                                                         in1=x[:, n, :], op0=ALU.mult, op1=ALU.add).then_inc(g["add_done"], 1)

                @block.sync
                def _(sp):
                    with sp.Fori(0, TT) as n:
                        sp.wait_ge(g["add_done"], TOPK * n + 3 * TOPK)
                        sp.dma_start(x_out[n], x[:, n, :]).then_inc(g["x_out"], 16)
                    sp.wait_ge(g["x_out"], 16 * TT)
            nc.clear_and_free_semaphores(list(g.values()))
            nc.all_engine_barrier()


FH = int(2 * D * 4 / 3)
FC = -(-FH // P)
FTAIL = FH - (FC - 1) * P
HALF_T = B * S // 2


def ternary_ffn(nc, env, raw, out):
    with ExitStack() as ctx:
        pre = env.prefix
        sb = lambda name, shape, dt=F32: ctx.enter_context(nc.sbuf_tensor(pre + name, shape, dt))
        sems = []

        def sem(name):
            s = ctx.enter_context(nc.semaphore(pre + name))
            sems.append(s)
            return s

        two = range(2)
        bank = [ctx.enter_context(nc.psum_tensor(f"{pre}bank{k}", [P, 512], F32)) for k in range(8)]
        x, ident = env.x, env.ident
        raws = [sb(f"raw{i}", [P, 4 * FH]) for i in range(2)]
        rawt = sb("rawt", [P, D])
        q1 = sb("q1", [P, 4, FH], F16)
        q3 = sb("q3", [P, 4, FH], F16)
        q2 = sb("q2", [P, FC, D], F32R)
        neg = sb("neg", [P, FC * D], BF16)
        junk = sb("junk", [P, FH], BF16)
        ones = sb("ones", [P, P])
        half = sb("half", [P, 1])
        eps = sb("eps", [P, 1])
        part = sb("part", [P, 3, FC])
        tot = sb("tot", [P, 3])
        size = sb("size", [P, 3])
        thr = sb("thr", [P, 3, 2])
        stats = [sb(f"stats{u}", [P, 6]) for u in two]
        mv = [sb(f"mv{u}", [P, 2]) for u in two]
        rs = [sb(f"rs{u}", [P, 1]) for u in two]
        h = [sb(f"h{u}", [P, D]) for u in two]
        hh = sb("hh", [P, 4, B * S], F16)
        hl = sb("hl", [P, 4, B * S], F16)
        sg = [sb(f"sg{u}", [P, HALF_T]) for u in two]
        gg = [sb(f"gg{u}", [P, HALF_T]) for u in two]
        gh = sb("gh", [P, FC, HALF_T], F32R)
        gl = sb("gl", [P, FC, HALF_T], F32R)
        o = h

        names = ("seen w1_in w3_in w2_in const part_done tot_done size_done s1 thr_done neg_done q_done stat aggr eps_done rstd h_done "
                 "tr hh_done hl_done p1_done p3_done silu_done gg_done gh_done gl_done y_done o_done o_out0 o_out1").split()
        g = {name: sem(name) for name in names}

        with nc.Block() as block:

            @block.sync
            def _(sp):
                sp.dma_start(raws[0][:, :], raw["w1"]).then_inc(g["w1_in"], 16)
                sp.dma_start(raws[1][:, 0:4 * FH], raw["w3"]).then_inc(g["w3_in"], 16)
                sp.wait_ge(g["q_done"], 1)
                sp.dma_start(raws[0][:, 0:(FC - 1) * D].rearrange("p (c d) -> p c d", d=D), raw["w2"])\
                    .then_inc(g["w2_in"], 16)
                sp.wait_ge(g["const"], 4)
                sp.dma_start(rawt[0:FTAIL, :], raw["w2t"]).then_inc(g["w2_in"], 16)
                with sp.Fori(0, TT // 2) as turn:
                    for u in two:
                        sp.wait_ge(g["o_done"], 2 * turn + u + 3)
                        sp.dma_start(out[2 * turn + u], o[u][:, :]).then_inc(g[f"o_out{u}"], 16)
                for u in two:
                    sp.wait_ge(g[f"o_out{u}"], 16 + 16 * (TT // 2))

            @block.gpsimd
            def _(pool):
                pool.memset(ones[:, :], 1.0).then_inc(g["const"], 1)
                pool.memset(half[:, :], -0.5).then_inc(g["const"], 1)
                pool.memset(eps[:, :], LN_EPS).then_inc(g["const"], 1)
                pool.memset(rawt[:, :], 0.0).then_inc(g["const"], 1)
                pool.wait_ge(g["const"], 4)
                with pool.Fori(0, TT // 2) as turn:
                    for u in two:
                        n = 2 * turn + u
                        pool.wait_ge(g["aggr"], n + 1)
                        pool.tensor_tensor(mv[u][:, 1:2], mv[u][:, 1:2], eps[:, :], ALU.add).then_inc(g["eps_done"], 1)
                        pool.wait_ge(g["eps_done"], n + 1)
                        pool.tensor_tensor(rs[u][:, :], mv[u][:, 1:2], half[:, :], ALU.pow).then_inc(g["rstd"], 1)

            @block.vector
            def _(dve):
                dve.wait_ge(g["const"], 4)
                for name in ("gg_done", "gl_done", "o_done"):
                    dve.sem_inc(g[name], 2)
                with dve.Fori(0, TT // 2) as turn:
                    for u in two:
                        dve.bn_stats(stats[u][:, :], x[:, 2 * turn + u, :]).then_inc(g["stat"], 1)
                    for u in two:
                        dve.wait_ge(g["stat"], 2 * turn + u + 1)
                        dve.sem_inc(g["seen"], 1)
                        dve.bn_aggr(mv[u][:, :], stats[u][:, :]).then_inc(g["aggr"], 1)
                    for u in two:
                        n = 2 * turn + u
                        dve.wait_ge(g["rstd"], n + 1)
                        dve.tensor_scalar(h[u][:, :], x[:, n, :], mv[u][:, 0:1], rs[u][:, 0:1], ALU.subtract,
                                          ALU.mult).then_inc(g["h_done"], 1)
                    for u in two:
                        n = 2 * turn + u
                        dve.wait_ge(g["hh_done"], n + 1)
                        dve.tensor_tensor(hl[:, :, bass.ds(n * P, P)], bank[u][:, :].rearrange("p (c n) -> p c n", c=4),
                                          hh[:, :, bass.ds(n * P, P)], ALU.subtract).then_inc(g["hl_done"], 1)

                def sizes(i, pieces, part_k):
                    dve.wait_ge(g["part_done"], part_k)
                    dve.tensor_reduce(tot[:, i:i + 1], part[:, i, 0:pieces], AX.X, ALU.add).then_inc(g["tot_done"], 1)
                    dve.wait_ge(g["size_done"], i + 1)
                    dve.tensor_scalar(size[:, i:i + 1], bank[2 + i][:, 0:1], 1.0 / (FH * D), None, ALU.mult)\
                        .then_inc(g["s1"], 1)
                    dve.wait_ge(g["s1"], i + 1)
                    dve.tensor_scalar(thr[:, i, 0:1], size[:, i:i + 1], 0.5, None, ALU.mult)
                    dve.tensor_scalar(thr[:, i, 1:2], size[:, i:i + 1], -0.5, None, ALU.mult).then_inc(g["thr_done"], 1)
                    dve.wait_ge(g["thr_done"], i + 1)

                def quantise(i, w, dst, nb, k, last=True):
                    dve.tensor_scalar(nb, w, thr[:, i, 1:2], None, ALU.is_lt).then_inc(g["neg_done"], 1)
                    dve.wait_ge(g["neg_done"], k)
                    t = dve.scalar_tensor_tensor(out=dst, in0=w, scalar=thr[:, i, 0:1], in1=nb, op0=ALU.is_gt,
                                                 op1=ALU.subtract)
                    if last:
                        t.then_inc(g["q_done"], 1)

                for i, (done, dst) in enumerate((("w1_in", q1), ("w3_in", q3))):
                    dve.wait_ge(g[done], 16)
                    w = raws[i][:, 0:4 * FH]
                    sizes(i, 4, 4 * i + 4)
                    if i:
                        dve.wait_ge(g["q_done"], 1)
                    quantise(i, w, dst[:, :, :].rearrange("p k n -> p (k n)"), neg[:, 0:4 * FH], i + 1)
                dve.wait_ge(g["w2_in"], 32)
                m = (FC - 1) * D
                w, wt = raws[0][:, 0:m], rawt[:, :]
                sizes(2, FC, 8 + FC)
                dve.wait_ge(g["q_done"], 2)
                q2f = q2[:, :, :].rearrange("p k n -> p (k n)")
                quantise(2, w, q2f[:, 0:m], neg[:, 0:m], 3, False)
                quantise(2, wt, q2f[:, m:m + D], neg[:, m:m + D], 4)

                with dve.Fori(0, 2) as t:
                    for c in range(FC):
                        n = t * FC + c
                        r = P if c < FC - 1 else FTAIL
                        u = c % 2
                        dve.wait_ge(g["silu_done"], n + 1)
                        dve.wait_ge(g["p3_done"], n + 1)
                        dve.wait_ge(g["gl_done"], n + 1)
                        dve.scalar_tensor_tensor(out=gg[u][0:r, :], in0=bank[2 + u][0:r, :], scalar=size[0:r, 1:2],
                                                 in1=sg[u][0:r, :], op0=ALU.mult, op1=ALU.mult).then_inc(g["gg_done"], 1)
                        dve.wait_ge(g["gh_done"], n + 1)
                        dve.tensor_tensor(gl[0:r, c, :], gg[u][0:r, :], gh[0:r, c, :].bitcast(F32), ALU.subtract)\
                            .then_inc(g["gl_done"], 1)
                    for j in range(TT // 2):
                        n = t * (TT // 2) + j
                        u = j % 2
                        dve.wait_ge(g["y_done"], n + 1)
                        dve.wait_ge(g[f"o_out{u}"], 16 * (2 * t + j // 2) + 16)
                        dve.scalar_tensor_tensor(out=o[u][:, :], in0=bank[4 + u][:, :], scalar=size[:, 2:3],
                                                 in1=x[:, n, :], op0=ALU.mult, op1=ALU.add).then_inc(g["o_done"], 1)

            @block.scalar
            def _(act):
                act.preload_act_table(ACT.Silu)
                for u in two:
                    act.sem_inc(g[f"o_out{u}"], 16)
                with act.Fori(0, TT // 2) as turn:
                    for u in two:
                        n = 2 * turn + u
                        act.wait_ge(g["tr"], n + 1)
                        act.activation(hh[:, :, bass.ds(n * P, P)], bank[u][:, :].rearrange("p (c n) -> p c n", c=4),
                                       ACT.Copy).then_inc(g["hh_done"], 1)
                for i, done in enumerate(("w1_in", "w3_in")):
                    act.wait_ge(g[done], 16)
                    for k in range(4):
                        if i or k:
                            act.wait_ge(g["part_done"], 4 * i + k)
                        act.activation(junk[:, :], raws[i][:, k * FH:(k + 1) * FH], ACT.Abs,
                                       accum_out=part[:, i, k:k + 1]).then_inc(g["part_done"], 1)
                act.wait_ge(g["w2_in"], 32)
                for k in range(FC):
                    w = raws[0][:, k * D:(k + 1) * D] if k < FC - 1 else rawt[:, :]
                    act.wait_ge(g["part_done"], 8 + k)
                    act.activation(junk[:, 0:D], w, ACT.Abs, accum_out=part[:, 2, k:k + 1]).then_inc(g["part_done"], 1)
                act.preload_act_table(ACT.Silu)
                act.wait_ge(g["s1"], 3)
                with act.Fori(0, 2) as t:
                    for c in range(FC):
                        n = t * FC + c
                        r = P if c < FC - 1 else FTAIL
                        u = c % 2
                        act.wait_ge(g["p1_done"], n + 1)
                        act.activation(sg[u][0:r, :], bank[u][0:r, :], ACT.Silu, scale=size[0:r, 0:1])\
                            .then_inc(g["silu_done"], 1)
                        act.wait_ge(g["gg_done"], n + 3)
                        act.activation(gh[0:r, c, :], gg[u][0:r, :], ACT.Copy).then_inc(g["gh_done"], 1)

            @block.tensor
            def _(pe):
                with pe.Fori(0, TT // 2) as turn:
                    for u in two:
                        n = 2 * turn + u
                        pe.wait_ge(g["h_done"], n + 1)
                        for k in range(4):
                            t = pe.transpose(bank[u][:, k * P:(k + 1) * P], h[u][:, k * P:(k + 1) * P], ident[:, :])
                        t.then_inc(g["tr"], 1)
                pe.wait_ge(g["const"], 4)
                for i in range(3):
                    pe.wait_ge(g["tot_done"], i + 1)
                    pe.matmul(bank[2 + i][:, 0:1], ones[:, :], tot[:, i:i + 1], start=True, stop=True)\
                        .then_inc(g["size_done"], 1)
                pe.wait_ge(g["hl_done"], TT)
                pe.wait_ge(g["q_done"], 3)
                with pe.Fori(0, 2) as t:
                    for c in range(FC):
                        r = P if c < FC - 1 else FTAIL
                        u = c % 2
                        n = t * FC + c
                        pe.wait_ge(g["gg_done"], n + 1)
                        for q, out_, done in ((q1, bank[u], "p1_done"), (q3, bank[2 + u], "p3_done")):
                            for k in range(4):
                                for a, part_ in enumerate((hh, hl)):
                                    m = pe.matmul(out_[0:r, :], q[:, k, c * P:c * P + r],
                                                  part_[:, k, bass.ds(t * HALF_T, HALF_T)],
                                                  start=(k == 0 and a == 0), stop=(k == 3 and a == 1))
                            m.then_inc(g[done], 1)
                    pe.wait_ge(g["gl_done"], FC * t + FC + 2)
                    for j in range(TT // 2):
                        n = t * (TT // 2) + j
                        u = j % 2
                        pe.wait_ge(g["o_done"], n + 1)
                        for c in range(FC):
                            r = P if c < FC - 1 else FTAIL
                            for a, part_ in enumerate((gh, gl)):
                                m = pe.matmul(bank[4 + u][:, :], part_[0:r, c, j * P:(j + 1) * P], q2[0:r, c, :],
                                              start=(c == 0 and a == 0), stop=(c == FC - 1 and a == 1))
                        m.then_inc(g["y_done"], 1)
        nc.clear_and_free_semaphores(sems)
        nc.all_engine_barrier()


def layout(a):
    f = np.float32
    P = 128

    def rows(w):
        k, n = w.shape[0] // P, w.shape[1]
        return w.reshape(k, P, n).transpose(1, 0, 2).reshape(P, k * n)

    def equal(v, n=P):
        return np.broadcast_to(v[None, :], (n, v.shape[0]))

    def head_out(w):
        return w.reshape(2, 4, 2, 32, -1).transpose(1, 3, 2, 0, 4).reshape(P, -1)

    def head_cols(v):
        return v.reshape(2, 4, 2, 32).transpose(1, 3, 2, 0).reshape(P, 4)

    out = {"x": a["x"].reshape(8, P, 512)}
    ctx = a["ctx_1024"]
    out["ctx"] = ctx.transpose(0, 2, 1).reshape(16, 2, P, 1601).transpose(0, 2, 1, 3)
    for L in range(2):
        g = lambda n: a[f"L{L}_xattn_{n}"]
        w = np.concatenate([g("Wk"), g("Wv")], 1).reshape(256, 16, 2, 32)
        b = np.concatenate([g("bk"), g("bv")]).reshape(16, 2, 32)
        x = f"L{L}x_"
        out[x + "wk"] = rows(w[:, :, 0].reshape(256, 512))
        out[x + "wv"] = rows(w[:, :, 1].reshape(256, 512))
        out[x + "wq"] = rows(g("Wq"))
        out[x + "dw"] = rows(g("Wkv_dca"))
        out[x + "bq"] = equal(g("bq"))
        out[x + "bd"] = equal(g("bkv_dca")[:512])
        out[x + "bk"] = equal(b[:, 0].reshape(512))
        out[x + "cols"] = np.stack([np.tile(g(n), 4) for n in ("qn_w", "qn_b", "kn_w", "kn_b", "kn_dca_w", "kn_dca_b")], 1)
        out[x + "cb"] = np.concatenate([head_cols(b[:, 1]), head_cols(g("bkv_dca")[512:])], 1)
        out[x + "yd"] = rows(ctx[:, -16:].reshape(256, 256).T)
        s = f"L{L}s_"
        out[s + "wo_x"] = head_out(g("Wo"))
        out[s + "bo_x"] = equal(g("bo"))
        if L == 0:
            h = lambda n: a["L0_attn_" + n]
            out[s + "wq"], out[s + "wk"], out[s + "wv"] = rows(h("Wq")), rows(h("Wk")), rows(h("Wv"))
            out[s + "wo"] = head_out(h("Wo"))
            out[s + "bq"], out[s + "bk"], out[s + "bo"] = equal(h("bq")), equal(h("bk")), equal(h("bo"))
            out[s + "cb"] = head_cols(h("bv"))
        else:
            h = lambda n: a["L1_attn_" + n]
            out[s + "wq"], out[s + "wk"], out[s + "wv"] = rows(h("wq")), rows(h("wk")), rows(h("wv"))
            out[s + "wo"] = head_out(h("wo"))
            inv = f(1.0) / f(10000.0) ** (np.arange(16, dtype=f) / f(16))
            angle = (np.arange(P) % 64).astype(f)[:, None] * inv[None, :]
            out[s + "cos"], out[s + "sin"] = np.cos(angle), np.sin(angle)
            sink = h("sink").reshape(8, 2)
            out[s + "sink"] = np.repeat(sink.T, 64, 0)
    w = lambda n: a["L0_ffn_" + n]
    out["m_nw"] = equal(w("norm_w"))
    out["m_gate"] = rows(w("gate_w").T)
    out["m_upper"] = np.triu(np.ones((P, P), f), 1)
    out["m_iota"] = np.broadcast_to(np.arange(32, dtype=f), (P, 32))
    out["m_tok"] = np.arange(8 * P, dtype=np.int32).reshape(8, P).T
    out["m_sgu"] = rows(np.concatenate([w("shared_gate_w"), w("shared_up_w")], 1))
    out["m_sd"] = rows(w("shared_down_w"))
    out["m_w13"] = w("w13").reshape(32, 4, P, 512).transpose(0, 2, 1, 3).reshape(32, P, 2048)
    out["m_w2"] = w("w2").reshape(32, 2, P, 512).transpose(0, 2, 1, 3).reshape(32, P, 1024)
    w = lambda n: a["L1_ffn_" + n]
    out["f_w1"], out["f_w3"] = rows(w("w1").T), rows(w("w3").T)
    main = 1365 // P * P
    out["f_w2"] = w("w2").T[:main].reshape(-1, P, 512).transpose(1, 0, 2)
    out["f_w2t"] = w("w2").T[main:]
    out["ident"] = np.eye(P, dtype=f)
    par = (np.arange(P) // 32) % 2
    out["pm"] = np.stack([par == 0, par == 1], 1).astype(f)
    return {k: np.ascontiguousarray(v) for k, v in out.items()}


class Env:
    pass


LAYERS = 2


def perceiver(nc, arrays, out):
    with ExitStack() as outer:
        dram = lambda name, shape, dt=F32: nc.dram_tensor(name, shape, dt).ap()
        qs_dram = dram("qs_dram", [B, P, PAIRS * 2 * P], F16)
        kd_dram = dram("kd_dram", [2, P, GROUPS, B, DCA], F16)
        vd_dram = dram("vd_dram", [B * DCA // P, P, PAIRS, 2, 64], F16)
        h_dram = dram("h_dram", [TT, P, D])
        slot_dram = dram("slot_dram", [SLOTS, 1], I32)
        eo_dram = dram("eo_dram", [SLOTS, D])
        x1_dram = dram("x1_dram", [TT, P, D])
        env = Env()
        sb = lambda name, shape, dt=F32: outer.enter_context(nc.sbuf_tensor(name, shape, dt))
        env.ident = sb("ident", [P, P])
        env.parity_mask = sb("parity_mask", [P, 2])
        env.cb_x = sb("cb_x", [P, 4])
        loaded = outer.enter_context(nc.semaphore("loaded"))
        with nc.Block() as block:

            @block.sync
            def _(sp):
                sp.dma_start(env.ident[:, :], arrays["ident"]).then_inc(loaded, 16)
                sp.dma_start(env.parity_mask[:, :], arrays["pm"]).then_inc(loaded, 16)
                sp.wait_ge(loaded, 32)
        nc.all_engine_barrier()

        for layer in range(LAYERS):
            x_src = arrays["x"] if layer == 0 else x1_dram
            part = lambda kind: {name[len(kind):]: a for name, a in arrays.items() if name.startswith(kind)}
            with ExitStack() as ctx:
                sb = lambda name, shape, dt=F32: ctx.enter_context(nc.sbuf_tensor(f"l{layer}_{name}", shape, dt))
                env.ob = sb("ob", [P, B, PAIRS * HD])
                with ExitStack() as weights:
                    wsb = lambda name, shape, dt=F32R: weights.enter_context(
                        nc.sbuf_tensor(f"l{layer}_{name}", shape, dt))
                    wk, wv = wsb("wk", [P, 2, KC, D]), wsb("wv", [P, 2, KC, D])
                    bk, kcol = wsb("bk", [P, D], F32), wsb("kcol", [P, 2], F32)
                    env.prefix = f"p{layer}_"
                    prepare_context_attention(nc, env, part(f"L{layer}x_"), x_src, qs_dram, kd_dram, vd_dram, wk, wv,
                                              bk[:, :], kcol[:, 0:1], kcol[:, 1:2])
                    env.prefix = f"a{layer}_"
                    context_attention(nc, env, arrays["ctx"], qs_dram, kd_dram, vd_dram, wk, wv, bk[:, :], kcol[:, 0:1],
                                      kcol[:, 1:2])
                env.x = sb("x", [P, TT, D])
                env.prefix = f"s{layer}_"
                self_attention(nc, env, layer, part(f"L{layer}s_"), x_src)
                env.prefix = f"f{layer}_"
                if layer == 0:
                    moe_ffn(nc, env, part("m_"), h_dram, slot_dram, eo_dram, x1_dram)
                else:
                    ternary_ffn(nc, env, part("f_"), out)


def kernel(**inputs):
    import numpy as _np
    import concourse.bacc as _bacc
    from concourse import mybir as _mybir
    from concourse.bass_utils import run_bass_kernel_spmd as _run

    arrays = layout({name: _np.asarray(a) for name, a in inputs.items()})
    nc = _bacc.Bacc("TRN2", target_bir_lowering=False, num_devices=1)
    aps = {name: nc.dram_tensor(f"in_{name}", a.shape, _mybir.dt.from_np(a.dtype), kind="ExternalInput").ap()
           for name, a in arrays.items()}
    out = nc.dram_tensor("out", (TT, P, D), _mybir.dt.float32, kind="ExternalOutput").ap()
    perceiver(nc, aps, out)
    r = _run(nc, [{f"in_{name}": a for name, a in arrays.items()}], core_ids=[0])
    return r.results[0]["out"].reshape(B, S, D)
```
